# Optimizing a Trainium2 kernel written in Bass

```python
import numpy as np
import jax
import jax.numpy as jnp

def _softmax(x, axis=-1):
    return jax.nn.softmax(x, axis=axis)

def _gelu(x):
    return jax.nn.gelu(x, approximate=True)

def _silu(x):
    return jax.nn.silu(x)

def _sigmoid(x):
    return jax.nn.sigmoid(x)

def _layernorm(x, axis=-1, eps=1e-05):
    m = jnp.mean(x, axis=axis, keepdims=True)
    v = jnp.var(x, axis=axis, keepdims=True)
    return (x - m) / jnp.sqrt(v + eps)

def _scatter_add(tgt, idx, src, axis=0):
    return tgt.at[idx].add(src)

def _segment_sum(src, seg, n):
    return jax.ops.segment_sum(src, seg, n)
kernel_name = 'mk_sandwich_d2_jaxref_r8_45fbae'

def setup_inputs(seed: int=0):
    np.random.seed(seed)
    _w = jnp.asarray

    def _L0_attn_setup():
        import jax, jax.numpy as jnp
        import numpy as np
        EPS = 1e-05

        def _scan_combine(left, right):
            a1, u1 = left
            a2, u2 = right
            return (a1 * a2, a2 * u1 + u2)
        key = jax.random.key(seed)
        ks = jax.random.split(key, 8)
        B, L, D = (2, 512, 256)
        N = D
        s_in = 1.0 / np.sqrt(D)
        s_out = 1.0 / np.sqrt(N)
        return {'x': jax.random.normal(ks[0], (B, L, D), jnp.float32), 'rms_w': jnp.ones((D,), jnp.float32), 'A_w': jax.random.normal(ks[1], (N, D), jnp.float32) * s_in, 'A_b': jnp.zeros((N,), jnp.float32), 'B_w': jax.random.normal(ks[2], (N, D), jnp.float32) * s_in, 'Ca_w': jax.random.normal(ks[3], (N, D), jnp.float32) * s_in, 'Cb_w': jax.random.normal(ks[4], (N, D), jnp.float32) * s_in, 'D_w': jax.random.normal(ks[5], (N, D), jnp.float32) * s_in, 'out_w': jax.random.normal(ks[6], (D, N), jnp.float32) * s_out, 'out_b': jnp.zeros((D,), jnp.float32)}
    _L0_attn_in = _L0_attn_setup()

    def _L0_ffn_setup():
        import jax, jax.numpy as jnp
        import numpy as np
        E, K, H, I = (64, 6, 256, 176)
        NS = 2
        IS = NS * I
        CAP = 32
        T_TOKENS = (1, 128)
        SCALE = 0.02

        def _moe_infer(x, gate_w, w_gate, w_up, w_down):
            T = x.shape[0]
            TK = T * K
            logits = x @ gate_w.T
            scores = jax.nn.softmax(logits, axis=-1)
            topk_w, topk_i = jax.lax.top_k(scores, K)
            flat_i = topk_i.reshape(-1)
            flat_w = topk_w.reshape(-1)
            token_ids = jnp.arange(TK, dtype=jnp.int32) // K
            order = jnp.argsort(flat_i)
            sorted_e = flat_i[order]
            counts = jnp.bincount(flat_i, length=E)
            starts = jnp.concatenate([jnp.zeros((1,), counts.dtype), jnp.cumsum(counts)[:-1]])
            pos_sorted = jnp.arange(TK) - starts[sorted_e]
            pos = jnp.zeros((TK,), jnp.int32).at[order].set(pos_sorted.astype(jnp.int32))
            valid = pos < CAP
            slot = jnp.where(valid, pos, CAP)
            buf = jnp.zeros((E, CAP + 1, H), x.dtype).at[flat_i, slot].set(x[token_ids])
            g = jnp.einsum('ech,ehi->eci', buf, w_gate)
            u = jnp.einsum('ech,ehi->eci', buf, w_up)
            y = jnp.einsum('eci,eih->ech', jax.nn.silu(g) * u, w_down)
            out_slots = y[flat_i, slot] * (flat_w * valid)[:, None]
            return out_slots.reshape(T, K, H).sum(axis=1)
        key = jax.random.key(seed)
        ks = jax.random.split(key, 8)
        f32 = jnp.float32
        return {'hidden_states': jax.random.normal(ks[0], (*T_TOKENS, H), f32), 'gate_w': jax.random.normal(ks[1], (E, H), f32) * SCALE, 'w_gate': jax.random.normal(ks[2], (E, H, I), f32) * SCALE, 'w_up': jax.random.normal(ks[3], (E, H, I), f32) * SCALE, 'w_down': jax.random.normal(ks[4], (E, I, H), f32) * SCALE, 'sw_gate': jax.random.normal(ks[5], (H, IS), f32) * SCALE, 'sw_up': jax.random.normal(ks[6], (H, IS), f32) * SCALE, 'sw_down': jax.random.normal(ks[7], (IS, H), f32) * SCALE}
    _L0_ffn_in = _L0_ffn_setup()

    def _L1_attn_setup():
        import jax, jax.numpy as jnp
        import numpy as np
        from jax import lax
        H = 16
        D = 128
        HID = 256
        CONV_K = 4
        CHUNK = 64
        EPS = 1e-06

        def silu(x):
            return x * jax.nn.sigmoid(x)

        def short_conv(x, w):
            B, T, C = x.shape
            K = w.shape[1]
            xp = jnp.pad(x, ((0, 0), (K - 1, 0), (0, 0)))
            y = sum((xp[:, j:j + T, :] * w[None, None, :, j] for j in range(K)))
            return silu(y)

        def l2norm(x):
            return x * lax.rsqrt(jnp.sum(x * x, -1, keepdims=True) + EPS)

        def rmsnorm(x, w):
            return x * lax.rsqrt(jnp.mean(x * x, -1, keepdims=True) + EPS) * w

        def kda_scan(q, k, v, g, beta):
            B, T, _, _ = q.shape
            NC = T // CHUNK

            def tm(a):
                a = jnp.moveaxis(a, 1, 0)
                return a.reshape((NC, CHUNK) + a.shape[1:])

            def step(S, inp):
                qt, kt, vt, gt, bt = inp
                S = S * jnp.exp(gt)[..., :, None]
                u = (vt - jnp.einsum('bhk,bhkv->bhv', kt, S)) * bt[..., None]
                S = S + kt[..., None] * u[..., None, :]
                ot = jnp.einsum('bhk,bhkv->bhv', qt, S)
                return (S, ot)

            @jax.checkpoint
            def chunk_body(S, inp):
                return lax.scan(step, S, inp)
            S0 = jnp.zeros((B, H, D, D), dtype=q.dtype)
            _, o = lax.scan(chunk_body, S0, (tm(q), tm(k), tm(v), tm(g), tm(beta)))
            o = o.reshape(T, B, H, D)
            return jnp.moveaxis(o, 0, 1)
        key = jax.random.key(seed)
        ks = jax.random.split(key, 16)
        s_h = 1.0 / np.sqrt(HID)
        s_d = 1.0 / np.sqrt(D)
        inp = {'hidden_states': jax.random.normal(ks[0], (2, 512, HID), dtype=jnp.float32), 'Wq': jax.random.normal(ks[1], (HID, H * D), dtype=jnp.float32) * s_h, 'Wk': jax.random.normal(ks[2], (HID, H * D), dtype=jnp.float32) * s_h, 'Wv': jax.random.normal(ks[3], (HID, H * D), dtype=jnp.float32) * s_h, 'conv_q_w': jax.random.normal(ks[4], (H * D, CONV_K), dtype=jnp.float32) * 0.5, 'conv_k_w': jax.random.normal(ks[5], (H * D, CONV_K), dtype=jnp.float32) * 0.5, 'conv_v_w': jax.random.normal(ks[6], (H * D, CONV_K), dtype=jnp.float32) * 0.5, 'A_log': jnp.log(jax.random.uniform(ks[7], (1, 1, H, 1), dtype=jnp.float32, minval=1.0, maxval=16.0)), 'Wfa': jax.random.normal(ks[8], (HID, D), dtype=jnp.float32) * s_h, 'Wfb': jax.random.normal(ks[9], (D, H * D), dtype=jnp.float32) * s_d, 'dt_bias': jax.random.normal(ks[10], (H * D,), dtype=jnp.float32) * 0.5, 'Wb': jax.random.normal(ks[11], (HID, H), dtype=jnp.float32) * s_h, 'Wga': jax.random.normal(ks[12], (HID, D), dtype=jnp.float32) * s_h, 'Wgb': jax.random.normal(ks[13], (D, H * D), dtype=jnp.float32) * s_d, 'o_norm_w': jnp.ones((D,), dtype=jnp.float32), 'Wo': jax.random.normal(ks[14], (H * D, HID), dtype=jnp.float32) * s_h}
        return inp
    _L1_attn_in = _L1_attn_setup()

    def _L1_ffn_setup():
        import jax, jax.numpy as jnp
        import numpy as np
        B, S, D, H = (4, 256, 256, 1024)

        def fwht(x):
            orig_shape = x.shape
            n = orig_shape[-1]
            x = x.reshape(-1, n)
            h = 1
            while h < n:
                xb = x.reshape(-1, n // (2 * h), 2, h)
                a = xb[:, :, 0, :]
                b = xb[:, :, 1, :]
                x = jnp.stack([a + b, a - b], axis=2).reshape(-1, n)
                h *= 2
            scale = jnp.asarray(1.0 / np.sqrt(n), dtype=x.dtype)
            return (x * scale).reshape(orig_shape)
        key = jax.random.key(seed)
        kx, k1, k2, k3 = jax.random.split(key, 4)
        x = jax.random.normal(kx, (B, S, D), dtype=jnp.float32)
        W1 = jax.random.normal(k1, (H, D), dtype=jnp.float32) * (1.0 / np.sqrt(D))
        W2 = jax.random.normal(k2, (D, H), dtype=jnp.float32) * (1.0 / np.sqrt(H))
        W3 = jax.random.normal(k3, (H, D), dtype=jnp.float32) * (1.0 / np.sqrt(D))
        return {'x': x, 'W1': W1, 'W2': W2, 'W3': W3}
    _L1_ffn_in = _L1_ffn_setup()
    _d = {'L0_attn_x': _L0_attn_in['x'], 'L0_attn_rms_w': _L0_attn_in['rms_w'], 'L0_attn_A_w': _L0_attn_in['A_w'], 'L0_attn_A_b': _L0_attn_in['A_b'], 'L0_attn_B_w': _L0_attn_in['B_w'], 'L0_attn_Ca_w': _L0_attn_in['Ca_w'], 'L0_attn_Cb_w': _L0_attn_in['Cb_w'], 'L0_attn_D_w': _L0_attn_in['D_w'], 'L0_attn_out_w': _L0_attn_in['out_w'], 'L0_attn_out_b': _L0_attn_in['out_b'], 'L0_ffn_gate_w': _L0_ffn_in['gate_w'], 'L0_ffn_w_gate': _L0_ffn_in['w_gate'], 'L0_ffn_w_up': _L0_ffn_in['w_up'], 'L0_ffn_w_down': _L0_ffn_in['w_down'], 'L0_ffn_sw_gate': _L0_ffn_in['sw_gate'], 'L0_ffn_sw_up': _L0_ffn_in['sw_up'], 'L0_ffn_sw_down': _L0_ffn_in['sw_down'], 'L1_attn_Wq': _L1_attn_in['Wq'], 'L1_attn_Wk': _L1_attn_in['Wk'], 'L1_attn_Wv': _L1_attn_in['Wv'], 'L1_attn_conv_q_w': _L1_attn_in['conv_q_w'], 'L1_attn_conv_k_w': _L1_attn_in['conv_k_w'], 'L1_attn_conv_v_w': _L1_attn_in['conv_v_w'], 'L1_attn_A_log': _L1_attn_in['A_log'], 'L1_attn_Wfa': _L1_attn_in['Wfa'], 'L1_attn_Wfb': _L1_attn_in['Wfb'], 'L1_attn_dt_bias': _L1_attn_in['dt_bias'], 'L1_attn_Wb': _L1_attn_in['Wb'], 'L1_attn_Wga': _L1_attn_in['Wga'], 'L1_attn_Wgb': _L1_attn_in['Wgb'], 'L1_attn_o_norm_w': _L1_attn_in['o_norm_w'], 'L1_attn_Wo': _L1_attn_in['Wo'], 'L1_ffn_W1': _L1_ffn_in['W1'], 'L1_ffn_W2': _L1_ffn_in['W2'], 'L1_ffn_W3': _L1_ffn_in['W3']}
    _x0 = _d['L0_attn_x']
    _d['L0_attn_x'] = jax.random.normal(jax.random.fold_in(jax.random.key(seed), 1), (4, 512, 256), dtype=_x0.dtype)
    del _x0
    return _d

def reference(L0_attn_x, L0_attn_rms_w, L0_attn_A_w, L0_attn_A_b, L0_attn_B_w, L0_attn_Ca_w, L0_attn_Cb_w, L0_attn_D_w, L0_attn_out_w, L0_attn_out_b, L0_ffn_gate_w, L0_ffn_w_gate, L0_ffn_w_up, L0_ffn_w_down, L0_ffn_sw_gate, L0_ffn_sw_up, L0_ffn_sw_down, L1_attn_Wq, L1_attn_Wk, L1_attn_Wv, L1_attn_conv_q_w, L1_attn_conv_k_w, L1_attn_conv_v_w, L1_attn_A_log, L1_attn_Wfa, L1_attn_Wfb, L1_attn_dt_bias, L1_attn_Wb, L1_attn_Wga, L1_attn_Wgb, L1_attn_o_norm_w, L1_attn_Wo, L1_ffn_W1, L1_ffn_W2, L1_ffn_W3):

    def _L0_attn_ref(x, rms_w, A_w, A_b, B_w, Ca_w, Cb_w, D_w, out_w, out_b):
        import jax, jax.numpy as jnp
        import numpy as np
        EPS = 1e-05

        def _scan_combine(left, right):
            a1, u1 = left
            a2, u2 = right
            return (a1 * a2, a2 * u1 + u2)
        norm = jnp.sqrt(jnp.mean(jnp.square(x), axis=-1, keepdims=True) + EPS)
        xn = x * (rms_w / norm)
        a = jax.nn.sigmoid(jnp.einsum('bld,nd->bln', xn, A_w) + A_b)
        b = jnp.einsum('bld,nd->bln', xn, B_w)
        c = jax.nn.silu(jnp.einsum('bld,nd->bln', xn, Ca_w)) * jnp.einsum('bld,nd->bln', xn, Cb_w)
        d = jax.nn.sigmoid(jnp.einsum('bld,nd->bln', xn, D_w))
        u = d * b
        _, h = jax.lax.associative_scan(_scan_combine, (a, u), axis=1)
        y = c * h
        out = jnp.einsum('bln,dn->bld', y, out_w) + out_b
        return out + x

    def _L0_ffn_ref(hidden_states, gate_w, w_gate, w_up, w_down, sw_gate, sw_up, sw_down):
        import jax, jax.numpy as jnp
        import numpy as np
        E, K, H, I = (64, 6, 256, 176)
        NS = 2
        IS = NS * I
        CAP = 32
        T_TOKENS = (1, 128)
        SCALE = 0.02

        def _moe_infer(x, gate_w, w_gate, w_up, w_down):
            T = x.shape[0]
            TK = T * K
            logits = x @ gate_w.T
            scores = jax.nn.softmax(logits, axis=-1)
            topk_w, topk_i = jax.lax.top_k(scores, K)
            flat_i = topk_i.reshape(-1)
            flat_w = topk_w.reshape(-1)
            token_ids = jnp.arange(TK, dtype=jnp.int32) // K
            order = jnp.argsort(flat_i)
            sorted_e = flat_i[order]
            counts = jnp.bincount(flat_i, length=E)
            starts = jnp.concatenate([jnp.zeros((1,), counts.dtype), jnp.cumsum(counts)[:-1]])
            pos_sorted = jnp.arange(TK) - starts[sorted_e]
            pos = jnp.zeros((TK,), jnp.int32).at[order].set(pos_sorted.astype(jnp.int32))
            valid = pos < CAP
            slot = jnp.where(valid, pos, CAP)
            buf = jnp.zeros((E, CAP + 1, H), x.dtype).at[flat_i, slot].set(x[token_ids])
            g = jnp.einsum('ech,ehi->eci', buf, w_gate)
            u = jnp.einsum('ech,ehi->eci', buf, w_up)
            y = jnp.einsum('eci,eih->ech', jax.nn.silu(g) * u, w_down)
            out_slots = y[flat_i, slot] * (flat_w * valid)[:, None]
            return out_slots.reshape(T, K, H).sum(axis=1)
        orig_shape = hidden_states.shape
        x = hidden_states.reshape(-1, orig_shape[-1])
        y = _moe_infer(x, gate_w, w_gate, w_up, w_down).reshape(orig_shape)
        shared = jax.nn.silu(hidden_states @ sw_gate) * (hidden_states @ sw_up) @ sw_down
        return y + shared

    def _L1_attn_ref(hidden_states, Wq, Wk, Wv, conv_q_w, conv_k_w, conv_v_w, A_log, Wfa, Wfb, dt_bias, Wb, Wga, Wgb, o_norm_w, Wo):
        import jax, jax.numpy as jnp
        import numpy as np
        from jax import lax
        H = 16
        D = 128
        HID = 256
        CONV_K = 4
        CHUNK = 64
        EPS = 1e-06

        def silu(x):
            return x * jax.nn.sigmoid(x)

        def short_conv(x, w):
            B, T, C = x.shape
            K = w.shape[1]
            xp = jnp.pad(x, ((0, 0), (K - 1, 0), (0, 0)))
            y = sum((xp[:, j:j + T, :] * w[None, None, :, j] for j in range(K)))
            return silu(y)

        def l2norm(x):
            return x * lax.rsqrt(jnp.sum(x * x, -1, keepdims=True) + EPS)

        def rmsnorm(x, w):
            return x * lax.rsqrt(jnp.mean(x * x, -1, keepdims=True) + EPS) * w

        def kda_scan(q, k, v, g, beta):
            B, T, _, _ = q.shape
            NC = T // CHUNK

            def tm(a):
                a = jnp.moveaxis(a, 1, 0)
                return a.reshape((NC, CHUNK) + a.shape[1:])

            def step(S, inp):
                qt, kt, vt, gt, bt = inp
                S = S * jnp.exp(gt)[..., :, None]
                u = (vt - jnp.einsum('bhk,bhkv->bhv', kt, S)) * bt[..., None]
                S = S + kt[..., None] * u[..., None, :]
                ot = jnp.einsum('bhk,bhkv->bhv', qt, S)
                return (S, ot)

            @jax.checkpoint
            def chunk_body(S, inp):
                return lax.scan(step, S, inp)
            S0 = jnp.zeros((B, H, D, D), dtype=q.dtype)
            _, o = lax.scan(chunk_body, S0, (tm(q), tm(k), tm(v), tm(g), tm(beta)))
            o = o.reshape(T, B, H, D)
            return jnp.moveaxis(o, 0, 1)
        B, T, _ = hidden_states.shape
        q = short_conv(hidden_states @ Wq, conv_q_w)
        k = short_conv(hidden_states @ Wk, conv_k_w)
        v = short_conv(hidden_states @ Wv, conv_v_w)
        g = (hidden_states @ Wfa @ Wfb).reshape(B, T, H, D)
        g = -jnp.exp(A_log) * jax.nn.softplus(g + dt_bias.reshape(1, 1, H, D))
        beta = jax.nn.sigmoid(hidden_states @ Wb)
        q = l2norm(q.reshape(B, T, H, D)) * D ** (-0.5)
        k = l2norm(k.reshape(B, T, H, D))
        v = v.reshape(B, T, H, D)
        o = kda_scan(q, k, v, g, beta)
        go = (hidden_states @ Wga @ Wgb).reshape(B, T, H, D)
        o = rmsnorm(o, o_norm_w) * jax.nn.sigmoid(go)
        o = o.reshape(B, T, H * D) @ Wo
        return o

    def _L1_ffn_ref(x, W1, W2, W3):
        import jax, jax.numpy as jnp
        import numpy as np
        B, S, D, H = (4, 256, 256, 1024)

        def fwht(x):
            orig_shape = x.shape
            n = orig_shape[-1]
            x = x.reshape(-1, n)
            h = 1
            while h < n:
                xb = x.reshape(-1, n // (2 * h), 2, h)
                a = xb[:, :, 0, :]
                b = xb[:, :, 1, :]
                x = jnp.stack([a + b, a - b], axis=2).reshape(-1, n)
                h *= 2
            scale = jnp.asarray(1.0 / np.sqrt(n), dtype=x.dtype)
            return (x * scale).reshape(orig_shape)
        up_gate = jnp.einsum('bsd,hd->bsh', x, W1)
        up_lin = jnp.einsum('bsd,hd->bsh', x, W3)
        hidden = jax.nn.silu(up_gate) * up_lin
        hidden = fwht(hidden)
        out = jnp.einsum('bsh,dh->bsd', hidden, W2)
        return out
    x = L0_attn_x
    x = x + _layernorm(_L0_attn_ref(_layernorm(x, axis=-1), L0_attn_rms_w, L0_attn_A_w, L0_attn_A_b, L0_attn_B_w, L0_attn_Ca_w, L0_attn_Cb_w, L0_attn_D_w, L0_attn_out_w, L0_attn_out_b), axis=-1)
    x = x + _layernorm(_L0_ffn_ref(_layernorm(x, axis=-1), L0_ffn_gate_w, L0_ffn_w_gate, L0_ffn_w_up, L0_ffn_w_down, L0_ffn_sw_gate, L0_ffn_sw_up, L0_ffn_sw_down), axis=-1)
    x = x + _layernorm(_L1_attn_ref(_layernorm(x, axis=-1), L1_attn_Wq, L1_attn_Wk, L1_attn_Wv, L1_attn_conv_q_w, L1_attn_conv_k_w, L1_attn_conv_v_w, L1_attn_A_log, L1_attn_Wfa, L1_attn_Wfb, L1_attn_dt_bias, L1_attn_Wb, L1_attn_Wga, L1_attn_Wgb, L1_attn_o_norm_w, L1_attn_Wo), axis=-1)
    x = x + _layernorm(_L1_ffn_ref(_layernorm(x, axis=-1), L1_ffn_W1, L1_ffn_W2, L1_ffn_W3), axis=-1)
    return x

_drawn_inputs = setup_inputs


def setup_inputs(seed=0):
    import zlib

    import numpy as np

    out = dict(_drawn_inputs(seed))
    spreads = {'L0_attn_rms_w': (1.0, 0.2),
     'L0_attn_A_b': (0.0, 0.8),
     'L0_attn_out_b': (0.0, 0.1),
     'L1_attn_o_norm_w': (1.0, 0.2)}
    factors = {}
    for name, (base, spread) in spreads.items():
        noise = np.random.default_rng([zlib.crc32(name.encode()), seed]).standard_normal(out[name].shape)
        drawn = base * np.exp(spread * noise) if base else spread * noise
        out[name] = jnp.asarray(drawn.astype(out[name].dtype))
    for name, factor in factors.items():
        out[name] = (out[name] * factor).astype(out[name].dtype)
    return out
```

```python
from contextlib import ExitStack

import numpy as np

import concourse.bass as bass
from concourse import mybir

F32 = mybir.dt.float32
I32 = mybir.dt.int32
U32 = mybir.dt.uint32
BF16 = mybir.dt.bfloat16
ALU = mybir.AluOpType
ACT = mybir.ActivationFunctionType
AX = mybir.AxisListType

P = 128
B, L, D = 4, 512, 256
T = B * L
NT = T // P
KC = D // P
LN_EPS = 1e-5


class Pools:

    def __init__(self, nc, ctx):
        self.nc, self.ctx, self.sems = nc, ctx, []
        ctx.callback(self.end)

    def sb(self, name, shape, dt=F32):
        return self.ctx.enter_context(self.nc.sbuf_tensor(name, shape, dt))

    def ps(self, name, shape=(P, 512), dt=F32):
        return self.ctx.enter_context(self.nc.psum_tensor(name, list(shape), dt))

    def sem(self, name):
        self.sems.append(self.nc.alloc_semaphore(name=name))
        return self.sems[-1]

    def end(self):
        self.nc.clear_and_free_semaphores(self.sems)
        self.nc.all_engine_barrier()


class NormIn:

    def __init__(self, nc, m, tag, x, ident, xT, xh, banks, rms=False, col_scale=None):
        self.nc, self.x, self.ident, self.xT, self.xh, self.banks = nc, x, ident, xT, xh, banks
        self.rms, self.col_scale = rms, col_scale
        self.st = m.sb(f"{tag}_st", [P, NT, 6])
        self.mv = m.sb(f"{tag}_mv", [P, NT, 2])
        self.ve = m.sb(f"{tag}_ve", [P, NT])
        self.sd = m.sb(f"{tag}_sd", [P, NT])
        self.rstd = m.sb(f"{tag}_rstd", [P, NT])
        if rms:
            self.ms = m.sb(f"{tag}_ms", [P, NT])
            self.rn = m.sb(f"{tag}_rn", [P, NT])
            self.xn = m.sb(f"{tag}_xn", [P, NT, D])
        self.stats = m.sem(f"{tag}_stats")
        self.rooted = m.sem(f"{tag}_rooted")
        self.normed = m.sem(f"{tag}_normed")
        self.turned = m.sem(f"{tag}_turned")
        self.kept = [m.sem(f"{tag}_kept0"), m.sem(f"{tag}_kept1")]

    def vector(self, dve, more=None):
        v = self.nc.vector
        for i in range(NT):
            v.bn_stats(out=self.st[:, i, :], in_=self.x[:, i, :]).then_inc(self.stats, 1)
        for i in range(NT):
            dve.wait_ge(self.stats, i + 1)
            v.bn_aggr(out=self.mv[:, i, :], in_=self.st[:, i, :]).then_inc(self.stats, 1)
        dve.wait_ge(self.stats, 2 * NT)
        v.tensor_scalar(self.ve[:, :], self.mv[:, :, 1], LN_EPS, None, ALU.add).then_inc(self.stats, 1)
        dve.wait_ge(self.rooted, 1)
        v.reciprocal(self.rstd[:, :], self.sd[:, :]).then_inc(self.stats, 1)
        dve.wait_ge(self.stats, 2 * NT + 2)
        src = self.xh
        n = 0
        if self.rms:
            v.tensor_tensor(self.ms[:, :], self.mv[:, :, 1], self.rstd[:, :], ALU.mult).then_inc(self.stats, 1)
            dve.wait_ge(self.stats, 2 * NT + 3)
            v.tensor_tensor(self.ms[:, :], self.ms[:, :], self.rstd[:, :], ALU.mult).then_inc(self.stats, 1)
            dve.wait_ge(self.stats, 2 * NT + 4)
            v.tensor_scalar(self.ms[:, :], self.ms[:, :], LN_EPS, None, ALU.add).then_inc(self.stats, 1)
            dve.wait_ge(self.rooted, 2)
            v.reciprocal(self.rn[:, :], self.sd[:, :]).then_inc(self.stats, 1)
            dve.wait_ge(self.stats, 2 * NT + 6)
            src = self.xn
        for i in range(NT):
            v.tensor_scalar(self.xh[:, i, :], self.x[:, i, :], self.mv[:, i, 0:1], self.rstd[:, i:i + 1],
                            ALU.subtract, ALU.mult).then_inc(self.normed, 1)
            if self.rms:
                dve.wait_ge(self.normed, 2 * i + 1)
                v.tensor_scalar(self.xn[:, i, :], self.xh[:, i, :], self.rn[:, i:i + 1], None,
                                ALU.mult).then_inc(self.normed, 1)
            if i % 4 == 3:
                g = i // 4
                if g >= 1:
                    self._keep(dve, v, g - 1, 1)
        self._keep(dve, v, NT // 4 - 1, 1)

    def _keep(self, eng, e, g, kc):
        eng.wait_ge(self.turned, g + 1)
        src, dst = self.banks[2 * (g % 2) + kc][:, :], self.xT[:, kc, g * 512:(g + 1) * 512]
        if self.col_scale is not None:
            s = self.col_scale[:, kc:kc + 1]
            if kc == 0:
                ins = e.activation(dst, src, ACT.Identity, scale=s)
            else:
                ins = e.tensor_scalar(dst, src, s, None, ALU.mult)
        else:
            ins = e.activation(dst, src, ACT.Identity) if kc == 0 else e.tensor_copy(dst, src)
        ins.then_inc(self.kept[kc], 1)

    def scalar(self, act):
        s = self.nc.scalar
        act.wait_ge(self.stats, 2 * NT + 1)
        s.activation(self.sd[:, :], self.ve[:, :], ACT.Sqrt).then_inc(self.rooted, 1)
        if self.rms:
            act.wait_ge(self.stats, 2 * NT + 5)
            s.activation(self.sd[:, :], self.ms[:, :], ACT.Sqrt).then_inc(self.rooted, 1)
        for g in range(NT // 4):
            self._keep(act, s, g, 0)

    def tensor(self, pe):
        src = self.xn if self.rms else self.xh
        per = 2 if self.rms else 1
        for g in range(NT // 4):
            pe.wait_ge(self.normed, per * 4 * (g + 1))
            if g >= 2:
                pe.wait_ge(self.kept[0], g - 1)
                pe.wait_ge(self.kept[1], g - 1)
            for kc in range(KC):
                for j in range(4):
                    mm = self.nc.tensor.transpose(self.banks[2 * (g % 2) + kc][:, j * P:(j + 1) * P],
                                                  src[:, 4 * g + j, kc * P:(kc + 1) * P], self.ident[:, :])
            mm.then_inc(self.turned, 1)

    def done(self, eng, groups=NT // 4):
        eng.wait_ge(self.kept[0], groups)
        eng.wait_ge(self.kept[1], groups)


class NormOut:

    def __init__(self, nc, m, tag, x, out):
        self.nc, self.x, self.out = nc, x, out
        self.st = m.sb(f"{tag}_st", [P, NT, 6])
        self.mv = m.sb(f"{tag}_mv", [P, NT, 2])
        self.ve = m.sb(f"{tag}_ve", [P, NT])
        self.sd = m.sb(f"{tag}_sd", [P, NT])
        self.rstd = m.sb(f"{tag}_rstd", [P, NT])
        self.tmp = m.sb(f"{tag}_tmp", [P, 2, D])
        self.stats = m.sem(f"{tag}_stats")
        self.rooted = m.sem(f"{tag}_rooted")
        self.scaled = m.sem(f"{tag}_scaled")
        self.added = m.sem(f"{tag}_added")

    def vector(self, dve, ready=None):
        v = self.nc.vector
        for i in range(NT):
            if ready is not None:
                ready(i)
            v.bn_stats(out=self.st[:, i, :], in_=self.out[:, i, :]).then_inc(self.stats, 1)
        for i in range(NT):
            dve.wait_ge(self.stats, i + 1)
            v.bn_aggr(out=self.mv[:, i, :], in_=self.st[:, i, :]).then_inc(self.stats, 1)
        dve.wait_ge(self.stats, 2 * NT)
        v.tensor_scalar(self.ve[:, :], self.mv[:, :, 1], LN_EPS, None, ALU.add).then_inc(self.stats, 1)
        dve.wait_ge(self.rooted, 1)
        v.reciprocal(self.rstd[:, :], self.sd[:, :]).then_inc(self.stats, 1)
        dve.wait_ge(self.stats, 2 * NT + 2)
        for i in range(NT + 1):
            if i < NT:
                if i >= 2:
                    dve.wait_ge(self.added, i - 1)
                v.tensor_scalar(self.tmp[:, i % 2, :], self.out[:, i, :], self.mv[:, i, 0:1], self.rstd[:, i:i + 1],
                                ALU.subtract, ALU.mult).then_inc(self.scaled, 1)
            if i >= 1:
                dve.wait_ge(self.scaled, i)
                v.tensor_tensor(self.x[:, i - 1, :], self.x[:, i - 1, :], self.tmp[:, (i - 1) % 2, :],
                                ALU.add).then_inc(self.added, 1)

    def scalar(self, act):
        act.wait_ge(self.stats, 2 * NT + 1)
        self.nc.scalar.activation(self.sd[:, :], self.ve[:, :], ACT.Sqrt).then_inc(self.rooted, 1)


def stage_recurrence(nc, x, ident, banks, w_in, w_out, vecs, out_b):
    PROJ = 5
    ctx = ExitStack()
    with ctx:
        m = Pools(nc, ctx)
        wi = m.sb("ra_wi", [P, KC, PROJ, D])
        wo = m.sb("ra_wo", [P, KC, D])
        vec = m.sb("ra_vec", [P, 2, KC])
        bias = m.sb("ra_bias", [P, D])
        xT = m.sb("ra_xT", [P, KC, T])
        xh = m.sb("ra_xh", [P, NT, D])
        sig = m.sb("ra_sig", [P, 2, 3, L])
        u = m.sb("ra_u", [P, 2, L])
        h = m.sb("ra_h", [P, 2, L])
        sc = m.sb("ra_sc", [P, 2, L])
        yT = m.sb("ra_yT", [P, 2, KC, L])
        pj, po = banks[0:5], banks[5:7]
        nin = NormIn(nc, m, "ra_in", x, ident, xT, xh, banks[0:4], rms=True, col_scale=vec[:, 0, :])
        nout = NormOut(nc, m, "ra_out", x, xh)
        loaded = m.sem("ra_loaded")
        projected = m.sem("ra_projected")
        squashed = m.sem("ra_squashed")
        gated = m.sem("ra_gated")
        mixed = m.sem("ra_mixed")
        summed = m.sem("ra_summed")
        R = B * KC
        block = ctx.enter_context(nc.Block())

        @block.sync
        def _(sp):
            sp.dma_start(vec[:, :, :], vecs).then_inc(loaded, 16)
            sp.dma_start(wi[:, :, :, :], w_in).then_inc(loaded, 16)
            sp.dma_start(wo[:, :, :], w_out).then_inc(loaded, 16)
            sp.dma_start(bias[:, :], out_b.partition_broadcast(P)).then_inc(loaded, 16)

        @block.tensor
        def _(pe):
            nin.tensor(pe)
            pe.wait_ge(loaded, 64)

            def outputs(b):
                pe.wait_ge(gated, 5 * (KC * b + KC))
                for j in range(L // P):
                    i = b * (L // P) + j
                    if i >= 2:
                        pe.wait_ge(summed, 2 * (i - 2) + 1)
                    for kc in range(KC):
                        mm = nc.tensor.matmul(po[i % 2][:, 0:D], yT[:, b % 2, kc, j * P:(j + 1) * P], wo[:, kc, :],
                                              start=kc == 0, stop=kc == KC - 1)
                    mm.then_inc(mixed, 1)

            for r in range(R):
                b, c = r // KC, r % KC
                nin.done(pe, b + 1) if r else nin.done(pe)
                for p in range(PROJ):
                    if r:
                        if p in (0, 1):
                            pe.wait_ge(squashed, 3 * (r - 1) + p + 1)
                        elif p == 2:
                            pe.wait_ge(gated, 5 * (r - 1) + 1)
                        elif p == 3:
                            pe.wait_ge(gated, 5 * (r - 1) + 3)
                            pe.wait_ge(squashed, 3 * r)
                        else:
                            pe.wait_ge(gated, 5 * (r - 1) + 4)
                    for kc in range(KC):
                        mm = nc.tensor.matmul(pj[p][:, :], wi[:, kc, p, c * P:(c + 1) * P],
                                              xT[:, kc, b * L:(b + 1) * L], start=kc == 0, stop=kc == KC - 1)
                    mm.then_inc(projected, 1)
                if r % KC == KC - 1 and b >= 1:
                    outputs(b - 1)
            outputs(B - 1)

        @block.scalar
        def _(act):
            act.wait_ge(loaded, 64)
            nin.scalar(act)
            for r in range(R):
                c = r % KC
                if r >= 2:
                    act.wait_ge(gated, 5 * (r - 1))
                act.wait_ge(projected, PROJ * r + 1)
                nc.scalar.activation(sig[:, r % 2, 0, :], pj[0][:, :], ACT.Sigmoid,
                                     bias=vec[:, 1, c:c + 1]).then_inc(squashed, 1)
                act.wait_ge(projected, PROJ * r + 2)
                nc.scalar.activation(sig[:, r % 2, 1, :], pj[1][:, :], ACT.Sigmoid).then_inc(squashed, 1)
                act.wait_ge(projected, PROJ * r + 4)
                nc.scalar.activation(sig[:, r % 2, 2, :], pj[3][:, :], ACT.Sigmoid).then_inc(squashed, 1)
            nout.scalar(act)

        @block.vector
        def _(dve):
            dve.wait_ge(loaded, 64)
            nin.vector(dve)
            v = nc.vector

            def outputs(b):
                for j in range(L // P):
                    i = b * (L // P) + j
                    dve.wait_ge(mixed, i + 1)
                    v.tensor_tensor(xh[:, i, :], po[i % 2][:, 0:D], xh[:, i, :], ALU.add).then_inc(summed, 1)
                    dve.wait_ge(summed, 2 * i + 1)
                    v.tensor_tensor(xh[:, i, :], xh[:, i, :], bias[:, :], ALU.add).then_inc(summed, 1)

            for r in range(R):
                b, c, q = r // KC, r % KC, r % 2
                dve.wait_ge(squashed, 3 * r + 2)
                dve.wait_ge(projected, PROJ * r + 3)
                v.tensor_tensor(u[:, q, :], pj[2][:, :], sig[:, q, 1, :], ALU.mult).then_inc(gated, 1)
                dve.wait_ge(gated, 5 * r + 1)
                v.tensor_tensor_scan(h[:, q, :], sig[:, q, 0, :], u[:, q, :], 0.0, ALU.mult, ALU.add).then_inc(gated, 1)
                dve.wait_ge(squashed, 3 * r + 3)
                v.tensor_tensor(sc[:, q, :], pj[3][:, :], sig[:, q, 2, :], ALU.mult).then_inc(gated, 1)
                dve.wait_ge(projected, PROJ * r + 5)
                dve.wait_ge(gated, 5 * r + 3)
                v.tensor_tensor(sc[:, q, :], pj[4][:, :], sc[:, q, :], ALU.mult).then_inc(gated, 1)
                dve.wait_ge(gated, 5 * r + 4)
                if c == 0 and b >= 2:
                    dve.wait_ge(mixed, (b - 1) * (L // P))
                v.tensor_tensor(yT[:, b % 2, c, :], sc[:, q, :], h[:, q, :], ALU.mult).then_inc(gated, 1)
                if c == KC - 1 and b >= 1:
                    outputs(b - 1)
            outputs(B - 1)
            nout.vector(dve, lambda i: dve.wait_ge(summed, 2 * i + 2))


E_, K_, I_ = 64, 6, 176
CAP = 32
IS_ = 2 * I_
EG = P // CAP
G_ = E_ // EG
IH = I_ // 2
SH = (0, 128, 256, IS_)
BIG = 1.0e30
ROW = D + E_


def stage_experts(nc, x, ident, bk, a):
    ctx = ExitStack()
    with ctx:
        m = Pools(nc, ctx)
        xT = m.sb("ex_xT", [P, KC, T])
        xh = m.sb("ex_xh", [P, NT, D])
        gw = m.sb("ex_gw", [P, KC, E_])
        xg = m.sb("ex_xg", [P, G_, ROW])
        early = xg[:, :, :].rearrange("p g r -> p (g r)")
        LR = NT * (E_ + 2)
        lg = early[:, 0:LR].rearrange("p (i e) -> p i e", e=E_ + 2)
        rep = early[:, LR:2 * LR].rearrange("p (i e) -> p i e", e=E_ + 2)
        mx = m.sb("ex_mx", [P, NT, 8])
        nmx = m.sb("ex_nmx", [P, NT])
        sums = m.sb("ex_sums", [P, NT])
        rs = m.sb("ex_rs", [P, NT])
        score = m.sb("ex_score", [P, NT, E_])
        ys = m.sb("ex_ys", [P, G_, D])
        key = ys[:, :, :].rearrange("p g d -> p (g d)")[0:E_, 0:T]
        k32 = m.sb("ex_k32", [E_, CAP])
        idxf = m.sb("ex_idxf", [P, G_])
        idx = m.sb("ex_idx", [P, G_], U32)
        iota = m.sb("ex_iota", [P, T])
        pick = m.sb("ex_pick", [E_, EG, G_])
        own = m.sb("ex_own", [P, G_, E_])
        zrow = m.sb("ex_zrow", [1, ROW])
        ws = m.sb("ex_ws", [P, G_])
        sw = m.sb("ex_sw", [P, KC, 2, IS_])
        swd = m.sb("ex_swd", [P, 3, D])
        ssl = m.sb("ex_ssl", [P, 2, L])
        hsh = m.sb("ex_hsh", [P, 3, T])
        NW = 2
        wgu = m.sb("ex_wgu", [P, NW, EG, KC, 2 * I_])
        wd = m.sb("ex_wd", [IH, NW, EG, 2, D])
        xgT = m.sb("ex_xgT", [P, 2, KC, P])
        sl = m.sb("ex_sl", [P, 2, I_])
        hh = m.sb("ex_hh", [P, 2, I_])
        hT = m.sb("ex_hT", [IH, 2, 2, P])
        oneh = m.sb("ex_oneh", [P, 2, G_, P])
        tab = nc.dram_tensor("ex_tab", (T + 1, ROW), F32, kind="Internal").ap()
        nin = NormIn(nc, m, "ex_in", x, ident, xT, xh, bk[0:4])
        nout = NormOut(nc, m, "ex_out", x, xh)

        loaded = m.sem("ex_loaded")
        w_in = [m.sem(f"ex_w_in{i}") for i in range(NW)]
        lit = m.sem("ex_lit")
        logits = m.sem("ex_logits")
        lg_kept = m.sem("ex_lg_kept")
        maxed = m.sem("ex_maxed")
        negm = m.sem("ex_negm")
        exped = m.sem("ex_exped")
        scored = m.sem("ex_scored")
        mask_t = m.sem("ex_mask_t")
        keyed = m.sem("ex_keyed")
        ranked = m.sem("ex_ranked")
        placed = m.sem("ex_placed")
        indexed = m.sem("ex_indexed")
        stored = m.sem("ex_stored")
        gathered = [m.sem(f"ex_gathered{i}") for i in range(G_)]
        weighed = m.sem("ex_weighed")
        sh_mm = m.sem("ex_sh_mm")
        sh_act = m.sem("ex_sh_act")
        sh_mul = m.sem("ex_sh_mul")
        xg_t = m.sem("ex_xg_t")
        xg_kept = m.sem("ex_xg_kept")
        gu_mm = m.sem("ex_gu_mm")
        gu_act = m.sem("ex_gu_act")
        gu_mul = m.sem("ex_gu_mul")
        h_t = m.sem("ex_h_t")
        h_kept = m.sem("ex_h_kept")
        d_mm = m.sem("ex_d_mm")
        y_made = m.sem("ex_y_made")
        hot = m.sem("ex_hot")
        comb = m.sem("ex_comb")
        out_made = m.sem("ex_out_made")

        pieces = [(c, g) for g in range(B) for c in range(3)]
        block = ctx.enter_context(nc.Block())

        @block.sync
        def _(sp):
            for dst, src in ((gw[:, :, :], a["ex_gw"]), (sw[:, :, :, :], a["ex_sw"]),
                             (pick[:, :, :], a["ex_pick"]), (own[:, :, :], a["ex_own"]),
                             (iota[:, :], a["ex_iota"].partition_broadcast(P))):
                sp.dma_start(dst, src).then_inc(loaded, 16)
            sp.dma_start(swd[:, 0:2, :], a["ex_swd"][0:256].rearrange("(c p) d -> p c d", p=P)).then_inc(loaded, 16)
            sp.dma_start(swd[0:96, 2, :], a["ex_swd"][256:IS_]).then_inc(loaded, 16)

            def weights(g):
                q = g % NW
                sp.dma_start(wgu[:, q, :, :, :], a["ex_wgu"][g]).then_inc(w_in[q], 16)
                sp.dma_start(wd[:, q, :, :, :], a["ex_wd"][g]).then_inc(w_in[q], 16)

            for g in range(NW):
                weights(g)
            sp.wait_ge(nin.normed, NT)
            sp.dma_start(tab[0:T, 0:D].rearrange("(i p) d -> p i d", p=P), xh[:, :, :]).then_inc(stored, 16)
            sp.wait_ge(lit, 1)
            sp.dma_start(tab[T:T + 1, :], zrow[:, :]).then_inc(stored, 16)
            sp.wait_ge(scored, 2)
            sp.dma_start(tab[0:T, D:ROW].rearrange("(i p) e -> p i e", p=P), score[:, :, :]).then_inc(stored, 16)
            for g in range(NW, G_):
                sp.wait_ge(d_mm, g - NW + 1)
                weights(g)
            sp.wait_ge(stored, 48)

        @block.tensor
        def _(pe):
            mmul, turn = nc.tensor.matmul, nc.tensor.transpose
            nin.tensor(pe)
            pe.wait_ge(loaded, 112)
            nin.done(pe)
            for i in range(NT):
                for kc in range(KC):
                    mm = mmul(bk[4 + i // 8][:, (i % 8) * E_:(i % 8 + 1) * E_], xT[:, kc, i * P:(i + 1) * P],
                              gw[:, kc, :], start=kc == 0, stop=kc == KC - 1)
            mm.then_inc(logits, 1)

            def shared(n):
                c, g = pieces[n]
                c0, c1 = SH[c], SH[c + 1]
                for s in range(2):
                    if n:
                        pe.wait_ge(sh_mul, n) if s else pe.wait_ge(sh_act, n)
                    for kc in range(KC):
                        mm = mmul(bk[6 + s][0:c1 - c0, :], sw[:, kc, s, c0:c1], xT[:, kc, g * L:(g + 1) * L],
                                  start=kc == 0, stop=kc == KC - 1)
                    mm.then_inc(sh_mm, 1)

            for n in range(3):
                shared(n)
            for g in range(B):
                for j in range(4):
                    i = 4 * g + j
                    pe.wait_ge(maxed, 3 * i + 3)
                    mm = turn(bk[g][0:E_, j * P:(j + 1) * P], rep[:, i, 0:E_], ident[:, :])
                mm.then_inc(mask_t, 1)
            for n in range(3, len(pieces)):
                shared(n)
            pe.wait_ge(ranked, 7)
            for e in range(EG):
                mm = mmul(bk[4][e * CAP:(e + 1) * CAP, 0:G_], k32[:, :], pick[:, e, :], start=True, stop=True)
            mm.then_inc(placed, 1)

            def turn_x(g):
                pe.wait_ge(gathered[g], 16)
                if g == 0:
                    pe.wait_ge(keyed, 4)
                if g >= 1:
                    pe.wait_ge(xg_kept, g)
                for kc in range(KC):
                    mm = turn(bk[2][:, kc * P:(kc + 1) * P], xg[:, g, kc * P:(kc + 1) * P], ident[:, :])
                mm.then_inc(xg_t, 1)

            def gate_up(g):
                q = g % NW
                pe.wait_ge(xg_kept, g + 1)
                pe.wait_ge(w_in[q], 32 * (g // NW + 1))
                if g >= 2:
                    pe.wait_ge(gu_mul, g - 1)
                for kc in range(KC):
                    for e in range(EG):
                        mm = mmul(bk[g % 2][e * CAP:(e + 1) * CAP, 0:2 * I_], xgT[:, g % 2, kc, e * CAP:(e + 1) * CAP],
                                  wgu[:, q, e, kc, :], start=kc == 0, stop=kc == KC - 1)
                mm.then_inc(gu_mm, 1)

            def down(g):
                q = g % NW
                pe.wait_ge(gu_mul, g + 1)
                if g >= 1:
                    pe.wait_ge(h_kept, g)
                for c in range(2):
                    mm = turn(bk[3][0:IH, c * P:(c + 1) * P], hh[:, g % 2, c * IH:(c + 1) * IH], ident[:, :])
                mm.then_inc(h_t, 1)
                pe.wait_ge(h_kept, g + 1)
                pe.wait_ge(indexed, 1)
                if g >= 2:
                    pe.wait_ge(y_made, g - 1)
                for c in range(2):
                    for e in range(EG):
                        mm = mmul(bk[4 + g % 2][e * CAP:(e + 1) * CAP, 0:D], hT[:, g % 2, c, e * CAP:(e + 1) * CAP],
                                  wd[:, q, e, c, :], start=c == 0, stop=c == 1)
                mm.then_inc(d_mm, 1)

            turn_x(0)
            for g in range(G_):
                if g + 1 < G_:
                    turn_x(g + 1)
                gate_up(g)
                if g >= 1:
                    down(g - 1)
            down(G_ - 1)
            pe.wait_ge(y_made, G_)
            pe.wait_ge(sh_mul, len(pieces))
            for i in range(NT):
                pe.wait_ge(hot, i + 1)
                if i >= 2:
                    pe.wait_ge(out_made, i - 1)
                o = bk[6 + i % 2][:, 0:D]
                for g in range(G_):
                    mmul(o, oneh[:, i % 2, g, :], ys[:, g, :], start=g == 0, stop=False)
                for c in range(3):
                    k = SH[c + 1] - SH[c]
                    mm = mmul(o, hsh[0:k, c, i * P:(i + 1) * P], swd[0:k, c, :], start=False, stop=c == 2)
                mm.then_inc(comb, 1)

        @block.vector
        def _(dve):
            v = nc.vector
            v.memset(lg[:, :, E_:E_ + 2], BIG).then_inc(lg_kept, 1)
            nin.vector(dve)

            def shared(n):
                c, g = pieces[n]
                k = SH[c + 1] - SH[c]
                dve.wait_ge(sh_act, n + 1)
                dve.wait_ge(sh_mm, 2 * n + 2)
                v.tensor_tensor(hsh[0:k, c, g * L:(g + 1) * L], ssl[0:k, n % 2, :], bk[7][0:k, :],
                                ALU.mult).then_inc(sh_mul, 1)

            dve.wait_ge(logits, 1)
            for s in range(2):
                v.tensor_copy(lg[:, 8 * s:8 * s + 8, 0:E_], bk[4 + s][:, :].rearrange("p (i e) -> p i e", e=E_)).then_inc(lg_kept, 1)
            dve.wait_ge(lg_kept, 3)
            for i in range(NT):
                v.max(out=mx[:, i, :], in_=lg[:, i, :]).then_inc(maxed, 1)
                dve.wait_ge(maxed, 3 * i + 1)
                v.match_replace(out=rep[:, i, :], in_to_replace=mx[:, i, :], in_values=lg[:, i, :],
                                imm_value=-BIG).then_inc(maxed, 1)
                dve.wait_ge(maxed, 3 * i + 2)
                v.tensor_scalar(rep[:, i, :], rep[:, i, :], -BIG, None, ALU.is_equal).then_inc(maxed, 1)
            v.tensor_scalar(nmx[:, :], mx[:, :, 2], -1.0, None, ALU.mult).then_inc(negm, 1)
            for n in range(3):
                shared(n)
            dve.wait_ge(loaded, 112)
            for g in range(B):
                dve.wait_ge(mask_t, g + 1)
                v.scalar_tensor_tensor(out=key[:, g * L:(g + 1) * L], in0=iota[0:E_, g * L:(g + 1) * L],
                                       scalar=float(T), in1=bk[g][0:E_, :], op0=ALU.subtract,
                                       op1=ALU.mult).then_inc(keyed, 1)
            dve.wait_ge(keyed, 4)
            v.tensor_scalar(key, key, -1.0, None, ALU.mult).then_inc(keyed, 1)
            dve.wait_ge(keyed, 5)
            for r in range(CAP // 8):
                if r:
                    v.match_replace(out=key, in_to_replace=k32[:, 8 * r - 8:8 * r], in_values=key,
                                    imm_value=0.0).then_inc(ranked, 1)
                    shared(2 * r + 2)
                    dve.wait_ge(ranked, 2 * r)
                v.max(out=k32[:, 8 * r:8 * r + 8], in_=key).then_inc(ranked, 1)
                shared(2 * r + 3)
                dve.wait_ge(ranked, 2 * r + 1)
            for n in range(2 * CAP // 8 + 2, len(pieces)):
                shared(n)
            dve.wait_ge(exped, NT)
            v.reciprocal(rs[:, :], sums[:, :]).then_inc(scored, 1)
            dve.wait_ge(scored, 1)
            v.tensor_tensor(score[:, :, :], score[:, :, :], rs[:, :].unsqueeze(2).to_broadcast([P, NT, E_]),
                            ALU.mult).then_inc(scored, 1)
            dve.wait_ge(placed, 1)
            v.tensor_scalar(idxf[:, :], bk[4][:, 0:G_], -1.0, float(T), ALU.mult, ALU.add).then_inc(indexed, 1)
            dve.wait_ge(indexed, 1)
            v.tensor_copy(idx[:, :], idxf[:, :]).then_inc(indexed, 1)
            for g in range(G_):
                dve.wait_ge(gathered[g], 16)
            v.tensor_tensor(own[:, :, :], own[:, :, :], xg[:, :, D:ROW], ALU.mult).then_inc(weighed, 1)
            dve.wait_ge(weighed, 1)
            v.tensor_reduce(ws[:, :], own[:, :, :], AX.X, ALU.add).then_inc(weighed, 1)
            dve.wait_ge(weighed, 2)

            def one_hot(i):
                if i >= 2:
                    dve.wait_ge(comb, i - 1)
                v.tensor_tensor(oneh[:, i % 2, :, :], iota[:, i * P:(i + 1) * P].unsqueeze(1).to_broadcast([P, G_, P]),
                                idxf[:, :].unsqueeze(2).to_broadcast([P, G_, P]), ALU.is_equal).then_inc(hot, 1)

            for g in range(G_ + 1):
                if g < G_:
                    dve.wait_ge(gu_act, g + 1)
                    if g >= 2:
                        dve.wait_ge(h_t, g - 1)
                    v.tensor_tensor(hh[:, g % 2, :], sl[:, g % 2, :], bk[g % 2][:, I_:2 * I_], ALU.mult).then_inc(gu_mul, 1)
                if g >= 1:
                    dve.wait_ge(d_mm, g)
                    v.tensor_scalar(ys[:, g - 1, :], bk[4 + (g - 1) % 2][:, 0:D], ws[:, g - 1:g], None,
                                    ALU.mult).then_inc(y_made, 1)
            for i in range(NT):
                one_hot(i)
            nout.vector(dve, lambda i: dve.wait_ge(out_made, i + 1))

        @block.scalar
        def _(act):
            s_ = nc.scalar
            nin.scalar(act)
            act.wait_ge(negm, 1)
            for i in range(NT):
                s_.activation(score[:, i, :], lg[:, i, 0:E_], ACT.Exp, bias=nmx[:, i:i + 1],
                              accum_out=sums[:, i:i + 1]).then_inc(exped, 1)
            for n, (c, g) in enumerate(pieces):
                k = SH[c + 1] - SH[c]
                act.wait_ge(sh_mm, 2 * n + 1)
                if n >= 2:
                    act.wait_ge(sh_mul, n - 1)
                s_.activation(ssl[0:k, n % 2, :], bk[6][0:k, :], ACT.Silu).then_inc(sh_act, 1)

            def keep_x(g):
                act.wait_ge(xg_t, g + 1)
                if g >= 2:
                    act.wait_ge(gu_mm, g - 1)
                s_.activation(xgT[:, g % 2, :, :], bk[2][:, 0:KC * P].rearrange("p (c t) -> p c t", c=KC),
                              ACT.Identity).then_inc(xg_kept, 1)

            def keep_h(g):
                act.wait_ge(h_t, g + 1)
                if g >= 2:
                    act.wait_ge(d_mm, g - 1)
                s_.activation(hT[:, g % 2, :, :], bk[3][0:IH, 0:2 * P].rearrange("p (c t) -> p c t", c=2),
                              ACT.Identity).then_inc(h_kept, 1)

            keep_x(0)
            for g in range(G_):
                if g + 1 < G_:
                    keep_x(g + 1)
                act.wait_ge(gu_mm, g + 1)
                if g >= 2:
                    act.wait_ge(gu_mul, g - 1)
                s_.activation(sl[:, g % 2, :], bk[g % 2][:, 0:I_], ACT.Silu).then_inc(gu_act, 1)
                if g >= 1:
                    keep_h(g - 1)
            keep_h(G_ - 1)
            for i in range(NT):
                act.wait_ge(comb, i + 1)
                s_.activation(xh[:, i, :], bk[6 + i % 2][:, 0:D], ACT.Identity).then_inc(out_made, 1)
            nout.scalar(act)

        @block.gpsimd
        def _(pool):
            nc.gpsimd.memset(zrow[:, :], 0.0).then_inc(lit, 1)
            pool.wait_ge(indexed, 2)
            pool.wait_ge(stored, 48)
            for g in range(G_):
                nc.gpsimd.indirect_dma_start(out=xg[:, g, :], out_offset=None, in_=tab,
                                             in_offset=bass.IndirectOffsetOnAxis(ap=idx[:, g:g + 1], axis=0)
                                             ).then_inc(gathered[g], 16)


def laid_out_experts(g, chunks):
    e, gg = np.arange(E_), np.arange(G_)
    pick = (e[:, None, None] == EG * gg[None, None, :] + np.arange(EG)[None, :, None]).astype(np.float32)
    own = (EG * gg[None, :, None] + (np.arange(P) // CAP)[:, None, None] == e[None, None, :]).astype(np.float32)
    gu = np.concatenate([g("L0_ffn_w_gate"), g("L0_ffn_w_up")], axis=2)
    return {
        "ex_gw": chunks(g("L0_ffn_gate_w").T),
        "ex_sw": np.stack([chunks(g("L0_ffn_sw_gate")), chunks(g("L0_ffn_sw_up"))], axis=2),
        "ex_swd": g("L0_ffn_sw_down"),
        "ex_pick": pick,
        "ex_own": own,
        "ex_iota": np.arange(T, dtype=np.float32),
        "ex_wgu": gu.reshape(G_, EG, KC, P, 2 * I_).transpose(0, 3, 1, 2, 4),
        "ex_wd": g("L0_ffn_w_down").reshape(G_, EG, 2, IH, D).transpose(0, 3, 1, 2, 4),
    }


H = 16
DK = 128
TAPS = 4
TB = L // P
LEVELS = 7
L2_EPS = 1e-6


def tot_at(j):
    return sum(L >> i for i in range(j))


def right(ap, j):
    w = 1 << j
    if len(ap.shape) == 2:
        return ap.rearrange("p (n s w) -> p n s w", s=2, w=w)[:, :, 1, :]
    return ap.rearrange("p q (n s w) -> p q n s w", s=2, w=w)[:, :, :, 1, :]


def left(ap, j):
    w = 1 << j
    if len(ap.shape) == 2:
        return ap.rearrange("p (n s w) -> p n s w", s=2, w=w)[:, :, 0, :]
    return ap.rearrange("p q (n s w) -> p q n s w", s=2, w=w)[:, :, :, 0, :]


def dense(ap, j):
    w = 1 << j
    if len(ap.shape) == 2:
        return ap.rearrange("p (n w) -> p n w", w=w)
    return ap.rearrange("p q (n w) -> p q n w", w=w)


def stage_delta(nc, x, ident, banks, a):
    ctx = ExitStack()
    with ctx:
        m = Pools(nc, ctx)
        acc = m.sb("da_acc", [P, NT, D])
        nout = NormOut(nc, m, "da_out", x, acc)
        faT = m.sb("da_faT", [P, T])
        gaT = m.sb("da_gaT", [P, T])
        xT = m.sb("da_xT", [P, KC, T])
        beta = m.sb("da_beta", [P, H + 1, NT])
        negA = m.sb("da_negA", [P, H + 1])

        with ExitStack() as c2:
            m2 = Pools(nc, c2)
            xh = m2.sb("da_xh", [P, NT, D])
            wfga = m2.sb("da_wfga", [P, KC, 2, DK])
            wb = m2.sb("da_wb", [P, KC, H + 1])
            alog = m2.sb("da_alog", [P, H + 1])
            nin = NormIn(nc, m2, "da_in", x, ident, xT, xh, banks[0:4])
            loaded = m2.sem("da_loaded")
            inner = m2.sem("da_inner")
            inner_kept = m2.sem("da_inner_kept")
            beta_mm = m2.sem("da_beta_mm")
            done = m2.sem("da_small")
            with nc.Block() as block:
                @block.sync
                def _(sp):
                    sp.dma_start(wfga[:, :, :, :], a["da_wfga"]).then_inc(loaded, 16)
                    sp.dma_start(wb[:, :, :], a["da_wb"]).then_inc(loaded, 16)
                    sp.dma_start(alog[:, :], a["da_alog"].partition_broadcast(P)).then_inc(loaded, 16)

                @block.tensor
                def _(pe):
                    nin.tensor(pe)
                    pe.wait_ge(loaded, 48)
                    for b in range(B):
                        nin.done(pe, b + 1) if b else nin.done(pe)
                        for s in range(2):
                            g = 2 * b + s
                            if g >= 2:
                                pe.wait_ge(inner_kept, g - 1)
                            for kc in range(KC):
                                mm = nc.tensor.matmul(banks[4 + s][:, :], wfga[:, kc, s, :],
                                                      xT[:, kc, b * L:(b + 1) * L], start=kc == 0, stop=kc == KC - 1)
                            mm.then_inc(inner, 1)
                    for i in range(NT):
                        for kc in range(KC):
                            mm = nc.tensor.matmul(banks[6][:, i * (H + 1):(i + 1) * (H + 1)], xT[:, kc, i * P:(i + 1) * P],
                                                  wb[:, kc, :], start=kc == 0, stop=kc == KC - 1)
                    mm.then_inc(beta_mm, 1)

                @block.scalar
                def _(act):
                    nin.scalar(act)
                    for b in range(B):
                        for s, dst in enumerate((faT, gaT)):
                            act.wait_ge(inner, 2 * b + s + 1)
                            nc.scalar.activation(dst[:, b * L:(b + 1) * L], banks[4 + s][:, :],
                                                 ACT.Identity).then_inc(inner_kept, 1)
                    act.wait_ge(beta_mm, 1)
                    nc.scalar.activation(beta[:, :, :].rearrange("p h i -> p i h"),
                                         banks[6][:, 0:NT * (H + 1)].rearrange("p (i h) -> p i h", h=H + 1), ACT.Sigmoid)
                    act.wait_ge(loaded, 48)
                    nc.scalar.activation(alog[:, :], alog[:, :], ACT.Exp).then_inc(done, 1)

                @block.vector
                def _(dve):
                    nin.vector(dve)
                    dve.wait_ge(done, 1)
                    nc.vector.tensor_scalar(negA[:, :], alog[:, :], -1.0, None, ALU.mult)

                @block.gpsimd
                def _(pool):
                    nc.gpsimd.memset(acc[:, :, :], 0.0)

        w = m.sb("da_w", [P, KC, 3, DK])
        wfg = m.sb("da_wfg", [P, 2, DK])
        hc = m.sb("da_hc", [P, 3 * TAPS + 1])
        wo_raw = m.sb("da_wo_raw", [P, D])
        wo = m.sb("da_wo", [P, D])
        onw = m.sb("da_onw", [P, 1])
        mask = m.sb("da_mask", [P, LEVELS, P // 2])
        ones = m.sb("da_ones", [P, 1])
        y = m.sb("da_y", [P, 3, L])
        vc = m.sb("da_vc", [P, L])
        sqr = m.sb("da_sqr", [P, 3, L])
        gx = m.sb("da_gx", [P, 2, L])
        kq = m.sb("da_kq", [P, 2, 2, L])
        dec = m.sb("da_dec", [P, 2, 2 * L])
        Vt = m.sb("da_Vt", [P, 2, TB, DK])
        sg = m.sb("da_sg", [P, 2, L])
        st = m.sb("da_st", [P, 2, 5, TB])
        rt = m.sb("da_rt", [P, 2, TB])
        kqP = m.sb("da_kqP", [P, 2, 2, L])
        kQ = m.sb("da_kQ", [P, 2, L])
        kQt = m.sb("da_kQt", [P, TB, DK])
        AT = m.sb("da_AT", [P, LEVELS, TB, P])
        Yf = m.sb("da_Yf", [P, LEVELS, TB, P])
        M = m.sb("da_M", [P, TB, P // 2])
        MT = m.sb("da_MT", [P, 2, TB, P])
        AqT = m.sb("da_AqT", [P, 2, TB, P])
        Rb = m.sb("da_R", [P, DK])
        U = m.sb("da_U", [P, 2, DK])
        S = m.sb("da_S", [P, 2, DK])
        og = m.sb("da_og", [P, L])
        osq = m.sb("da_osq", [P, L])
        ca = m.sb("da_ca", [P, 3, TB])
        pp, pa, pY, pM, pZT, pS, pO = banks[0:2], banks[2], banks[3], banks[4], banks[5], banks[6], banks[7]
        pR, pU, pSn = pS[:, 0:DK], pS[:, DK:2 * DK], pS[:, 2 * DK:3 * DK]

        consts = m.sem("da_consts")
        zeroed = m.sem("da_zeroed")
        onw_half = m.sem("da_onw_half")
        head_used = m.sem("da_head_used")
        w_in = m.sem("da_w_in")
        wo_in = m.sem("da_wo_in")
        wo_scaled = m.sem("da_wo_scaled")
        proj = [m.sem(f"da_proj_{s}") for s in "qkvfg"]
        tap0 = [m.sem(f"da_tap0_{s}") for s in "qkv"]
        tapped = [m.sem(f"da_tapped_{s}") for s in "qkv"]
        silud = [m.sem(f"da_silu_{s}") for s in "qkv"]
        squared = m.sem("da_squared")
        kq_mul = m.sem("da_kq_mul")
        gate_in = m.sem("da_gate_in")
        gate_ln = m.sem("da_gate_ln")
        gate_sp = m.sem("da_gate_sp")
        gate_out = m.sem("da_gate_out")
        tanhd = m.sem("da_tanhd")
        stat_mm = m.sem("da_stat_mm")
        stat_v = m.sem("da_stat_v")
        rooted = m.sem("da_rooted")
        v_turned = m.sem("da_v_turned")
        v_kept = m.sem("da_v_kept")
        kqP_begun = m.sem("da_kqP_begun")
        kQ_begun = m.sem("da_kQ_begun")
        tot = m.sem("da_tot")
        scaled = m.sem("da_scaled")
        pairs = m.sem("da_pairs")
        start = m.sem("da_start")
        masked = m.sem("da_masked")
        y_mm = m.sem("da_y_mm")
        y_kept = m.sem("da_y_kept")
        zt_mm = m.sem("da_zt_mm")
        grownT = m.sem("da_grownT")
        m_turned = m.sem("da_m_turned")
        m_kept = m.sem("da_m_kept")
        kq_turned = m.sem("da_kq_turned")
        kq_kept = m.sem("da_kq_kept")
        r_mm = m.sem("da_r_mm")
        r_made = m.sem("da_r_made")
        u_mm = m.sem("da_u_mm")
        u_kept = m.sem("da_u_kept")
        s_mm = m.sem("da_s_mm")
        s_made = m.sem("da_s_made")
        o_mm = m.sem("da_o_mm")
        og_made = m.sem("da_og_made")
        osq_made = m.sem("da_osq_made")
        so_mm = m.sem("da_so_mm")
        ca_v = m.sem("da_ca_v")
        ca_s = m.sem("da_ca_s")
        wo_mm = m.sem("da_wo_mm")
        acc_made = m.sem("da_acc_made")
        CREDIT = {"DVE": ((grownT, 7), (masked, 14), (acc_made, 4)), "ACT": ((v_kept, 1), (kq_kept, 1))}
        ZEROED = 12

        block = ctx.enter_context(nc.Block())

        @block.sync
        def _(sp):
            sp.dma_start(mask[:, :, :], a["da_mask"]).then_inc(consts, 16)
            sp.dma_start(onw[:, :], a["da_onw"]).then_inc(consts, 16)

            def load_head(h):
                sp.dma_start(w[:, :, :, :], a["da_wqkv"][h]).then_inc(w_in, 16)
                sp.dma_start(wfg[:, :, :], a["da_wfgb"][h]).then_inc(w_in, 16)
                sp.dma_start(hc[:, :], a["da_hc"][h]).then_inc(w_in, 16)

            load_head(0)
            sp.dma_start(wo_raw[:, :], a["da_wo"][0]).then_inc(wo_in, 16)
            with sp.Fori(0, H) as h:
                n1 = h * B + B
                sp.wait_ge(wo_scaled, h + 1)
                sp.sem_inc(head_used, 1)
                sp.wait_ge(proj[4], n1)
                for s in range(3):
                    sp.wait_ge(tapped[s], h * (3 * B) + 3 * B)
                sp.wait_ge(gate_in, n1)
                sp.sem_inc(head_used, 1)
                load_head(h + 1)
                sp.dma_start(wo_raw[:, :], a["da_wo"][h + 1]).then_inc(wo_in, 16)
            sp.wait_ge(w_in, 48 * (H + 1))
            sp.wait_ge(wo_in, 16 * (H + 1))

        @block.tensor
        def _(pe):
            mmul, turn = nc.tensor.matmul, nc.tensor.transpose

            def project(s, n, b, half=None):
                if half == 1:
                    pass
                elif s == 0 and not isinstance(n, int):
                    pe.wait_ge(v_kept, n + 1)
                elif s == 3 and not isinstance(n, int):
                    pe.wait_ge(kq_kept, n)
                elif s == 1:
                    pe.wait_ge(gate_in, n + 1)
                elif s == 2:
                    pe.wait_ge(tapped[0], 3 * n + 3)
                elif s == 4:
                    pe.wait_ge(tapped[1], 3 * n + 3)
                out = pp[(0, 1, 0, 1, 1)[s]][:, :]
                if s < 3:
                    for kc in range(KC) if half is None else (half,):
                        mm = mmul(out, w[:, kc, s, :], xT[:, kc, b * L:(b + 1) * L], start=kc == 0, stop=kc == KC - 1)
                else:
                    mm = mmul(out, wfg[:, s - 3, :], (faT, gaT)[s - 3][:, b * L:(b + 1) * L], start=True, stop=True)
                if half != 0:
                    mm.then_inc(proj[s], 1)

            def sums(n, parts=(0, 1, 2)):
                if parts[0] == 0:
                    pe.wait_ge(squared, n + 1)
                    pe.wait_ge(kq_mul, n + 1)
                    pe.wait_ge(tanhd, n + 1)
                for s in parts:
                    for i in range(TB):
                        mm = mmul(pp[1][:, s * TB + i:s * TB + i + 1], sqr[:, s, i * P:(i + 1) * P], ones[:, :],
                                  start=True, stop=True)
                if parts[-1] == 2:
                    mm.then_inc(stat_mm, 1)

            def turn_v(n):
                pe.wait_ge(silud[2], n + 1)
                for i in range(TB):
                    mm = turn(pp[0][:, i * P:(i + 1) * P], vc[:, i * P:(i + 1) * P], ident[:, :])
                mm.then_inc(v_turned, 1)

            def pair(j, n, p):
                if j == 0:
                    pe.wait_ge(kqP_begun, n + 1)
                    pe.wait_ge(kQ_begun, n + 1)
                else:
                    pe.wait_ge(scaled, 14 * n + 2 * j)
                pe.wait_ge(masked, 14 * n + 14 + 2 * j)
                for i in range(TB):
                    out = pa[:, :].rearrange("p (s i t) -> p s i t", s=2, i=TB)[:, :, i, :]
                    mm = mmul(dense(out, j), kQ[:, p, i * P:(i + 1) * P], right(kqP[:, p, :, i * P:(i + 1) * P], j),
                              start=True, stop=True)
                mm.then_inc(pairs, 1)

            def level_y(j, n):
                pe.wait_ge(masked, 14 * n + 14 + 2 * j + 1)
                if j == 0:
                    pe.wait_ge(start, 3 * n + 3)
                else:
                    pe.wait_ge(m_kept, 6 * n + j)
                for i in range(TB):
                    out = pY[:, i * 64:(i + 1) * 64]
                    if j < LEVELS - 1:
                        mm = mmul(dense(out, j), AT[:, j, i, :], dense(M[:, i, :], j), start=True, stop=True)
                    else:
                        mm = mmul(out[64:P], AT[:, j, i, 64:P], M[:, i, :], start=True, stop=True)
                mm.then_inc(y_mm, 1)

            def level_zt(j, n, p):
                pe.wait_ge(y_kept, 7 * n + j + 1)
                for i in range(TB):
                    out = pZT[:, i * 64:(i + 1) * 64]
                    if j < LEVELS - 1:
                        mm = mmul(dense(out, j), Yf[:, j, i, :], right(MT[:, p, i, :], j), start=True, stop=True)
                    else:
                        mm = mmul(out[0:64], Yf[:, j, i, 0:64], MT[:, p, i, 64:P], start=True, stop=True)
                mm.then_inc(zt_mm, 1)

            def turn_m(j, n, p):
                pe.wait_ge(grownT, 7 * n + 7 + j + 1)
                for i in range(TB):
                    mm = turn(pM[:, i * P:(i + 1) * P], MT[:, p, i, :], ident[:, :])
                mm.then_inc(m_turned, 1)

            def turn_kq(n, p):
                pe.wait_ge(scaled, 14 * n + 14)
                pe.wait_ge(stat_v, 5 * n + 8)
                for i in range(TB):
                    mm = turn(pp[1][:, i * P:(i + 1) * P], kQ[:, p, i * P:(i + 1) * P], ident[:, :])
                mm.then_inc(kq_turned, 1)

            def state_r(i, n, q):
                pe.wait_ge(s_made, 3 * n + i)
                mmul(pR, kqP[:, q, 0, i * P:(i + 1) * P], S[:, i % 2, :], start=True, stop=True).then_inc(r_mm, 1)

            def state_u(i, n, q):
                if i:
                    pe.wait_ge(r_made, 3 * n + i)
                else:
                    pe.wait_ge(v_kept, n + 1)
                    pe.wait_ge(grownT, 7 * n + 7)
                    pe.wait_ge(acc_made, 4 * n + 4)
                mmul(pU, MT[:, q, i, :], Rb[:, :] if i else Vt[:, q, 0, :], start=True, stop=True).then_inc(u_mm, 1)

            def state_s(i, n, q):
                t = slice(i * P, (i + 1) * P)
                pe.wait_ge(u_kept, 4 * n + i + 1)
                if i < TB - 1:
                    if i == 0:
                        pe.wait_ge(kq_kept, n + 1)
                    mmul(pSn, kQt[:, i, :], U[:, i % 2, :], start=True, stop=True).then_inc(s_mm, 1)
                if i:
                    mmul(pO[:, t], S[:, i % 2, :], kqP[:, q, 1, t], start=True, stop=False)
                else:
                    pe.wait_ge(masked, 14 * n + 14)
                mmul(pO[:, t], U[:, i % 2, :], AqT[:, q, i, :], start=i == 0, stop=True).then_inc(o_mm, 1)

            def out_norm(n):
                pe.wait_ge(osq_made, n + 1)
                for i in range(TB):
                    mm = mmul(pO[:, i:i + 1], osq[:, i * P:(i + 1) * P], ones[:, :], start=True, stop=True)
                mm.then_inc(so_mm, 1)

            def out_mm(half, n, b, h):
                if half:
                    pe.wait_ge(ca_v, n + 1)
                elif b == 1 or isinstance(n, int):
                    pe.wait_ge(wo_scaled, h + 1)
                for i in (0, 1):
                    t = 2 * half + i
                    mm = mmul((pO if half else pS)[:, i * D:(i + 1) * D], og[:, t * P:(t + 1) * P], wo[:, :],
                              start=True, stop=True)
                mm.then_inc(wo_mm, 1)

            pe.wait_ge(zeroed, ZEROED)
            pe.wait_ge(w_in, 48)
            for s in (3, 0, 1, 2, 4):
                project(s, 0, 0)
            sums(0)
            turn_v(0)
            pair(0, 0, 0)
            with pe.Fori(0, H) as h:
                for b in range(B):
                    n, n1, b1, p, q = h * B + b, h * B + b + 1, (b + 1) % B, b % 2, (b + 1) % 2
                    level_y(0, n)
                    state_u(0, n, q)
                    pair(1, n, p)
                    state_s(0, n, q)
                    level_zt(0, n, p)
                    state_r(1, n, q)
                    if b1 == 0:
                        pe.wait_ge(w_in, 48 * (h + 2))
                    project(3, n1, b1)
                    turn_m(0, n, p)
                    state_u(1, n, q)
                    project(0, n1, b1, 0)

                    level_y(1, n)
                    state_s(1, n, q)
                    pair(2, n, p)
                    state_r(2, n, q)
                    level_zt(1, n, p)
                    state_u(2, n, q)
                    project(0, n1, b1, 1)
                    turn_m(1, n, p)
                    state_s(2, n, q)
                    project(1, n1, b1, 0)

                    level_y(2, n)
                    state_r(3, n, q)
                    pair(3, n, p)
                    state_u(3, n, q)
                    level_zt(2, n, p)
                    project(1, n1, b1, 1)
                    turn_m(2, n, p)
                    state_s(3, n, q)
                    project(2, n1, b1, 0)

                    level_y(3, n)
                    pair(4, n, p)
                    level_zt(3, n, p)
                    project(2, n1, b1, 1)
                    turn_m(3, n, p)
                    out_norm(n)

                    level_y(4, n)
                    pair(5, n, p)
                    out_mm(0, n, b, h)
                    level_zt(4, n, p)
                    out_mm(1, n, b, h)
                    turn_m(4, n, p)
                    project(4, n1, b1)

                    level_y(5, n)
                    pair(6, n, p)
                    level_zt(5, n, p)
                    sums(n1, (0,))
                    turn_m(5, n, p)
                    sums(n1, (1, 2))

                    level_y(6, n)
                    turn_v(n1)
                    level_zt(6, n, p)
                    pair(0, n1, q)
                    turn_kq(n, p)
            n = H * B
            for i in range(TB):
                if i:
                    state_r(i, n, 1)
                state_u(i, n, 1)
                state_s(i, n, 1)
            out_norm(n)
            out_mm(0, n, 0, H - 1)
            out_mm(1, n, 0, H - 1)

        @block.vector
        def _(dve):
            v = nc.vector

            def tap(s, k, n):
                if k == 1:
                    dve.wait_ge(tap0[s], n + 1)
                else:
                    dve.wait_ge(tapped[s], 3 * n + k - 1)
                v.scalar_tensor_tensor(out=y[:, s, k:L], in0=pp[(0, 1, 0)[s]][:, 0:L - k],
                                       scalar=hc[:, s * TAPS + 3 - k:s * TAPS + 4 - k], in1=y[:, s, k:L],
                                       op0=ALU.mult, op1=ALU.add).then_inc(tapped[s], 1)

            def mul_kq(n, p):
                dve.wait_ge(silud[0], n + 1)
                dve.wait_ge(silud[1], n + 1)
                v.tensor_tensor(sqr[:, 2, :], kq[:, p, 0, :], kq[:, p, 1, :], ALU.mult).then_inc(kq_mul, 1)

            def softplus(n):
                dve.wait_ge(gate_ln, 3 * n + 3)
                v.scalar_tensor_tensor(out=gx[:, 1, :], in0=gx[:, 0, :], scalar=0.0, in1=gx[:, 1, :],
                                       op0=ALU.max, op1=ALU.add).then_inc(gate_sp, 1)

            def stats(n, p, b, h):
                dve.wait_ge(stat_mm, n + 1)
                v.tensor_scalar(st[:, p, 0, :], pp[1][:, 0:TB], L2_EPS, None, ALU.add).then_inc(stat_v, 1)
                v.tensor_scalar(st[:, p, 1, :], pp[1][:, TB:2 * TB], L2_EPS, L2_EPS * DK, ALU.add,
                                ALU.mult).then_inc(stat_v, 1)
                v.tensor_copy(st[:, p, 2, :], pp[1][:, 2 * TB:3 * TB]).then_inc(stat_v, 1)
                dve.wait_ge(stat_v, 5 * n + 1)
                v.reciprocal(st[:, p, 3, :], st[:, p, 0, :]).then_inc(stat_v, 1)
                dve.wait_ge(stat_v, 5 * n + 4)
                v.tensor_tensor(st[:, p, 4, :], st[:, p, 3, :], beta[:, h, b * TB:(b + 1) * TB],
                                ALU.mult).then_inc(stat_v, 1)

            def begin(dst, k, p):
                n = dst.shape[-1]
                eye = ident[:, ::P // n].unsqueeze(1).to_broadcast([P, TB, n])
                v.tensor_tensor(dst, eye, st[:, p, k, :].unsqueeze(2).to_broadcast([P, TB, n]),
                                ALU.mult).then_inc(start, 1)

            def masks(j, n, p):
                dve.wait_ge(pairs, 7 * n + j + 1)
                src = pa[:, :].rearrange("p (s i t) -> p s i t", s=2, i=TB)
                mk = dense(mask[:, j, :].unsqueeze(1).to_broadcast([P, TB, P // 2]), j)
                mku = dense(mask[:, j, :].bitcast(U32).unsqueeze(1).to_broadcast([P, TB, P // 2]), j)
                if j == 0:
                    dve.wait_ge(start, 3 * n + 3)
                else:
                    dve.wait_ge(masked, 14 * n + 14 + 2 * j)
                v.tensor_tensor(right(AT[:, j, :, :], j), dense(src[:, 0], j), mk, ALU.mult).then_inc(masked, 1)
                v.copy_predicated(right(AqT[:, p, :, :], j), mku, dense(src[:, 1], j)).then_inc(masked, 1)

            def keep_m(j, n):
                dve.wait_ge(m_turned, 6 * n + j + 1)
                v.tensor_copy(dense(M[:, :, :], j + 1),
                              left(pM[:, :].rearrange("p (i t) -> p i t", i=TB), j + 1)).then_inc(m_kept, 1)

            def growT(j, n, p):
                dve.wait_ge(zt_mm, 7 * n + j + 1)
                k = P if j < LEVELS - 1 else 64
                v.tensor_tensor(right(MT[0:k, p, :, :], j), right(MT[0:k, p, :, :], j),
                                dense(pZT[0:k, 0:256].rearrange("p (i t) -> p i t", i=TB), j),
                                ALU.subtract).then_inc(grownT, 1)

            def state_r(i, n, q):
                dve.wait_ge(r_mm, 3 * n + i)
                v.tensor_tensor(Rb[:, :], Vt[:, q, i, :], pR, ALU.subtract).then_inc(r_made, 1)

            def state_s(i, n, q):
                dve.wait_ge(s_mm, 3 * n + i + 1)
                if i == 0:
                    v.tensor_copy(S[:, 1, :], pSn).then_inc(s_made, 1)
                else:
                    dve.wait_ge(s_made, 3 * n + i)
                    c = tot_at(LEVELS) + i
                    v.scalar_tensor_tensor(out=S[:, (i + 1) % 2, :], in0=S[:, i % 2, :], scalar=dec[:, q, c:c + 1],
                                           in1=pSn, op0=ALU.mult, op1=ALU.add).then_inc(s_made, 1)

            def gated(n, q):
                dve.wait_ge(o_mm, 4 * n + 4)
                v.scalar_tensor_tensor(out=og[:, :], in0=sg[:, q, :], scalar=1.0, in1=pO[:, :],
                                       op0=ALU.add, op1=ALU.mult).then_inc(og_made, 1)

            def norm(n, q):
                dve.wait_ge(so_mm, n + 1)
                v.scalar_tensor_tensor(out=ca[:, 0, :], in0=pO[:, 0:TB], scalar=1.0 / DK, in1=st[:, q, 1, :],
                                       op0=ALU.mult, op1=ALU.add).then_inc(ca_v, 1)

            def collect(half, n, b):
                if half == 0:
                    dve.wait_ge(ca_s, 2 * n + 2)
                dve.wait_ge(wo_mm, 2 * n + half + 1)
                for i in (0, 1):
                    t = 2 * half + i
                    row = (b - 1) % B * TB + t
                    v.scalar_tensor_tensor(out=acc[:, row, :], in0=(pO if half else pS)[:, i * D:(i + 1) * D],
                                           scalar=ca[:, 2, t:t + 1], in1=acc[:, row, :],
                                           op0=ALU.mult, op1=ALU.add).then_inc(acc_made, 1)

            v.memset(ones[:, :], 1.0).then_inc(zeroed, 1)
            v.memset(AT[:, :, :, :], 0.0).then_inc(zeroed, 1)
            for s, c in CREDIT["DVE"]:
                dve.sem_inc(s, c)
            dve.wait_ge(consts, 32)
            dve.wait_ge(w_in, 48)
            dve.wait_ge(zeroed, ZEROED)
            for s in range(3):
                for k in range(1, TAPS):
                    tap(s, k, 0)
                if s == 1:
                    softplus(0)
            mul_kq(0, 0)
            stats(0, 0, 0, 0)
            dve.wait_ge(stat_v, 5)
            begin(AqT[:, 0, :, :], 2, 0)
            begin(MT[:, 0, :, :], 4, 0)
            begin(M[:, :, :], 4, 0)
            masks(0, 0, 0)
            with dve.Fori(0, H) as h:
                for b in range(B):
                    n, n1, b1, p, q = h * B + b, h * B + b + 1, (b + 1) % B, b % 2, (b + 1) % 2
                    masks(1, n, p)
                    state_s(0, n, q)
                    growT(0, n, p)
                    state_r(1, n, q)
                    keep_m(0, n)

                    state_s(1, n, q)
                    masks(2, n, p)
                    state_r(2, n, q)
                    growT(1, n, p)
                    softplus(n1)
                    keep_m(1, n)
                    state_s(2, n, q)
                    if b1 == 0:
                        dve.wait_ge(w_in, 48 * (h + 2))
                    tap(0, 1, n1)

                    state_r(3, n, q)
                    masks(3, n, p)
                    tap(0, 2, n1)
                    growT(2, n, p)
                    tap(0, 3, n1)
                    keep_m(2, n)
                    tap(1, 1, n1)
                    gated(n, q)

                    masks(4, n, p)
                    tap(1, 2, n1)
                    growT(3, n, p)
                    tap(1, 3, n1)
                    keep_m(3, n)
                    norm(n, q)
                    tap(2, 1, n1)

                    masks(5, n, p)
                    tap(2, 2, n1)
                    growT(4, n, p)
                    tap(2, 3, n1)
                    keep_m(4, n)
                    collect(0, n, b)
                    mul_kq(n1, q)

                    masks(6, n, p)
                    growT(5, n, p)
                    collect(1, n, b)
                    keep_m(5, n)
                    stats(n1, q, b1, h + 1 if b == B - 1 else h)

                    dve.wait_ge(stat_v, 5 * n + 10)
                    begin(AqT[:, q, :, :], 2, q)
                    dve.wait_ge(y_mm, 7 * n + 7)
                    begin(M[:, :, :], 4, q)
                    growT(6, n, p)
                    begin(MT[:, q, :, :], 4, q)
                    masks(0, n1, q)
            n = H * B
            for i in range(TB):
                if i:
                    state_r(i, n, 1)
                if i < TB - 1:
                    state_s(i, n, 1)
            gated(n, 1)
            norm(n, 1)
            collect(0, n, 0)
            collect(1, n, 0)
            nout.vector(dve, lambda i: dve.wait_ge(acc_made, 4 * B * H + 8))

        @block.scalar
        def _(act):
            s_ = nc.scalar

            def first_tap(s, n):
                act.wait_ge(proj[s], n + 1)
                s_.activation(y[:, s, :], pp[(0, 1, 0)[s]][:, :], ACT.Identity,
                              scale=hc[:, s * TAPS + 3:s * TAPS + 4]).then_inc(tap0[s], 1)

            def silu(s, n, p):
                act.wait_ge(tapped[s], 3 * n + 3)
                dst = (kq[:, p, 1, :], kq[:, p, 0, :], vc[:, :])[s]
                s_.activation(dst, y[:, s, :], ACT.Silu).then_inc(silud[s], 1)

            def begin_kQ(n, p):
                act.wait_ge(silud[1], n + 1)
                s_.activation(kQ[:, p, :], kq[:, p, 0, :], ACT.Identity).then_inc(kQ_begun, 1)

            def squares(n, p):
                s_.activation(sqr[:, 0:2, :], kq[:, p, :, :], ACT.Square).then_inc(squared, 1)

            def tanh_gate(n, p):
                act.wait_ge(proj[4], n + 1)
                s_.activation(sg[:, p, :], pp[1][:, :], ACT.Tanh, scale=0.5).then_inc(tanhd, 1)

            def gate_input(n):
                act.wait_ge(proj[3], n + 1)
                s_.activation(gx[:, 0, :], pp[1][:, :], ACT.Identity,
                              bias=hc[:, 3 * TAPS:3 * TAPS + 1]).then_inc(gate_in, 1)

            def gate_log(k, n):
                if k == 0:
                    act.wait_ge(gate_in, n + 1)
                    s_.activation(gx[:, 1, :], gx[:, 0, :], ACT.Abs).then_inc(gate_ln, 1)
                elif k == 1:
                    act.wait_ge(gate_ln, 3 * n + 1)
                    s_.activation(gx[:, 1, :], gx[:, 1, :], ACT.Exp, scale=-1.0).then_inc(gate_ln, 1)
                else:
                    act.wait_ge(gate_ln, 3 * n + 2)
                    s_.activation(gx[:, 1, :], gx[:, 1, :], ACT.Ln, bias=1.0).then_inc(gate_ln, 1)

            def decays(p, h):
                s_.activation(dec[:, p, 0:L], gx[:, 1, :], ACT.Exp, scale=negA[:, bass.ds(h, 1)]).then_inc(gate_out, 1)

            def roots(n, p):
                act.wait_ge(stat_v, 5 * n + 1)
                s_.activation(rt[:, 0, :], st[:, p, 0, :], ACT.Ln).then_inc(rooted, 1)
                act.wait_ge(rooted, 2 * n + 1)
                s_.activation(rt[:, 1, :], rt[:, 0, :], ACT.Exp, scale=0.5).then_inc(rooted, 1)

            def keep_v(n, p):
                act.wait_ge(rooted, 2 * n + 2)
                act.wait_ge(v_turned, n + 1)
                for i in range(TB):
                    k = s_.activation(Vt[:, p, i, :], pp[0][:, i * P:(i + 1) * P], ACT.Identity,
                                      scale=rt[:, 1, i:i + 1])
                k.then_inc(v_kept, 1)

            def keep_y(j, n):
                act.wait_ge(y_mm, 7 * n + j + 1)
                k = 0 if j < LEVELS - 1 else 64
                s_.activation(left(Yf[k:P, j, :, :], j), dense(pY[k:P, 0:256].rearrange("p (i t) -> p i t", i=TB), j),
                              ACT.Identity).then_inc(y_kept, 1)

            def keep_kq(n):
                act.wait_ge(kq_turned, n + 1)
                s_.activation(kQt[:, :, :], pp[1][:, :].rearrange("p (i t) -> p i t", i=TB),
                              ACT.Identity).then_inc(kq_kept, 1)

            def keep_u(i, n):
                act.wait_ge(u_mm, 4 * n + i + 1)
                s_.activation(U[:, i % 2, :], pU, ACT.Identity).then_inc(u_kept, 1)

            def square_out(n):
                act.wait_ge(og_made, n + 1)
                s_.activation(osq[:, :], pO[:, :], ACT.Square).then_inc(osq_made, 1)

            def norm(n):
                act.wait_ge(ca_v, n + 1)
                s_.activation(ca[:, 1, :], ca[:, 0, :], ACT.Ln).then_inc(ca_s, 1)
                act.wait_ge(ca_s, 2 * n + 1)
                s_.activation(ca[:, 2, :], ca[:, 1, :], ACT.Exp, scale=-0.5).then_inc(ca_s, 1)

            for s, c in CREDIT["ACT"]:
                act.sem_inc(s, c)
            act.wait_ge(w_in, 48)
            act.wait_ge(zeroed, ZEROED)
            s_.preload_act_table_set("natural_log_exp_and_others")
            gate_input(0)
            first_tap(0, 0)
            for k in range(3):
                gate_log(k, 0)
            first_tap(1, 0)
            first_tap(2, 0)
            act.wait_ge(gate_sp, 1)
            decays(0, 0)
            s_.preload_act_table_set("silu_and_others")
            for s in range(3):
                silu(s, 0, 0)
            begin_kQ(0, 0)
            squares(0, 0)
            tanh_gate(0, 0)
            s_.preload_act_table_set("natural_log_exp_and_others")
            roots(0, 0)
            keep_v(0, 0)
            with act.Fori(0, H) as h:
                for b in range(B):
                    n, n1, b1, p, q = h * B + b, h * B + b + 1, (b + 1) % B, b % 2, (b + 1) % 2
                    h1 = h + 1 if b == B - 1 else h
                    keep_y(0, n)
                    keep_u(0, n)
                    if b1 == 0:
                        act.wait_ge(w_in, 48 * (h + 2))
                    gate_input(n1)
                    gate_log(0, n1)
                    keep_u(1, n)
                    gate_log(1, n1)

                    keep_y(1, n)
                    gate_log(2, n1)
                    keep_u(2, n)
                    first_tap(0, n1)

                    keep_y(2, n)
                    act.wait_ge(gate_sp, n1 + 1)
                    keep_u(3, n)
                    decays(q, h1)
                    first_tap(1, n1)
                    square_out(n)

                    keep_y(3, n)
                    first_tap(2, n1)
                    norm(n)

                    s_.preload_act_table_set("silu_and_others")
                    keep_y(4, n)
                    silu(0, n1, q)
                    silu(1, n1, q)
                    begin_kQ(n1, q)
                    squares(n1, q)

                    keep_y(5, n)
                    tanh_gate(n1, q)
                    silu(2, n1, q)
                    s_.preload_act_table_set("natural_log_exp_and_others")

                    keep_y(6, n)
                    roots(n1, q)
                    keep_v(n1, q)
                    keep_kq(n)
            n = H * B
            for i in range(TB):
                keep_u(i, n)
            square_out(n)
            norm(n)
            nout.scalar(act)

        @block.gpsimd
        def _(pool):
            g = nc.gpsimd

            def products(n, p):
                for j in range(LEVELS):
                    if j:
                        pool.wait_ge(tot, 7 * n + j)
                    src = dec[:, p, tot_at(j):tot_at(j + 1)].rearrange("p (n s) -> p n s", s=2)
                    g.tensor_tensor(dec[:, p, tot_at(j + 1):tot_at(j + 2)], src[:, :, 0], src[:, :, 1],
                                    ALU.mult).then_inc(tot, 1)

            def begin(n, p):
                pool.wait_ge(gate_out, n + 1)
                pool.wait_ge(silud[0], n + 1)
                pool.wait_ge(silud[1], n + 1)
                if not isinstance(n, int):
                    pool.wait_ge(o_mm, 4 * n)
                g.tensor_tensor(kqP[:, p, :, :], kq[:, p, :, :],
                                dec[:, p, 0:L].unsqueeze(1).to_broadcast([P, 2, L]), ALU.mult).then_inc(kqP_begun, 1)

            def scale(j, n, p):
                w_ = 1 << j
                nb = L >> (j + 1)
                pool.wait_ge(pairs, 7 * n + j + 1)
                if j:
                    pool.wait_ge(tot, 7 * n + j)
                    pool.wait_ge(scaled, 14 * n + 2 * j)
                f = dec[:, p, tot_at(j):tot_at(j + 1)].rearrange("p (n s) -> p n s", s=2)
                r = right(kqP[:, p, :, :], j)
                g.tensor_tensor(r, r, f[:, :, 0].unsqueeze(1).unsqueeze(3).to_broadcast([P, 2, nb, w_]),
                                ALU.mult).then_inc(scaled, 1)
                k = left(kQ[:, p, :], j)
                g.tensor_tensor(k, k, f[:, :, 1].unsqueeze(2).to_broadcast([P, nb, w_]),
                                ALU.mult).then_inc(scaled, 1)

            g.memset(Yf[:, :, :, :], 0.0).then_inc(zeroed, 1)
            for t in (Vt[:, 1, :, :], MT[:, 1, :, :], AqT[:, 1, :, :], kqP[:, 1, :, :], kQt[:, :, :], sg[:, 1, :],
                      dec[:, 1, :], wo[:, :]):
                g.memset(t, 0.0).then_inc(zeroed, 1)
            g.memset(st[:, 1, :, :], 1.0).then_inc(zeroed, 1)
            pool.wait_ge(consts, 32)
            g.tensor_scalar(onw[:, :], onw[:, :], 0.5, None, ALU.mult).then_inc(onw_half, 1)
            pool.wait_ge(onw_half, 1)
            begin(0, 0)
            products(0, 0)
            scale(0, 0, 0)
            with pool.Fori(0, H) as h:
                for b in range(B):
                    n, n1, p, q = h * B + b, h * B + b + 1, b % 2, (b + 1) % 2
                    for j in range(1, 6):
                        scale(j, n, p)
                    if b == 0:
                        pool.wait_ge(wo_in, 16 * (h + 1))
                        pool.wait_ge(wo_mm, 2 * n + 2)
                        g.tensor_tensor(wo[:, :], wo_raw[:, :], onw[:, 0:1].to_broadcast([P, D]),
                                        ALU.mult).then_inc(wo_scaled, 1)
                    begin(n1, q)
                    scale(6, n, p)
                    products(n1, q)
                    scale(0, n1, q)


def laid_out_delta(g, chunks):
    def again(w):
        return np.concatenate([w, w[:1]])

    def by_head(name):
        return g(name).reshape(KC, P, H, DK).transpose(2, 1, 0, 3)

    s = np.arange(P)[:, None, None]
    j = np.arange(LEVELS)[None, :, None]
    t = np.arange(P // 2)[None, None, :]
    w = 1 << j
    pair_mask = ((s // (2 * w) == t // w) & (s % (2 * w) < w)).astype(np.float32)
    conv = [g(f"L1_attn_conv_{n}_w").reshape(H, DK, TAPS) for n in "qkv"]
    return {
        "da_wfga": np.stack([chunks(g("L1_attn_Wfa")), chunks(g("L1_attn_Wga"))], axis=2),
        "da_wb": chunks(again(g("L1_attn_Wb").T).T),
        "da_alog": again(g("L1_attn_A_log").reshape(H)),
        "da_wqkv": again(np.stack([by_head(f"L1_attn_W{n}") for n in "qkv"], axis=3)),
        "da_wfgb": again(np.stack([g("L1_attn_Wfb").reshape(P, H, DK), g("L1_attn_Wgb").reshape(P, H, DK)],
                                  axis=2).transpose(1, 0, 2, 3)),
        "da_hc": again(np.concatenate(conv + [g("L1_attn_dt_bias").reshape(H, DK, 1)], axis=2)),
        "da_wo": again(g("L1_attn_Wo").reshape(H, DK, D)),
        "da_onw": g("L1_attn_o_norm_w").reshape(DK, 1),
        "da_mask": pair_mask,
    }


HF = 1024
HC = HF // P


def stage_hadamard_ffn(nc, x, ident, bk, a):
    ctx = ExitStack()
    with ctx:
        m = Pools(nc, ctx)
        xT = m.sb("ff_xT", [P, KC, T])
        xh = m.sb("ff_xh", [P, NT, D])
        w13 = m.sb("ff_w13", [P, KC, 2, HF])
        w2 = m.sb("ff_w2", [P, 2, HC, D])
        sign = m.sb("ff_sign", [P, P])
        sl = m.sb("ff_sl", [P, 2, L])
        hid = m.sb("ff_hid", [P, 2, HC, L])
        nin = NormIn(nc, m, "ff_in", x, ident, xT, xh, bk[0:4])
        nout = NormOut(nc, m, "ff_out", x, xh)
        w2_in = m.sem("ff_w2_in")
        w13_in = m.sem("ff_w13_in")
        sign_mm = m.sem("ff_sign_mm")
        sign_kept = m.sem("ff_sign_kept")
        turned = m.sem("ff_turned")
        mm_g = m.sem("ff_mm_g")
        mm_u = m.sem("ff_mm_u")
        acted = m.sem("ff_acted")
        gated = m.sem("ff_gated")
        out_mm = m.sem("ff_out_mm")
        out_kept = m.sem("ff_out_kept")
        block = ctx.enter_context(nc.Block())

        @block.sync
        def _(sp):
            sp.dma_start(sign[:, :], a["ff_sign"]).then_inc(w2_in, 16)
            sp.dma_start(w2[:, 0, :, :], a["ff_w2"]).then_inc(w2_in, 16)
            sp.dma_start(w13[:, :, :, :], a["ff_w13"]).then_inc(w13_in, 16)

        @block.tensor
        def _(pe):
            mmul = nc.tensor.matmul
            pe.wait_ge(w2_in, 32)
            for c in range(HC // 2):
                for s in range(2):
                    mm = mmul(bk[4 + c][:, s * D:(s + 1) * D], sign[:, :], w2[:, 0, 2 * c + s, :], start=True, stop=True)
                mm.then_inc(sign_mm, 1)
            nin.tensor(pe)
            pe.wait_ge(w13_in, 16)
            pe.wait_ge(sign_kept, HC // 2)

            def piece(n):
                g, c, q = n // HC, n % HC, n % 2
                if n == 0:
                    nin.done(pe)
                for s, done in ((0, mm_g), (1, mm_u)):
                    if n >= 2:
                        pe.wait_ge(gated, n - 1)
                    for kc in range(KC):
                        mm = mmul(bk[2 * q + s][:, :], w13[:, kc, s, c * P:(c + 1) * P], xT[:, kc, g * L:(g + 1) * L],
                                  start=kc == 0, stop=kc == KC - 1)
                    mm.then_inc(done, 1)

            def outputs(g):
                pe.wait_ge(gated, HC * (g + 1))
                if g == 0:
                    pe.wait_ge(turned, 6)
                for j in range(L // P):
                    i = g * (L // P) + j
                    if i >= 2:
                        pe.wait_ge(out_kept, i - 1)
                    for c in range(HC):
                        mm = mmul(bk[4 + i % 2][:, 0:D], hid[:, g % 2, c, j * P:(j + 1) * P], w2[:, 1, c, :],
                                  start=c == 0, stop=c == HC - 1)
                    mm.then_inc(out_mm, 1)

            for g in range(B):
                for c in range(HC):
                    piece(g * HC + c)
                    if c == 1 and g >= 1:
                        outputs(g - 1)
            outputs(B - 1)

        @block.scalar
        def _(act):
            s_ = nc.scalar
            for c in range(HC // 2):
                act.wait_ge(sign_mm, c + 1)
                s_.activation(w2[:, 0, 2 * c:2 * c + 2, :], bk[4 + c][:, :].rearrange("p (s d) -> p s d", s=2),
                              ACT.Identity, scale=1.0 / 32.0).then_inc(sign_kept, 1)
            nin.scalar(act)

            def keep(i):
                act.wait_ge(out_mm, i + 1)
                s_.activation(xh[:, i, :], bk[4 + i % 2][:, 0:D], ACT.Identity).then_inc(out_kept, 1)

            for n in range(B * HC):
                act.wait_ge(mm_g, n + 1)
                if n >= 2:
                    act.wait_ge(gated, n - 1)
                s_.activation(sl[:, n % 2, :], bk[2 * (n % 2)][:, :], ACT.Silu).then_inc(acted, 1)
                if n % HC == 1 and n > HC:
                    for j in range(4):
                        keep(4 * (n // HC - 1) + j)
            for j in range(4):
                keep(4 * (B - 1) + j)
            nout.scalar(act)

        @block.vector
        def _(dve):
            v = nc.vector
            dve.wait_ge(sign_kept, HC // 2)
            for r in range(3):
                src = w2[:, r % 2, :, :].rearrange("p (n s w) d -> p n s (w d)", s=2, w=1 << r)
                dst = w2[:, (r + 1) % 2, :, :].rearrange("p (n s w) d -> p n s (w d)", s=2, w=1 << r)
                if r:
                    dve.wait_ge(turned, 2 * r)
                v.tensor_tensor(dst[:, :, 0], src[:, :, 0], src[:, :, 1], ALU.add).then_inc(turned, 1)
                v.tensor_tensor(dst[:, :, 1], src[:, :, 0], src[:, :, 1], ALU.subtract).then_inc(turned, 1)
            nin.vector(dve)
            for n in range(B * HC):
                g, c, q = n // HC, n % HC, n % 2
                dve.wait_ge(acted, n + 1)
                dve.wait_ge(mm_u, n + 1)
                if c == 0 and g >= 2:
                    dve.wait_ge(out_mm, 4 * (g - 1))
                v.tensor_tensor(hid[:, g % 2, c, :], sl[:, q, :], bk[2 * q + 1][:, :], ALU.mult).then_inc(gated, 1)
            nout.vector(dve, lambda i: dve.wait_ge(out_kept, i + 1))


def laid_out_ffn(g, chunks):
    s = np.ones((1, 1), np.float32)
    while s.shape[0] < P:
        s = np.block([[s, s], [s, -s]])
    return {
        "ff_w13": np.stack([chunks(g("L1_ffn_W1").T), chunks(g("L1_ffn_W3").T)], axis=2),
        "ff_w2": chunks(g("L1_ffn_W2").T),
        "ff_sign": s.astype(np.float32),
    }


def program(nc, a, out, stages=4):
    ctx = ExitStack()
    with ctx:
        m = Pools(nc, ctx)
        x = m.sb("x", [P, NT, D])
        ident = m.sb("ident", [P, P])
        banks = [m.ps(f"bank{i}") for i in range(8)]
        x_in = m.sem("x_in")
        with nc.Block() as block:
            @block.sync
            def _(sp):
                sp.dma_start(x[:, :, :], a["x"].rearrange("(i p) d -> p i d", p=P)).then_inc(x_in, 16)
                sp.dma_start(ident[:, :], a["ident"]).then_inc(x_in, 16)
                sp.wait_ge(x_in, 32)
        if stages >= 1:
            stage_recurrence(nc, x, ident, banks, a["ra_w_in"], a["ra_w_out"], a["ra_vecs"], a["ra_out_b"])
        if stages >= 2:
            stage_experts(nc, x, ident, banks, a)
        if stages >= 3:
            stage_delta(nc, x, ident, banks, a)
        if stages >= 4:
            stage_hadamard_ffn(nc, x, ident, banks, a)
        x_out = m.sem("x_out")
        with nc.Block() as block:
            @block.sync
            def _(sp):
                sp.dma_start(out.rearrange("(i p) d -> p i d", p=P), x[:, :, :]).then_inc(x_out, 16)
                sp.wait_ge(x_out, 16)


def laid_out(i):
    def chunks(w):
        return w.reshape(-1, P, w.shape[-1]).transpose(1, 0, 2)

    g = lambda n: np.asarray(i[n])
    w_in = np.stack([chunks(g(f"L0_attn_{n}_w").T) for n in ("A", "D", "B", "Ca", "Cb")], axis=2)
    r = {
        "x": g("L0_attn_x").reshape(T, D),
        "ident": np.eye(P, dtype=np.float32),
        "ra_w_in": w_in,
        "ra_w_out": chunks(g("L0_attn_out_w").T),
        "ra_vecs": np.stack([g("L0_attn_rms_w").reshape(KC, P).T, g("L0_attn_A_b").reshape(KC, P).T], axis=1),
        "ra_out_b": g("L0_attn_out_b"),
    }
    for more in (laid_out_experts, laid_out_delta, laid_out_ffn):
        r.update(more(g, chunks))
    return {k: np.ascontiguousarray(v) for k, v in r.items()}


STAGES = 4


def kernel(**inputs):
    import concourse.bacc as bacc
    from concourse.bass_utils import run_bass_kernel_spmd

    nc = bacc.Bacc("TRN2", target_bir_lowering=False, num_devices=1)
    arrays = laid_out(inputs)
    args = {k: nc.dram_tensor(f"in_{k}", v.shape, mybir.dt.from_np(v.dtype), kind="ExternalInput").ap()
            for k, v in arrays.items()}
    out = nc.dram_tensor("out_x", (T, D), F32, kind="ExternalOutput").ap()
    program(nc, args, out, STAGES)
    r = run_bass_kernel_spmd(nc, [{f"in_{k}": v for k, v in arrays.items()}], core_ids=[0])
    return r.results[0]["out_x"].reshape(B, L, D)
```

```python
from contextlib import ExitStack

import numpy as np

import concourse.bass as bass
from concourse import mybir

F32 = mybir.dt.float32
I32 = mybir.dt.int32
U32 = mybir.dt.uint32
BF16 = mybir.dt.bfloat16
ALU = mybir.AluOpType
ACT = mybir.ActivationFunctionType
AX = mybir.AxisListType

P = 128
B, L, D = 4, 512, 256
T = B * L
NT = T // P
KC = D // P
LN_EPS = 1e-5


class Pools:

    def __init__(self, nc, ctx):
        self.nc, self.ctx, self.sems = nc, ctx, []
        ctx.callback(self.end)

    def sb(self, name, shape, dt=F32):
        return self.ctx.enter_context(self.nc.sbuf_tensor(name, shape, dt))

    def ps(self, name, shape=(P, 512), dt=F32):
        return self.ctx.enter_context(self.nc.psum_tensor(name, list(shape), dt))

    def sem(self, name):
        self.sems.append(self.nc.alloc_semaphore(name=name))
        return self.sems[-1]

    def end(self):
        self.nc.clear_and_free_semaphores(self.sems)
        self.nc.all_engine_barrier()


class NormIn:

    def __init__(self, nc, m, tag, x, ident, xT, xh, banks, rms=False, col_scale=None):
        self.nc, self.x, self.ident, self.xT, self.xh, self.banks = nc, x, ident, xT, xh, banks
        self.rms, self.col_scale = rms, col_scale
        self.st = m.sb(f"{tag}_st", [P, NT, 6])
        self.mv = m.sb(f"{tag}_mv", [P, NT, 2])
        self.ve = m.sb(f"{tag}_ve", [P, NT])
        self.sd = m.sb(f"{tag}_sd", [P, NT])
        self.rstd = m.sb(f"{tag}_rstd", [P, NT])
        self.off = m.sb(f"{tag}_off", [P, NT])
        if rms:
            self.ms = m.sb(f"{tag}_ms", [P, NT])
            self.rn = m.sb(f"{tag}_rn", [P, NT])
            self.xn = m.sb(f"{tag}_xn", [P, NT, D])
        self.stats = m.sem(f"{tag}_stats")
        self.rooted = m.sem(f"{tag}_rooted")
        self.normed = m.sem(f"{tag}_normed")
        self.normed_act = m.sem(f"{tag}_normed_act")
        self.turned = m.sem(f"{tag}_turned")
        self.kept = [m.sem(f"{tag}_kept0"), m.sem(f"{tag}_kept1")]

    def vector(self, dve, more=None):
        v = self.nc.vector
        for i in range(NT):
            v.bn_stats(out=self.st[:, i, :], in_=self.x[:, i, :]).then_inc(self.stats, 1)
        for i in range(NT):
            dve.wait_ge(self.stats, i + 1)
            v.bn_aggr(out=self.mv[:, i, :], in_=self.st[:, i, :]).then_inc(self.stats, 1)
        dve.wait_ge(self.stats, 2 * NT)
        v.tensor_scalar(self.ve[:, :], self.mv[:, :, 1], LN_EPS, None, ALU.add).then_inc(self.stats, 1)
        dve.wait_ge(self.rooted, 1)
        v.reciprocal(self.rstd[:, :], self.sd[:, :]).then_inc(self.stats, 1)
        dve.wait_ge(self.stats, 2 * NT + 2)
        if not self.rms:
            v.scalar_tensor_tensor(out=self.off[:, :], in0=self.mv[:, :, 0], scalar=-1.0, in1=self.rstd[:, :],
                                   op0=ALU.mult, op1=ALU.mult).then_inc(self.stats, 1)
        if self.rms:
            v.tensor_tensor(self.ms[:, :], self.mv[:, :, 1], self.rstd[:, :], ALU.mult).then_inc(self.stats, 1)
            dve.wait_ge(self.stats, 2 * NT + 3)
            v.tensor_tensor(self.ms[:, :], self.ms[:, :], self.rstd[:, :], ALU.mult).then_inc(self.stats, 1)
            dve.wait_ge(self.stats, 2 * NT + 4)
            v.tensor_scalar(self.ms[:, :], self.ms[:, :], LN_EPS, None, ALU.add).then_inc(self.stats, 1)
            dve.wait_ge(self.rooted, 2)
            v.reciprocal(self.rn[:, :], self.sd[:, :]).then_inc(self.stats, 1)
            dve.wait_ge(self.stats, 2 * NT + 6)
        for i in range(NT):
            if self.rms or i % 4 < 2:
                v.tensor_scalar(self.xh[:, i, :], self.x[:, i, :], self.mv[:, i, 0:1], self.rstd[:, i:i + 1],
                                ALU.subtract, ALU.mult).then_inc(self.normed, 1)
            if self.rms:
                dve.wait_ge(self.normed, 2 * i + 1)
                v.tensor_scalar(self.xn[:, i, :], self.xh[:, i, :], self.rn[:, i:i + 1], None,
                                ALU.mult).then_inc(self.normed, 1)
            if i % 4 == 3:
                g = i // 4
                if g >= 1:
                    self._keep(dve, v, g - 1, 1)
        self._keep(dve, v, NT // 4 - 1, 1)

    def _keep(self, eng, e, g, kc):
        eng.wait_ge(self.turned, g + 1)
        src, dst = self.banks[2 * (g % 2) + kc][:, :], self.xT[:, kc, g * 512:(g + 1) * 512]
        if self.col_scale is not None:
            s = self.col_scale[:, kc:kc + 1]
            if kc == 0:
                ins = e.activation(dst, src, ACT.Identity, scale=s)
            else:
                ins = e.tensor_scalar(dst, src, s, None, ALU.mult)
        else:
            ins = e.activation(dst, src, ACT.Identity) if kc == 0 else e.tensor_copy(dst, src)
        ins.then_inc(self.kept[kc], 1)

    def scalar(self, act):
        s = self.nc.scalar
        act.wait_ge(self.stats, 2 * NT + 1)
        s.activation(self.sd[:, :], self.ve[:, :], ACT.Sqrt).then_inc(self.rooted, 1)
        if self.rms:
            act.wait_ge(self.stats, 2 * NT + 5)
            s.activation(self.sd[:, :], self.ms[:, :], ACT.Sqrt).then_inc(self.rooted, 1)
        if not self.rms:
            act.wait_ge(self.stats, 2 * NT + 3)
        for g in range(NT // 4 + 1):
            if not self.rms and g < NT // 4:
                for i in (4 * g + 2, 4 * g + 3):
                    s.activation(self.xh[:, i, :], self.x[:, i, :], ACT.Identity, bias=self.off[:, i:i + 1],
                                 scale=self.rstd[:, i:i + 1]).then_inc(self.normed_act, 1)
            if g:
                self._keep(act, s, g - 1, 0)

    def all_normed(self, eng, groups=NT // 4):
        eng.wait_ge(self.normed, 2 * groups)
        eng.wait_ge(self.normed_act, 2 * groups)

    def tensor(self, pe):
        src = self.xn if self.rms else self.xh
        for g in range(NT // 4):
            if self.rms:
                pe.wait_ge(self.normed, 8 * (g + 1))
            else:
                self.all_normed(pe, g + 1)
            if g >= 2:
                pe.wait_ge(self.kept[0], g - 1)
                pe.wait_ge(self.kept[1], g - 1)
            for kc in range(KC):
                for j in range(4):
                    mm = self.nc.tensor.transpose(self.banks[2 * (g % 2) + kc][:, j * P:(j + 1) * P],
                                                  src[:, 4 * g + j, kc * P:(kc + 1) * P], self.ident[:, :])
            mm.then_inc(self.turned, 1)

    def done(self, eng, groups=NT // 4):
        eng.wait_ge(self.kept[0], groups)
        eng.wait_ge(self.kept[1], groups)


class NormOut:

    def __init__(self, nc, m, tag, x, out):
        self.nc, self.x, self.out = nc, x, out
        self.st = m.sb(f"{tag}_st", [P, NT, 6])
        self.mv = m.sb(f"{tag}_mv", [P, NT, 2])
        self.ve = m.sb(f"{tag}_ve", [P, NT])
        self.sd = m.sb(f"{tag}_sd", [P, NT])
        self.rstd = m.sb(f"{tag}_rstd", [P, NT])
        self.off = m.sb(f"{tag}_off", [P, NT])
        self.stats = m.sem(f"{tag}_stats")
        self.rooted = m.sem(f"{tag}_rooted")
        self.scaled = m.sem(f"{tag}_scaled")

    def vector(self, dve, ready=None):
        v = self.nc.vector
        for i in range(NT):
            if ready is not None:
                ready(i)
            v.bn_stats(out=self.st[:, i, :], in_=self.out[:, i, :]).then_inc(self.stats, 1)
        for i in range(NT):
            dve.wait_ge(self.stats, i + 1)
            v.bn_aggr(out=self.mv[:, i, :], in_=self.st[:, i, :]).then_inc(self.stats, 1)
        dve.wait_ge(self.stats, 2 * NT)
        v.tensor_scalar(self.ve[:, :], self.mv[:, :, 1], LN_EPS, None, ALU.add).then_inc(self.stats, 1)
        dve.wait_ge(self.rooted, 1)
        v.reciprocal(self.rstd[:, :], self.sd[:, :]).then_inc(self.stats, 1)
        dve.wait_ge(self.stats, 2 * NT + 2)
        v.scalar_tensor_tensor(out=self.off[:, :], in0=self.mv[:, :, 0], scalar=-1.0, in1=self.rstd[:, :],
                               op0=ALU.mult, op1=ALU.mult).then_inc(self.stats, 1)
        for i in range(NT):
            dve.wait_ge(self.scaled, i + 1)
            v.tensor_tensor(self.x[:, i, :], self.x[:, i, :], self.out[:, i, :], ALU.add)

    def scalar(self, act):
        s = self.nc.scalar
        act.wait_ge(self.stats, 2 * NT + 1)
        s.activation(self.sd[:, :], self.ve[:, :], ACT.Sqrt).then_inc(self.rooted, 1)
        act.wait_ge(self.stats, 2 * NT + 3)
        for i in range(NT):
            s.activation(self.out[:, i, :], self.out[:, i, :], ACT.Identity, bias=self.off[:, i:i + 1],
                         scale=self.rstd[:, i:i + 1]).then_inc(self.scaled, 1)


def stage_recurrence(nc, x, ident, banks, w_in, w_out, vecs, out_b):
    PROJ = 5
    ctx = ExitStack()
    with ctx:
        m = Pools(nc, ctx)
        wi = m.sb("ra_wi", [P, KC, PROJ, D])
        wo = m.sb("ra_wo", [P, KC, D])
        vec = m.sb("ra_vec", [P, 2, KC])
        bias = m.sb("ra_bias", [P, D])
        xT = m.sb("ra_xT", [P, KC, T])
        xh = m.sb("ra_xh", [P, NT, D])
        sig = m.sb("ra_sig", [P, 2, 3, L])
        u = m.sb("ra_u", [P, 2, L])
        h = m.sb("ra_h", [P, 2, L])
        sc = m.sb("ra_sc", [P, 2, L])
        yT = m.sb("ra_yT", [P, 2, KC, L])
        pj, po = banks[0:5], banks[5:7]
        nin = NormIn(nc, m, "ra_in", x, ident, xT, xh, banks[0:4], rms=True, col_scale=vec[:, 0, :])
        nout = NormOut(nc, m, "ra_out", x, xh)
        loaded = m.sem("ra_loaded")
        projected = m.sem("ra_projected")
        squashed = m.sem("ra_squashed")
        gated = m.sem("ra_gated")
        mixed = m.sem("ra_mixed")
        summed = m.sem("ra_summed")
        R = B * KC
        block = ctx.enter_context(nc.Block())

        @block.sync
        def _(sp):
            sp.dma_start(vec[:, :, :], vecs).then_inc(loaded, 16)
            sp.dma_start(wi[:, :, :, :], w_in).then_inc(loaded, 16)
            sp.dma_start(wo[:, :, :], w_out).then_inc(loaded, 16)
            sp.dma_start(bias[:, :], out_b.partition_broadcast(P)).then_inc(loaded, 16)

        @block.tensor
        def _(pe):
            nin.tensor(pe)
            pe.wait_ge(loaded, 64)

            def outputs(b):
                pe.wait_ge(gated, 5 * (KC * b + KC))
                for j in range(L // P):
                    i = b * (L // P) + j
                    if i >= 2:
                        pe.wait_ge(summed, 2 * (i - 2) + 1)
                    for kc in range(KC):
                        mm = nc.tensor.matmul(po[i % 2][:, 0:D], yT[:, b % 2, kc, j * P:(j + 1) * P], wo[:, kc, :],
                                              start=kc == 0, stop=kc == KC - 1)
                    mm.then_inc(mixed, 1)

            for r in range(R):
                b, c = r // KC, r % KC
                nin.done(pe, b + 1) if r else nin.done(pe)
                for p in range(PROJ):
                    if r:
                        if p in (0, 1):
                            pe.wait_ge(squashed, 3 * (r - 1) + p + 1)
                        elif p == 2:
                            pe.wait_ge(gated, 5 * (r - 1) + 1)
                        elif p == 3:
                            pe.wait_ge(gated, 5 * (r - 1) + 3)
                            pe.wait_ge(squashed, 3 * r)
                        else:
                            pe.wait_ge(gated, 5 * (r - 1) + 4)
                    for kc in range(KC):
                        mm = nc.tensor.matmul(pj[p][:, :], wi[:, kc, p, c * P:(c + 1) * P],
                                              xT[:, kc, b * L:(b + 1) * L], start=kc == 0, stop=kc == KC - 1)
                    mm.then_inc(projected, 1)
                if r % KC == KC - 1 and b >= 1:
                    outputs(b - 1)
            outputs(B - 1)

        @block.scalar
        def _(act):
            act.wait_ge(loaded, 64)
            nin.scalar(act)
            for r in range(R):
                c = r % KC
                if r >= 2:
                    act.wait_ge(gated, 5 * (r - 1))
                act.wait_ge(projected, PROJ * r + 1)
                nc.scalar.activation(sig[:, r % 2, 0, :], pj[0][:, :], ACT.Sigmoid,
                                     bias=vec[:, 1, c:c + 1]).then_inc(squashed, 1)
                act.wait_ge(projected, PROJ * r + 2)
                nc.scalar.activation(sig[:, r % 2, 1, :], pj[1][:, :], ACT.Sigmoid).then_inc(squashed, 1)
                act.wait_ge(projected, PROJ * r + 4)
                nc.scalar.activation(sig[:, r % 2, 2, :], pj[3][:, :], ACT.Sigmoid).then_inc(squashed, 1)
            nout.scalar(act)

        @block.vector
        def _(dve):
            dve.wait_ge(loaded, 64)
            nin.vector(dve)
            v = nc.vector

            def outputs(b):
                for j in range(L // P):
                    i = b * (L // P) + j
                    dve.wait_ge(mixed, i + 1)
                    v.tensor_tensor(xh[:, i, :], po[i % 2][:, 0:D], xh[:, i, :], ALU.add).then_inc(summed, 1)
                    dve.wait_ge(summed, 2 * i + 1)
                    v.tensor_tensor(xh[:, i, :], xh[:, i, :], bias[:, :], ALU.add).then_inc(summed, 1)

            for r in range(R):
                b, c, q = r // KC, r % KC, r % 2
                dve.wait_ge(squashed, 3 * r + 2)
                dve.wait_ge(projected, PROJ * r + 3)
                v.tensor_tensor(u[:, q, :], pj[2][:, :], sig[:, q, 1, :], ALU.mult).then_inc(gated, 1)
                dve.wait_ge(gated, 5 * r + 1)
                v.tensor_tensor_scan(h[:, q, :], sig[:, q, 0, :], u[:, q, :], 0.0, ALU.mult, ALU.add).then_inc(gated, 1)
                dve.wait_ge(squashed, 3 * r + 3)
                v.tensor_tensor(sc[:, q, :], pj[3][:, :], sig[:, q, 2, :], ALU.mult).then_inc(gated, 1)
                dve.wait_ge(projected, PROJ * r + 5)
                dve.wait_ge(gated, 5 * r + 3)
                v.tensor_tensor(sc[:, q, :], pj[4][:, :], sc[:, q, :], ALU.mult).then_inc(gated, 1)
                dve.wait_ge(gated, 5 * r + 4)
                if c == 0 and b >= 2:
                    dve.wait_ge(mixed, (b - 1) * (L // P))
                v.tensor_tensor(yT[:, b % 2, c, :], sc[:, q, :], h[:, q, :], ALU.mult).then_inc(gated, 1)
                if c == KC - 1 and b >= 1:
                    outputs(b - 1)
            outputs(B - 1)
            nout.vector(dve, lambda i: dve.wait_ge(summed, 2 * i + 2))


E_, K_, I_ = 64, 6, 176
CAP = 32
IS_ = 2 * I_
EG = P // CAP
G_ = E_ // EG
IH = I_ // 2
SH = (0, 128, 256, IS_)
BIG = 1.0e30
ROW = D + E_


def stage_experts(nc, x, ident, bk, a):
    ctx = ExitStack()
    with ctx:
        m = Pools(nc, ctx)
        xT = m.sb("ex_xT", [P, KC, T])
        xh = m.sb("ex_xh", [P, NT, D])
        gw = m.sb("ex_gw", [P, KC, E_])
        xg = m.sb("ex_xg", [P, G_, ROW])
        early = xg[:, :, :].rearrange("p g r -> p (g r)")
        LR = NT * (E_ + 2)
        lg = early[:, 0:LR].rearrange("p (i e) -> p i e", e=E_ + 2)
        rep = early[:, LR:2 * LR].rearrange("p (i e) -> p i e", e=E_ + 2)
        mx = m.sb("ex_mx", [P, NT, 8])
        nmx = m.sb("ex_nmx", [P, NT])
        esum = m.sb("ex_esum", [P, NT])
        rs = m.sb("ex_rs", [P, NT])
        score = m.sb("ex_score", [P, NT, E_])
        key = early[0:E_, 2 * LR:2 * LR + T]
        k32 = m.sb("ex_k32", [E_, CAP])
        idxf = m.sb("ex_idxf", [P, G_])
        idx = m.sb("ex_idx", [P, G_], U32)
        iota = m.sb("ex_iota", [P, T])
        pick = m.sb("ex_pick", [E_, EG, G_])
        yf = m.sb("ex_yf", [P, 2, 2, D])
        ssl = yf[:, :, :, :].rearrange("p q s d -> p q (s d)")
        yp = m.sb("ex_yp", [P, 3, G_, D], BF16)
        own = m.sb("ex_own", [P, G_, E_])
        zrow = m.sb("ex_zrow", [1, ROW])
        zeros = m.sb("ex_zeros", [P, 2 * D], BF16)
        ws = m.sb("ex_ws", [P, G_])
        sw = m.sb("ex_sw", [P, KC, 2, IS_])
        swd = m.sb("ex_swd", [P, 3, D])
        hsh = m.sb("ex_hsh", [P, 3, L])
        NW = 3
        wgu = m.sb("ex_wgu", [P, NW, EG, KC, 2 * I_])
        wd = m.sb("ex_wd", [IH, NW, EG, 2, D])
        xgT = m.sb("ex_xgT", [P, 2, KC, P])
        sl = m.sb("ex_sl", [P, 2, I_])
        hh = m.sb("ex_hh", [P, 2, I_])
        hT = m.sb("ex_hT", [IH, 2, 2, P])
        oneh = m.sb("ex_oneh", [P, 2, G_, P], BF16)
        tab = nc.dram_tensor("ex_tab", (T + 1, ROW), F32, kind="Internal").ap()
        nin = NormIn(nc, m, "ex_in", x, ident, xT, xh, bk[0:4])
        nout = NormOut(nc, m, "ex_out", x, xh)
        HT = NT // 2
        b_gu, b_h, b_x, b_d, b_sum = bk[0], bk[1], bk[2], bk[3], bk[4:8]

        loaded = m.sem("ex_loaded")
        w_in = [m.sem(f"ex_w_in{i}") for i in range(NW)]
        lit = m.sem("ex_lit")
        logits = m.sem("ex_logits")
        lg_kept = m.sem("ex_lg_kept")
        maxed = m.sem("ex_maxed")
        negm = m.sem("ex_negm")
        exped = m.sem("ex_exped")
        scored = m.sem("ex_scored")
        mask_t = m.sem("ex_mask_t")
        keyed = m.sem("ex_keyed")
        ranked = m.sem("ex_ranked")
        placed = m.sem("ex_placed")
        indexed = m.sem("ex_indexed")
        stored_x = m.sem("ex_stored_x")
        stored = m.sem("ex_stored")
        gathered = [m.sem(f"ex_gathered{i}") for i in range(G_)]
        weighed = m.sem("ex_weighed")
        sh_mm = m.sem("ex_sh_mm")
        sh_act = m.sem("ex_sh_act")
        sh_mul = m.sem("ex_sh_mul")
        sh_down = m.sem("ex_sh_down")
        sh_kept = m.sem("ex_sh_kept")
        xg_t = m.sem("ex_xg_t")
        xg_kept = m.sem("ex_xg_kept")
        gu_mm = m.sem("ex_gu_mm")
        gu_act = m.sem("ex_gu_act")
        gu_mul = m.sem("ex_gu_mul")
        h_t = m.sem("ex_h_t")
        h_kept = m.sem("ex_h_kept")
        d_mm = m.sem("ex_d_mm")
        y_made = m.sem("ex_y_made")
        y_part = [m.sem(f"ex_y_part{i}") for i in range(3)]
        y_rest = m.sem("ex_y_rest")
        hot = m.sem("ex_hot")
        sums = m.sem("ex_sums")
        comb = m.sem("ex_comb")
        out_made = m.sem("ex_out_made")

        pieces = [(c, g) for g in range(B) for c in range(3)]
        block = ctx.enter_context(nc.Block())

        @block.sync
        def _(sp):
            for dst, src in ((gw[:, :, :], a["ex_gw"]), (sw[:, :, :, :], a["ex_sw"]),
                             (pick[:, :, :], a["ex_pick"]), (own[:, :, :], a["ex_own"]),
                             (iota[:, :], a["ex_iota"].partition_broadcast(P))):
                sp.dma_start(dst, src).then_inc(loaded, 16)
            sp.dma_start(swd[:, 0:2, :], a["ex_swd"][0:256].rearrange("(c p) d -> p c d", p=P)).then_inc(loaded, 16)
            sp.dma_start(swd[0:96, 2, :], a["ex_swd"][256:IS_]).then_inc(loaded, 16)

            def weights(g):
                q = g % NW
                sp.dma_start(wgu[:, q, :, :, :], a["ex_wgu"][g]).then_inc(w_in[q], 16)
                sp.dma_start(wd[:, q, :, :, :], a["ex_wd"][g]).then_inc(w_in[q], 16)

            weights(0)
            nin.all_normed(sp)
            sp.dma_start(tab[0:T, 0:D].rearrange("(i p) d -> p i d", p=P), xh[:, :, :]).then_inc(stored_x, 16)
            sp.wait_ge(lit, 1)
            sp.dma_start(tab[T:T + 1, :], zrow[:, :]).then_inc(stored, 16)
            for g in range(1, NW):
                weights(g)
            sp.wait_ge(scored, 2)
            sp.dma_start(tab[0:T, D:ROW].rearrange("(i p) e -> p i e", p=P), score[:, :, :]).then_inc(stored, 16)
            for g in range(NW, G_):
                sp.wait_ge(d_mm, g - NW + 1)
                weights(g)
            sp.wait_ge(stored_x, 16)
            sp.wait_ge(stored, 32)

        @block.tensor
        def _(pe):
            mmul, turn = nc.tensor.matmul, nc.tensor.transpose
            nin.tensor(pe)
            pe.wait_ge(loaded, 112)
            for i in range(NT):
                if i % 4 == 0:
                    nin.done(pe, i // 4 + 1)
                for kc in range(KC):
                    mm = mmul(bk[4 + i // 8][:, (i % 8) * E_:(i % 8 + 1) * E_], xT[:, kc, i * P:(i + 1) * P],
                              gw[:, kc, :], start=kc == 0, stop=kc == KC - 1)
                if i % 8 == 7:
                    mm.then_inc(logits, 1)

            def shared(n):
                c, g = pieces[n]
                c0, c1 = SH[c], SH[c + 1]
                for s in range(2):
                    if n:
                        pe.wait_ge(sh_mul, n) if s else pe.wait_ge(sh_act, n)
                    for kc in range(KC):
                        mm = mmul(bk[6 + s][0:c1 - c0, :], sw[:, kc, s, c0:c1], xT[:, kc, g * L:(g + 1) * L],
                                  start=kc == 0, stop=kc == KC - 1)
                    mm.then_inc(sh_mm, 1)

            def shared_down(g):
                pe.wait_ge(sh_mul, 3 * g + 3)
                for j in range(4):
                    i = 4 * g + j
                    if i >= 2:
                        pe.wait_ge(sh_kept, i - 1)
                    else:
                        pe.wait_ge(lg_kept, 3)
                    for c in range(3):
                        k = SH[c + 1] - SH[c]
                        mm = mmul(bk[4 + i % 2][:, 0:D], hsh[0:k, c, j * P:(j + 1) * P], swd[0:k, c, :],
                                  start=c == 0, stop=c == 2)
                    mm.then_inc(sh_down, 1)

            for n in range(3):
                shared(n)
            for g in range(B):
                for j in range(4):
                    i = 4 * g + j
                    pe.wait_ge(maxed, 3 * i + 3)
                    mm = turn(bk[g][0:E_, j * P:(j + 1) * P], rep[:, i, 0:E_], ident[:, :])
                mm.then_inc(mask_t, 1)

            def place():
                pe.wait_ge(ranked, 7)
                pe.wait_ge(keyed, 4)
                for e in range(EG):
                    mm = mmul(bk[0][e * CAP:(e + 1) * CAP, 0:G_], k32[:, :], pick[:, e, :], start=True, stop=True)
                mm.then_inc(placed, 1)

            for g in range(1, B):
                shared(3 * g)
                shared_down(g - 1)
                shared(3 * g + 1)
                shared(3 * g + 2)
                if g == 2:
                    place()
            shared_down(B - 1)

            def turn_x(g):
                pe.wait_ge(gathered[g], 16)
                if g >= 1:
                    pe.wait_ge(xg_kept, g)
                for kc in range(KC):
                    mm = turn(b_x[:, kc * P:(kc + 1) * P], xg[:, g, kc * P:(kc + 1) * P], ident[:, :])
                mm.then_inc(xg_t, 1)

            def gate_up(g):
                q = g % NW
                pe.wait_ge(xg_kept, g + 1)
                pe.wait_ge(w_in[q], 32 * (g // NW + 1))
                if g == 0:
                    pe.wait_ge(indexed, 1)
                else:
                    pe.wait_ge(gu_mul, g)
                for kc in range(KC):
                    for e in range(EG):
                        mm = mmul(b_gu[e * CAP:(e + 1) * CAP, 0:2 * I_], xgT[:, g % 2, kc, e * CAP:(e + 1) * CAP],
                                  wgu[:, q, e, kc, :], start=kc == 0, stop=kc == KC - 1)
                mm.then_inc(gu_mm, 1)

            def turn_h(g):
                pe.wait_ge(gu_mul, g + 1)
                if g >= 1:
                    pe.wait_ge(h_kept, g)
                for c in range(2):
                    mm = turn(b_h[0:IH, c * P:(c + 1) * P], hh[:, g % 2, c * IH:(c + 1) * IH], ident[:, :])
                mm.then_inc(h_t, 1)

            def down(g):
                q = g % NW
                pe.wait_ge(h_kept, g + 1)
                if g >= 1:
                    pe.wait_ge(y_made, g)
                for c in range(2):
                    for e in range(EG):
                        mm = mmul(b_d[e * CAP:(e + 1) * CAP, 0:D], hT[:, g % 2, c, e * CAP:(e + 1) * CAP],
                                  wd[:, q, e, c, :], start=c == 0, stop=c == 1)
                mm.then_inc(d_mm, 1)

            def combine(g):
                if g == 0:
                    pe.wait_ge(lit, 2)
                    pe.wait_ge(sh_kept, NT)
                    pe.wait_ge(sh_mul, len(pieces))
                pe.wait_ge(hot, g + 1)
                if g == 0:
                    for b in b_sum:
                        mmul(b[:, :], oneh[:, 0, 0, :], zeros[:, :], start=True, stop=False)
                for part in range(3):
                    pe.wait_ge(y_part[part], g + 1)
                    for i in range(HT):
                        mm = mmul(b_sum[i // 2][:, (i % 2) * D:(i % 2 + 1) * D], oneh[:, g % 2, i, :], yp[:, part, g, :],
                                  start=False, stop=g == G_ - 1 and part == 2 and i % 2 == 1)
                mm.then_inc(sums, 1)

            turn_x(0)
            for g in range(G_):
                gate_up(g)
                if g + 1 < G_:
                    turn_x(g + 1)
                if g >= 1:
                    combine(g - 1)
                turn_h(g)
                down(g)
            combine(G_ - 1)
            for i in range(HT, NT):
                pe.wait_ge(hot, G_ + i - HT + 1)
                if i - HT >= 4:
                    pe.wait_ge(out_made, i - 3)
                elif i == HT:
                    pe.wait_ge(gu_mul, G_)
                    pe.wait_ge(h_kept, G_)
                    pe.wait_ge(y_made, G_)
                for g in range(G_):
                    for part in range(3):
                        mm = mmul(bk[i % 4][:, 0:D], oneh[:, i % 2, g, :], yp[:, part, g, :],
                                  start=g == 0 and part == 0, stop=g == G_ - 1 and part == 2)
                mm.then_inc(comb, 1)

        @block.vector
        def _(dve):
            v = nc.vector
            v.memset(lg[:, :, E_:E_ + 2], BIG).then_inc(lg_kept, 1)
            nin.vector(dve)

            def shared(n):
                c, g = pieces[n]
                k = SH[c + 1] - SH[c]
                dve.wait_ge(sh_act, n + 1)
                dve.wait_ge(sh_mm, 2 * n + 2)
                if g:
                    dve.wait_ge(sh_down, 4 * g)
                v.tensor_tensor(hsh[0:k, c, :], ssl[0:k, n % 2, :], bk[7][0:k, :], ALU.mult).then_inc(sh_mul, 1)

            for s in range(2):
                dve.wait_ge(logits, s + 1)
                v.tensor_copy(lg[:, 8 * s:8 * s + 8, 0:E_], bk[4 + s][:, :].rearrange("p (i e) -> p i e", e=E_)).then_inc(lg_kept, 1)
            dve.wait_ge(lg_kept, 3)
            for i in range(NT):
                v.max(out=mx[:, i, :], in_=lg[:, i, :]).then_inc(maxed, 1)
                dve.wait_ge(maxed, 3 * i + 1)
                v.match_replace(out=rep[:, i, :], in_to_replace=mx[:, i, :], in_values=lg[:, i, :],
                                imm_value=-BIG).then_inc(maxed, 1)
                dve.wait_ge(maxed, 3 * i + 2)
                v.tensor_scalar(rep[:, i, :], rep[:, i, :], -BIG, -1.0, ALU.is_equal, ALU.mult).then_inc(maxed, 1)
                if i in (5, 10):
                    shared(i // 5 - 1)
            v.tensor_scalar(nmx[:, :], mx[:, :, 2], -1.0, None, ALU.mult).then_inc(negm, 1)
            shared(2)
            dve.wait_ge(loaded, 112)
            for g in range(B):
                dve.wait_ge(mask_t, g + 1)
                v.scalar_tensor_tensor(out=key[:, g * L:(g + 1) * L], in0=iota[0:E_, g * L:(g + 1) * L],
                                       scalar=float(T), in1=bk[g][0:E_, :], op0=ALU.subtract,
                                       op1=ALU.mult).then_inc(keyed, 1)
            dve.wait_ge(keyed, 4)
            for r in range(CAP // 8):
                if r:
                    v.match_replace(out=key, in_to_replace=k32[:, 8 * r - 8:8 * r], in_values=key,
                                    imm_value=0.0).then_inc(ranked, 1)
                    if r >= 2:
                        shared(2 * r - 1)
                    dve.wait_ge(ranked, 2 * r)
                v.max(out=k32[:, 8 * r:8 * r + 8], in_=key).then_inc(ranked, 1)
                if r == 1:
                    dve.wait_ge(exped, NT)
                    v.reciprocal(rs[:, :], esum[:, :]).then_inc(scored, 1)
                    dve.wait_ge(scored, 1)
                    v.tensor_tensor(score[:, :, :], score[:, :, :], rs[:, :].unsqueeze(2).to_broadcast([P, NT, E_]),
                                    ALU.mult).then_inc(scored, 1)
                if r == 2:
                    shared(4)
                dve.wait_ge(ranked, 2 * r + 1)
            for n in range(6, 9):
                shared(n)
            dve.wait_ge(placed, 1)
            v.tensor_scalar(idxf[:, :], bk[0][:, 0:G_], -1.0, float(T), ALU.mult, ALU.add).then_inc(indexed, 1)
            dve.wait_ge(indexed, 1)
            v.tensor_copy(idx[:, :], idxf[:, :]).then_inc(indexed, 1)
            for n in range(9, len(pieces)):
                shared(n)

            def weigh(g):
                dve.wait_ge(gathered[g], 16)
                v.tensor_tensor(own[:, g, :], own[:, g, :], xg[:, g, D:ROW], ALU.mult).then_inc(weighed, 1)
                dve.wait_ge(weighed, 2 * g + 1)
                v.tensor_reduce(ws[:, g:g + 1], own[:, g, :], AX.X, ALU.add).then_inc(weighed, 1)

            def last_part(g):
                dve.wait_ge(y_part[1], g + 1)
                v.tensor_tensor(yp[:, 2, g, :], yf[:, g % 2, 1, :], yp[:, 1, g, :], ALU.subtract).then_inc(y_part[2], 1)

            def hot_group(g):
                if g >= 2:
                    dve.wait_ge(sums, g - 1)
                v.tensor_tensor(oneh[:, g % 2, 0:HT, :], iota[:, 0:HT * P].rearrange("p (i t) -> p i t", t=P),
                                idxf[:, g:g + 1].unsqueeze(2).to_broadcast([P, HT, P]), ALU.is_equal).then_inc(hot, 1)

            def hot_tile(i):
                if i < HT + 2:
                    dve.wait_ge(sums, G_ - 1 + i - HT)
                else:
                    dve.wait_ge(comb, i - HT - 1)
                v.tensor_tensor(oneh[:, i % 2, :, :], iota[:, i * P:(i + 1) * P].unsqueeze(1).to_broadcast([P, G_, P]),
                                idxf[:, :].unsqueeze(2).to_broadcast([P, G_, P]), ALU.is_equal).then_inc(hot, 1)

            for g in range(G_):
                weigh(g)
                dve.wait_ge(gu_act, g + 1)
                if g >= 2:
                    dve.wait_ge(h_t, g - 1)
                v.tensor_tensor(hh[:, g % 2, :], sl[:, g % 2, :], b_gu[:, I_:2 * I_], ALU.mult).then_inc(gu_mul, 1)
                hot_group(g)
                dve.wait_ge(weighed, 2 * g + 2)
                dve.wait_ge(d_mm, g + 1)
                v.tensor_scalar(yf[:, g % 2, 0, :], b_d[:, 0:D], ws[:, g:g + 1], None, ALU.mult).then_inc(y_made, 1)
                dve.wait_ge(y_part[0], g + 1)
                v.tensor_tensor(yf[:, g % 2, 1, :], yf[:, g % 2, 0, :], yp[:, 0, g, :], ALU.subtract).then_inc(y_rest, 1)
                last_part(g)
            def out_tile(i):
                if i == 0:
                    dve.wait_ge(sums, G_)
                    dve.wait_ge(sh_kept, NT)
                if i >= HT:
                    dve.wait_ge(comb, i - HT + 1)
                src = bk[i % 4][:, 0:D] if i >= HT else b_sum[i // 2][:, (i % 2) * D:(i % 2 + 1) * D]
                v.tensor_tensor(xh[:, i, :], xh[:, i, :], src, ALU.add).then_inc(out_made, 1)
                if HT <= i < NT - 2:
                    hot_tile(i + 2)
                dve.wait_ge(out_made, i + 1)

            hot_tile(HT)
            hot_tile(HT + 1)
            nout.vector(dve, out_tile)

        @block.scalar
        def _(act):
            s_ = nc.scalar
            nin.scalar(act)

            def shared(n):
                c, g = pieces[n]
                k = SH[c + 1] - SH[c]
                act.wait_ge(sh_mm, 2 * n + 1)
                if n >= 2:
                    act.wait_ge(sh_mul, n - 1)
                s_.activation(ssl[0:k, n % 2, :], bk[6][0:k, :], ACT.Silu).then_inc(sh_act, 1)

            def keep_shared(g):
                if g == 0:
                    act.wait_ge(stored_x, 16)
                for i in range(4 * g, 4 * g + 4):
                    act.wait_ge(sh_down, i + 1)
                    s_.activation(xh[:, i, :], bk[4 + i % 2][:, 0:D], ACT.Identity).then_inc(sh_kept, 1)

            for n in range(3):
                shared(n)
            act.wait_ge(negm, 1)
            for i in range(NT):
                s_.activation(score[:, i, :], lg[:, i, 0:E_], ACT.Exp, bias=nmx[:, i:i + 1],
                              accum_out=esum[:, i:i + 1]).then_inc(exped, 1)
            for g in range(1, B):
                shared(3 * g)
                keep_shared(g - 1)
                shared(3 * g + 1)
                shared(3 * g + 2)
            keep_shared(B - 1)

            def keep_x(g):
                act.wait_ge(xg_t, g + 1)
                if g >= 2:
                    act.wait_ge(gu_mm, g - 1)
                s_.activation(xgT[:, g % 2, :, :], b_x[:, 0:KC * P].rearrange("p (c t) -> p c t", c=KC),
                              ACT.Identity).then_inc(xg_kept, 1)

            def keep_h(g):
                act.wait_ge(h_t, g + 1)
                if g >= 2:
                    act.wait_ge(d_mm, g - 1)
                s_.activation(hT[:, g % 2, :, :], b_h[0:IH, 0:2 * P].rearrange("p (c t) -> p c t", c=2),
                              ACT.Identity).then_inc(h_kept, 1)

            keep_x(0)
            for g in range(G_):
                act.wait_ge(gu_mm, g + 1)
                if g >= 2:
                    act.wait_ge(gu_mul, g - 1)
                s_.activation(sl[:, g % 2, :], b_gu[:, 0:I_], ACT.Silu).then_inc(gu_act, 1)
                if g + 1 < G_:
                    keep_x(g + 1)
                keep_h(g)
                act.wait_ge(y_made, g + 1)
                s_.activation(yp[:, 0, g, :], yf[:, g % 2, 0, :], ACT.Identity).then_inc(y_part[0], 1)
                act.wait_ge(y_rest, g + 1)
                s_.activation(yp[:, 1, g, :], yf[:, g % 2, 1, :], ACT.Identity).then_inc(y_part[1], 1)
            nout.scalar(act)

        @block.gpsimd
        def _(pool):
            nc.gpsimd.memset(zrow[:, :], 0.0).then_inc(lit, 1)
            nc.gpsimd.memset(zeros[:, :], 0.0).then_inc(lit, 1)
            pool.wait_ge(indexed, 2)
            pool.wait_ge(stored_x, 16)
            pool.wait_ge(stored, 32)
            for g in range(G_):
                nc.gpsimd.indirect_dma_start(out=xg[:, g, :], out_offset=None, in_=tab,
                                             in_offset=bass.IndirectOffsetOnAxis(ap=idx[:, g:g + 1], axis=0)
                                             ).then_inc(gathered[g], 16)


def laid_out_experts(g, chunks):
    e, gg = np.arange(E_), np.arange(G_)
    pick = (e[:, None, None] == EG * gg[None, None, :] + np.arange(EG)[None, :, None]).astype(np.float32)
    own = (EG * gg[None, :, None] + (np.arange(P) // CAP)[:, None, None] == e[None, None, :]).astype(np.float32)
    gu = np.concatenate([g("L0_ffn_w_gate"), g("L0_ffn_w_up")], axis=2)
    return {
        "ex_gw": chunks(g("L0_ffn_gate_w").T),
        "ex_sw": np.stack([chunks(g("L0_ffn_sw_gate")), chunks(g("L0_ffn_sw_up"))], axis=2),
        "ex_swd": g("L0_ffn_sw_down"),
        "ex_pick": pick,
        "ex_own": own,
        "ex_iota": np.arange(T, dtype=np.float32),
        "ex_wgu": gu.reshape(G_, EG, KC, P, 2 * I_).transpose(0, 3, 1, 2, 4),
        "ex_wd": g("L0_ffn_w_down").reshape(G_, EG, 2, IH, D).transpose(0, 3, 1, 2, 4),
    }


H = 16
DK = 128
TAPS = 4
TB = L // P
LEVELS = 7
L2_EPS = 1e-6
F16 = mybir.dt.float16
WS = 256.0
PARTS = ((0, 0), (0, 1), (1, 0))


def tot_at(j):
    return sum(L >> i for i in range(j))


def right(ap, j):
    w = 1 << j
    if len(ap.shape) == 2:
        return ap.rearrange("p (n s w) -> p n s w", s=2, w=w)[:, :, 1, :]
    return ap.rearrange("p q (n s w) -> p q n s w", s=2, w=w)[:, :, :, 1, :]


def left(ap, j):
    w = 1 << j
    if len(ap.shape) == 2:
        return ap.rearrange("p (n s w) -> p n s w", s=2, w=w)[:, :, 0, :]
    return ap.rearrange("p q (n s w) -> p q n s w", s=2, w=w)[:, :, :, 0, :]


def dense(ap, j):
    w = 1 << j
    if len(ap.shape) == 2:
        return ap.rearrange("p (n w) -> p n w", w=w)
    return ap.rearrange("p q (n w) -> p q n w", w=w)


def stage_delta(nc, x, ident, banks, a):
    ctx = ExitStack()
    with ctx:
        m = Pools(nc, ctx)
        acc = m.sb("da_acc", [P, NT, D])
        nout = NormOut(nc, m, "da_out", x, acc)
        fgs = m.sb("da_fgs", [P, 2, 2, T], F16)
        xs = m.sb("da_xs", [P, 2, KC, T], F16)
        beta = m.sb("da_beta", [P, H + 1, NT])
        negA = m.sb("da_negA", [P, H + 1])
        AT = m.sb("da_AT", [P, LEVELS, TB, P])
        Yf = m.sb("da_Yf", [P, LEVELS, TB, P])
        w_raw = m.sb("da_w_raw", [P, KC * 3 + 2, DK])
        hc_raw = m.sb("da_hc_raw", [P, 3 * TAPS + 1])
        mask = m.sb("da_mask", [P, LEVELS, P // 2])
        onw = m.sb("da_onw", [P, 1])
        consts = m.sem("da_consts")
        w_in = m.sem("da_w_in")

        with ExitStack() as c2:
            m2 = Pools(nc, c2)
            xh = m2.sb("da_xh", [P, NT, D])
            xT = m2.sb("da_xT", [P, KC, T])
            wfga = m2.sb("da_wfga", [P, KC, 2, DK])
            wb = m2.sb("da_wb", [P, KC, H + 1])
            alog = m2.sb("da_alog", [P, H + 1])
            nin = NormIn(nc, m2, "da_in", x, ident, xT, xh, banks[0:4])
            loaded = m2.sem("da_loaded")
            inner = m2.sem("da_inner")
            inner_hi = m2.sem("da_inner_hi")
            inner_kept = m2.sem("da_inner_kept")
            x_hi = m2.sem("da_x_hi")
            beta_mm = m2.sem("da_beta_mm")
            done = m2.sem("da_small")
            with nc.Block() as block:
                @block.sync
                def _(sp):
                    sp.dma_start(wfga[:, :, :, :], a["da_wfga"]).then_inc(loaded, 16)
                    sp.dma_start(wb[:, :, :], a["da_wb"]).then_inc(loaded, 16)
                    sp.dma_start(w_raw[:, :, :], a["da_w"][0]).then_inc(w_in, 16)
                    sp.dma_start(hc_raw[:, :], a["da_hc"][0]).then_inc(w_in, 16)
                    sp.dma_start(mask[:, :, :], a["da_mask"]).then_inc(consts, 16)
                    sp.dma_start(onw[:, :], a["da_onw"]).then_inc(consts, 16)
                    sp.dma_start(alog[:, :], a["da_alog"].partition_broadcast(P)).then_inc(loaded, 16)

                @block.tensor
                def _(pe):
                    nin.tensor(pe)
                    pe.wait_ge(loaded, 48)
                    for b in range(B):
                        nin.done(pe, b + 1) if b else nin.done(pe)
                        for s in range(2):
                            g = 2 * b + s
                            if g >= 2:
                                pe.wait_ge(inner_kept, g - 1)
                            for kc in range(KC):
                                mm = nc.tensor.matmul(banks[4 + s][:, :], wfga[:, kc, s, :],
                                                      xT[:, kc, b * L:(b + 1) * L], start=kc == 0, stop=kc == KC - 1)
                            mm.then_inc(inner, 1)
                    for i in range(NT):
                        for kc in range(KC):
                            mm = nc.tensor.matmul(banks[6][:, i * (H + 1):(i + 1) * (H + 1)], xT[:, kc, i * P:(i + 1) * P],
                                                  wb[:, kc, :], start=kc == 0, stop=kc == KC - 1)
                    mm.then_inc(beta_mm, 1)

                @block.scalar
                def _(act):
                    nin.scalar(act)
                    for b in range(B):
                        nin.done(act, b + 1)
                        nc.scalar.activation(xs[:, 0, :, b * L:(b + 1) * L], xT[:, :, b * L:(b + 1) * L],
                                             ACT.Identity).then_inc(x_hi, 1)
                        for s in range(2):
                            act.wait_ge(inner, 2 * b + s + 1)
                            nc.scalar.activation(fgs[:, 0, s, b * L:(b + 1) * L], banks[4 + s][:, :],
                                                 ACT.Identity).then_inc(inner_hi, 1)
                    act.wait_ge(beta_mm, 1)
                    nc.scalar.activation(beta[:, :, :].rearrange("p h i -> p i h"),
                                         banks[6][:, 0:NT * (H + 1)].rearrange("p (i h) -> p i h", h=H + 1), ACT.Sigmoid)
                    act.wait_ge(loaded, 48)
                    nc.scalar.activation(alog[:, :], alog[:, :], ACT.Exp).then_inc(done, 1)

                @block.vector
                def _(dve):
                    nin.vector(dve)
                    for b in range(B):
                        t = slice(b * L, (b + 1) * L)
                        for s in range(2):
                            dve.wait_ge(inner_hi, 2 * b + s + 1)
                            nc.vector.tensor_tensor(fgs[:, 1, s, t], banks[4 + s][:, :], fgs[:, 0, s, t],
                                                    ALU.subtract).then_inc(inner_kept, 1)
                    dve.wait_ge(done, 1)
                    nc.vector.tensor_scalar(negA[:, :], alog[:, :], -1.0, None, ALU.mult)

                @block.gpsimd
                def _(pool):
                    for t in (acc[:, :, :], AT[:, :, :, :], Yf[:, :, :, :]):
                        nc.gpsimd.memset(t, 0.0)
                    for b in range(B):
                        t = slice(b * L, (b + 1) * L)
                        pool.wait_ge(x_hi, b + 1)
                        nin.done(pool, b + 1)
                        nc.gpsimd.tensor_tensor(xs[:, 1, :, t], xT[:, :, t], xs[:, 0, :, t], ALU.subtract)

        w = m.sb("da_w", [P, 2, KC * 3 + 2, DK], F16)
        hc = m.sb("da_hc", [P, 3 * TAPS + 1])
        wo_raw = m.sb("da_wo_raw", [P, D])
        wo = m.sb("da_wo", [P, D])
        ones = m.sb("da_ones", [P, 1])
        y = m.sb("da_y", [P, 3, L])
        vc = m.sb("da_vc", [P, L])
        sqr = m.sb("da_sqr", [P, 3, L])
        gx = m.sb("da_gx", [P, 2, L])
        kq = m.sb("da_kq", [P, 2, 2, L])
        dec = m.sb("da_dec", [P, 2, 2 * L])
        Vt = m.sb("da_Vt", [P, 2, TB, DK])
        sg = m.sb("da_sg", [P, 2, L])
        st = m.sb("da_st", [P, 2, 5, TB])
        rt = m.sb("da_rt", [P, 2, TB])
        kqP = m.sb("da_kqP", [P, 2, 2, L])
        kQ = m.sb("da_kQ", [P, 2, L])
        kQt = m.sb("da_kQt", [P, TB, DK])
        M = m.sb("da_M", [P, TB, P // 2])
        MT = m.sb("da_MT", [P, 2, TB, P])
        AqT = m.sb("da_AqT", [P, 2, TB, P])
        Rb = m.sb("da_R", [P, DK])
        U = m.sb("da_U", [P, 2, DK])
        S = m.sb("da_S", [P, 2, DK])
        og = m.sb("da_og", [P, L])
        osq = m.sb("da_osq", [P, L])
        ca = m.sb("da_ca", [P, 3, TB])
        pp, pa, pY, pM, pZT, pS, pO = banks[0:2], banks[2], banks[3], banks[4], banks[5], banks[6], banks[7]
        pR, pU, pSn = pS[:, 0:DK], pS[:, DK:2 * DK], pS[:, 2 * DK:3 * DK]

        zeroed = m.sem("da_zeroed")
        onw_half = m.sem("da_onw_half")
        head_used = m.sem("da_head_used")
        w_hi = m.sem("da_w_hi")
        w_lo = m.sem("da_w_lo")
        wo_in = m.sem("da_wo_in")
        wo_scaled = m.sem("da_wo_scaled")
        proj = [m.sem(f"da_proj_{s}") for s in "qkvfg"]
        tap0 = [m.sem(f"da_tap0_{s}") for s in "qkv"]
        tapped = [m.sem(f"da_tapped_{s}") for s in "qkv"]
        silud = [m.sem(f"da_silu_{s}") for s in "qkv"]
        squared = m.sem("da_squared")
        kq_mul = m.sem("da_kq_mul")
        gate_in = m.sem("da_gate_in")
        gate_ln = m.sem("da_gate_ln")
        gate_sp = m.sem("da_gate_sp")
        gate_out = m.sem("da_gate_out")
        tanhd = m.sem("da_tanhd")
        stat_mm = m.sem("da_stat_mm")
        stat_v = m.sem("da_stat_v")
        rooted = m.sem("da_rooted")
        v_turned = m.sem("da_v_turned")
        v_kept = m.sem("da_v_kept")
        kqP_begun = m.sem("da_kqP_begun")
        kQ_begun = m.sem("da_kQ_begun")
        tot = m.sem("da_tot")
        scaled = m.sem("da_scaled")
        pairs = m.sem("da_pairs")
        start = m.sem("da_start")
        masked = m.sem("da_masked")
        y_mm = m.sem("da_y_mm")
        y_kept = m.sem("da_y_kept")
        zt_mm = m.sem("da_zt_mm")
        grownT = m.sem("da_grownT")
        m_turned = m.sem("da_m_turned")
        m_kept = m.sem("da_m_kept")
        kq_turned = m.sem("da_kq_turned")
        kq_kept = m.sem("da_kq_kept")
        r_mm = m.sem("da_r_mm")
        r_made = m.sem("da_r_made")
        u_mm = m.sem("da_u_mm")
        u_kept = m.sem("da_u_kept")
        s_mm = m.sem("da_s_mm")
        s_made = m.sem("da_s_made")
        o_mm = m.sem("da_o_mm")
        og_made = m.sem("da_og_made")
        osq_made = m.sem("da_osq_made")
        so_mm = m.sem("da_so_mm")
        ca_v = m.sem("da_ca_v")
        ca_s = m.sem("da_ca_s")
        wo_mm = m.sem("da_wo_mm")
        acc_made = m.sem("da_acc_made")
        CREDIT = {"DVE": ((grownT, 7), (masked, 14), (acc_made, 4)), "ACT": ((v_kept, 1), (kq_kept, 1))}
        ZEROED = 10

        block = ctx.enter_context(nc.Block())

        @block.sync
        def _(sp):
            def load_head(h):
                sp.dma_start(w_raw[:, :, :], a["da_w"][h]).then_inc(w_in, 16)
                sp.dma_start(hc_raw[:, :], a["da_hc"][h]).then_inc(w_in, 16)

            sp.dma_start(wo_raw[:, :], a["da_wo"][0]).then_inc(wo_in, 16)
            with sp.Fori(0, H) as h:
                sp.wait_ge(w_hi, h * 3 + 3)
                sp.sem_inc(head_used, 1)
                sp.wait_ge(w_lo, h + 1)
                sp.sem_inc(head_used, 1)
                load_head(h + 1)
                sp.wait_ge(wo_scaled, h + 1)
                sp.sem_inc(head_used, 1)
                sp.dma_start(wo_raw[:, :], a["da_wo"][h + 1]).then_inc(wo_in, 16)
            sp.wait_ge(w_in, 32 * (H + 1))
            sp.wait_ge(wo_in, 16 * (H + 1))

        @block.tensor
        def _(pe):
            mmul, turn = nc.tensor.matmul, nc.tensor.transpose

            def project(s, n, b, half=None):
                if half == 1:
                    pass
                elif s == 0 and not isinstance(n, int):
                    pe.wait_ge(v_kept, n + 1)
                elif s == 3 and not isinstance(n, int):
                    pe.wait_ge(kq_kept, n)
                elif s == 1:
                    pe.wait_ge(gate_in, n + 1)
                elif s == 2:
                    pe.wait_ge(tapped[0], 3 * n + 3)
                elif s == 4:
                    pe.wait_ge(tapped[1], 3 * n + 3)
                out = pp[(0, 1, 0, 1, 1)[s]][:, :]
                if s < 3:
                    chunks = [(3 * kc + s, kc, xs) for kc in (range(KC) if half is None else (half,))]
                else:
                    chunks = [(3 * KC + s - 3, s - 3, fgs)]
                for r, c, src in chunks:
                    for i, (pw, px) in enumerate(PARTS):
                        mm = mmul(out, w[:, pw, r, :], src[:, px, c, b * L:(b + 1) * L],
                                  start=i == 0 and (s >= 3 or c == 0), stop=i == 2 and (s >= 3 or c == KC - 1))
                if half != 0:
                    mm.then_inc(proj[s], 1)

            def sums(n, parts=(0, 1, 2)):
                if parts[0] == 0:
                    pe.wait_ge(squared, n + 1)
                    pe.wait_ge(kq_mul, n + 1)
                    pe.wait_ge(tanhd, n + 1)
                for s in parts:
                    for i in range(TB):
                        mm = mmul(pp[1][:, s * TB + i:s * TB + i + 1], sqr[:, s, i * P:(i + 1) * P], ones[:, :],
                                  start=True, stop=True)
                if parts[-1] == 2:
                    mm.then_inc(stat_mm, 1)

            def turn_v(n):
                pe.wait_ge(silud[2], n + 1)
                for i in range(TB):
                    mm = turn(pp[0][:, i * P:(i + 1) * P], vc[:, i * P:(i + 1) * P], ident[:, :])
                mm.then_inc(v_turned, 1)

            def pair(j, n, p):
                if j == 0:
                    pe.wait_ge(kqP_begun, n + 1)
                    pe.wait_ge(kQ_begun, n + 1)
                else:
                    pe.wait_ge(scaled, 14 * n + 2 * j)
                pe.wait_ge(masked, 14 * n + 14 + 2 * j)
                for i in range(TB):
                    out = pa[:, :].rearrange("p (s i t) -> p s i t", s=2, i=TB)[:, :, i, :]
                    mm = mmul(dense(out, j), kQ[:, p, i * P:(i + 1) * P], right(kqP[:, p, :, i * P:(i + 1) * P], j),
                              start=True, stop=True)
                mm.then_inc(pairs, 1)

            def level_y(j, n):
                pe.wait_ge(masked, 14 * n + 14 + 2 * j + 1)
                if j == 0:
                    pe.wait_ge(start, 3 * n + 3)
                else:
                    pe.wait_ge(m_kept, 6 * n + j)
                for i in range(TB):
                    out = pY[:, i * 64:(i + 1) * 64]
                    if j < LEVELS - 1:
                        mm = mmul(dense(out, j), AT[:, j, i, :], dense(M[:, i, :], j), start=True, stop=True)
                    else:
                        mm = mmul(out[64:P], AT[:, j, i, 64:P], M[:, i, :], start=True, stop=True)
                mm.then_inc(y_mm, 1)

            def level_zt(j, n, p):
                pe.wait_ge(y_kept, 7 * n + j + 1)
                for i in range(TB):
                    out = pZT[:, i * 64:(i + 1) * 64]
                    if j < LEVELS - 1:
                        mm = mmul(dense(out, j), Yf[:, j, i, :], right(MT[:, p, i, :], j), start=True, stop=True)
                    else:
                        mm = mmul(out[0:64], Yf[:, j, i, 0:64], MT[:, p, i, 64:P], start=True, stop=True)
                mm.then_inc(zt_mm, 1)

            def turn_m(j, n, p):
                pe.wait_ge(grownT, 7 * n + 7 + j + 1)
                for i in range(TB):
                    mm = turn(pM[:, i * P:(i + 1) * P], MT[:, p, i, :], ident[:, :])
                mm.then_inc(m_turned, 1)

            def turn_kq(n, p):
                pe.wait_ge(scaled, 14 * n + 14)
                pe.wait_ge(stat_v, 5 * n + 8)
                for i in range(TB):
                    mm = turn(pp[1][:, i * P:(i + 1) * P], kQ[:, p, i * P:(i + 1) * P], ident[:, :])
                mm.then_inc(kq_turned, 1)

            def state_r(i, n, q):
                pe.wait_ge(s_made, 3 * n + i)
                mmul(pR, kqP[:, q, 0, i * P:(i + 1) * P], S[:, i % 2, :], start=True, stop=True).then_inc(r_mm, 1)

            def state_u(i, n, q):
                if i:
                    pe.wait_ge(r_made, 3 * n + i)
                else:
                    pe.wait_ge(v_kept, n + 1)
                    pe.wait_ge(grownT, 7 * n + 7)
                    pe.wait_ge(acc_made, 4 * n + 4)
                mmul(pU, MT[:, q, i, :], Rb[:, :] if i else Vt[:, q, 0, :], start=True, stop=True).then_inc(u_mm, 1)

            def state_s(i, n, q):
                t = slice(i * P, (i + 1) * P)
                pe.wait_ge(u_kept, 4 * n + i + 1)
                if i < TB - 1:
                    if i == 0:
                        pe.wait_ge(kq_kept, n + 1)
                    mmul(pSn, kQt[:, i, :], U[:, i % 2, :], start=True, stop=True).then_inc(s_mm, 1)
                if i:
                    mmul(pO[:, t], S[:, i % 2, :], kqP[:, q, 1, t], start=True, stop=False)
                else:
                    pe.wait_ge(masked, 14 * n + 14)
                mmul(pO[:, t], U[:, i % 2, :], AqT[:, q, i, :], start=i == 0, stop=True).then_inc(o_mm, 1)

            def out_norm(n):
                pe.wait_ge(osq_made, n + 1)
                for i in range(TB):
                    mm = mmul(pO[:, i:i + 1], osq[:, i * P:(i + 1) * P], ones[:, :], start=True, stop=True)
                mm.then_inc(so_mm, 1)

            def out_mm(half, n, b, h):
                if half:
                    pe.wait_ge(ca_v, n + 1)
                elif b == 1 or isinstance(n, int):
                    pe.wait_ge(wo_scaled, h + 1)
                for i in (0, 1):
                    t = 2 * half + i
                    mm = mmul((pO if half else pS)[:, i * D:(i + 1) * D], og[:, t * P:(t + 1) * P], wo[:, :],
                              start=True, stop=True)
                mm.then_inc(wo_mm, 1)

            pe.wait_ge(zeroed, ZEROED)
            pe.wait_ge(w_hi, 3)
            pe.wait_ge(w_lo, 1)
            for s in (3, 0, 1, 2, 4):
                project(s, 0, 0)
            sums(0)
            turn_v(0)
            pair(0, 0, 0)
            with pe.Fori(0, H) as h:
                for b in range(B):
                    n, n1, b1, p, q = h * B + b, h * B + b + 1, (b + 1) % B, b % 2, (b + 1) % 2
                    level_y(0, n)
                    state_u(0, n, q)
                    if b1 == 0:
                        pe.wait_ge(w_hi, 3 * h + 6)
                        pe.wait_ge(w_lo, h + 2)
                    project(3, n1, b1)
                    state_s(0, n, q)
                    pair(1, n, p)
                    level_zt(0, n, p)
                    state_r(1, n, q)
                    project(0, n1, b1, 0)
                    turn_m(0, n, p)
                    state_u(1, n, q)
                    project(0, n1, b1, 1)

                    level_y(1, n)
                    state_s(1, n, q)
                    pair(2, n, p)
                    state_r(2, n, q)
                    level_zt(1, n, p)
                    state_u(2, n, q)
                    project(1, n1, b1, 0)
                    turn_m(1, n, p)
                    state_s(2, n, q)

                    level_y(2, n)
                    state_r(3, n, q)
                    pair(3, n, p)
                    state_u(3, n, q)
                    level_zt(2, n, p)
                    state_s(3, n, q)
                    project(1, n1, b1, 1)
                    turn_m(2, n, p)
                    project(2, n1, b1, 0)

                    level_y(3, n)
                    pair(4, n, p)
                    level_zt(3, n, p)
                    project(2, n1, b1, 1)
                    turn_m(3, n, p)
                    out_norm(n)

                    level_y(4, n)
                    pair(5, n, p)
                    out_mm(0, n, b, h)
                    level_zt(4, n, p)
                    out_mm(1, n, b, h)
                    turn_m(4, n, p)
                    project(4, n1, b1)

                    level_y(5, n)
                    pair(6, n, p)
                    level_zt(5, n, p)
                    sums(n1, (0,))
                    turn_m(5, n, p)
                    sums(n1, (1, 2))

                    level_y(6, n)
                    turn_v(n1)
                    level_zt(6, n, p)
                    pair(0, n1, q)
                    turn_kq(n, p)
            n = H * B
            for i in range(TB):
                if i:
                    state_r(i, n, 1)
                state_u(i, n, 1)
                state_s(i, n, 1)
            out_norm(n)
            out_mm(0, n, 0, H - 1)
            out_mm(1, n, 0, H - 1)

        @block.vector
        def _(dve):
            v = nc.vector

            def tap(s, k, n):
                if k == 1:
                    dve.wait_ge(tap0[s], n + 1)
                else:
                    dve.wait_ge(tapped[s], 3 * n + k - 1)
                v.scalar_tensor_tensor(out=y[:, s, k:L], in0=pp[(0, 1, 0)[s]][:, 0:L - k],
                                       scalar=hc[:, s * TAPS + 3 - k:s * TAPS + 4 - k], in1=y[:, s, k:L],
                                       op0=ALU.mult, op1=ALU.add).then_inc(tapped[s], 1)

            def split_w(h):
                dve.wait_ge(w_in, 32 * (h + 1))
                dve.wait_ge(w_hi, 3 * h + 1)
                v.scalar_tensor_tensor(out=w[:, 1, :, :], in0=w_raw[:, :, :], scalar=WS, in1=w[:, 0, :, :],
                                       op0=ALU.mult, op1=ALU.subtract).then_inc(w_lo, 1)

            def mul_kq(n, p):
                dve.wait_ge(silud[0], n + 1)
                dve.wait_ge(silud[1], n + 1)
                v.tensor_tensor(sqr[:, 2, :], kq[:, p, 0, :], kq[:, p, 1, :], ALU.mult).then_inc(kq_mul, 1)

            def softplus(n):
                dve.wait_ge(gate_ln, 3 * n + 3)
                v.scalar_tensor_tensor(out=gx[:, 1, :], in0=gx[:, 0, :], scalar=0.0, in1=gx[:, 1, :],
                                       op0=ALU.max, op1=ALU.add).then_inc(gate_sp, 1)

            def stats(n, p, b, h):
                dve.wait_ge(stat_mm, n + 1)
                v.tensor_scalar(st[:, p, 0, :], pp[1][:, 0:TB], L2_EPS, None, ALU.add).then_inc(stat_v, 1)
                v.tensor_scalar(st[:, p, 1, :], pp[1][:, TB:2 * TB], L2_EPS, L2_EPS * DK, ALU.add,
                                ALU.mult).then_inc(stat_v, 1)
                v.tensor_copy(st[:, p, 2, :], pp[1][:, 2 * TB:3 * TB]).then_inc(stat_v, 1)
                dve.wait_ge(stat_v, 5 * n + 1)
                v.reciprocal(st[:, p, 3, :], st[:, p, 0, :]).then_inc(stat_v, 1)
                dve.wait_ge(stat_v, 5 * n + 4)
                v.tensor_tensor(st[:, p, 4, :], st[:, p, 3, :], beta[:, h, b * TB:(b + 1) * TB],
                                ALU.mult).then_inc(stat_v, 1)

            def begin(dst, k, p):
                n = dst.shape[-1]
                eye = ident[:, ::P // n].unsqueeze(1).to_broadcast([P, TB, n])
                v.tensor_tensor(dst, eye, st[:, p, k, :].unsqueeze(2).to_broadcast([P, TB, n]),
                                ALU.mult).then_inc(start, 1)

            def mask_a(j, n):
                dve.wait_ge(pairs, 7 * n + j + 1)
                if j:
                    dve.wait_ge(masked, 14 * n + 14 + 2 * j)
                else:
                    dve.wait_ge(start, 3 * n + 3)
                src = pa[:, :].rearrange("p (s i t) -> p s i t", s=2, i=TB)
                mk = dense(mask[:, j, :].unsqueeze(1).to_broadcast([P, TB, P // 2]), j)
                v.tensor_tensor(right(AT[:, j, :, :], j), dense(src[:, 0], j), mk, ALU.mult).then_inc(masked, 1)

            def mask_aq(j, n, p):
                src = pa[:, :].rearrange("p (s i t) -> p s i t", s=2, i=TB)
                mku = dense(mask[:, j, :].bitcast(U32).unsqueeze(1).to_broadcast([P, TB, P // 2]), j)
                v.copy_predicated(right(AqT[:, p, :, :], j), mku, dense(src[:, 1], j)).then_inc(masked, 1)

            def keep_m(j, n):
                dve.wait_ge(m_turned, 6 * n + j + 1)
                v.tensor_copy(dense(M[:, :, :], j + 1),
                              left(pM[:, :].rearrange("p (i t) -> p i t", i=TB), j + 1)).then_inc(m_kept, 1)

            def growT(j, n, p):
                dve.wait_ge(zt_mm, 7 * n + j + 1)
                k = P if j < LEVELS - 1 else 64
                v.tensor_tensor(right(MT[0:k, p, :, :], j), right(MT[0:k, p, :, :], j),
                                dense(pZT[0:k, 0:256].rearrange("p (i t) -> p i t", i=TB), j),
                                ALU.subtract).then_inc(grownT, 1)

            def state_r(i, n, q):
                dve.wait_ge(r_mm, 3 * n + i)
                v.tensor_tensor(Rb[:, :], Vt[:, q, i, :], pR, ALU.subtract).then_inc(r_made, 1)

            def state_s(i, n, q):
                dve.wait_ge(s_mm, 3 * n + i + 1)
                if i == 0:
                    v.tensor_copy(S[:, 1, :], pSn).then_inc(s_made, 1)
                else:
                    dve.wait_ge(s_made, 3 * n + i)
                    c = tot_at(LEVELS) + i
                    v.scalar_tensor_tensor(out=S[:, (i + 1) % 2, :], in0=S[:, i % 2, :], scalar=dec[:, q, c:c + 1],
                                           in1=pSn, op0=ALU.mult, op1=ALU.add).then_inc(s_made, 1)

            def gated(n, q):
                dve.wait_ge(o_mm, 4 * n + 4)
                v.scalar_tensor_tensor(out=og[:, :], in0=sg[:, q, :], scalar=1.0, in1=pO[:, :],
                                       op0=ALU.add, op1=ALU.mult).then_inc(og_made, 1)

            def norm(n, q):
                dve.wait_ge(so_mm, n + 1)
                v.scalar_tensor_tensor(out=ca[:, 0, :], in0=pO[:, 0:TB], scalar=1.0 / DK, in1=st[:, q, 1, :],
                                       op0=ALU.mult, op1=ALU.add).then_inc(ca_v, 1)

            def collect(half, n, b):
                if half == 0:
                    dve.wait_ge(ca_s, 2 * n + 2)
                dve.wait_ge(wo_mm, 2 * n + half + 1)
                for i in (0, 1):
                    t = 2 * half + i
                    row = (b - 1) % B * TB + t
                    v.scalar_tensor_tensor(out=acc[:, row, :], in0=(pO if half else pS)[:, i * D:(i + 1) * D],
                                           scalar=ca[:, 2, t:t + 1], in1=acc[:, row, :],
                                           op0=ALU.mult, op1=ALU.add).then_inc(acc_made, 1)

            v.memset(ones[:, :], 1.0).then_inc(zeroed, 1)
            for s, c in CREDIT["DVE"]:
                dve.sem_inc(s, c)
            dve.wait_ge(consts, 32)
            dve.wait_ge(zeroed, ZEROED)
            split_w(0)
            dve.wait_ge(w_hi, 3)
            for s in range(3):
                for k in range(1, TAPS):
                    tap(s, k, 0)
                if s == 1:
                    softplus(0)
            mul_kq(0, 0)
            stats(0, 0, 0, 0)
            dve.wait_ge(stat_v, 5)
            begin(AqT[:, 0, :, :], 2, 0)
            begin(MT[:, 0, :, :], 4, 0)
            begin(M[:, :, :], 4, 0)
            mask_a(0, 0)
            mask_aq(0, 0, 0)
            with dve.Fori(0, H) as h:
                for b in range(B):
                    n, n1, b1, p, q = h * B + b, h * B + b + 1, (b + 1) % B, b % 2, (b + 1) % 2
                    state_s(0, n, q)
                    mask_a(1, n)
                    mask_aq(1, n, p)
                    growT(0, n, p)
                    state_r(1, n, q)
                    keep_m(0, n)
                    if b1 == 0:
                        dve.wait_ge(w_hi, 3 * h + 6)

                    state_s(1, n, q)
                    mask_a(2, n)
                    state_r(2, n, q)
                    mask_aq(2, n, p)
                    growT(1, n, p)
                    tap(0, 1, n1)
                    keep_m(1, n)
                    state_s(2, n, q)
                    softplus(n1)
                    tap(0, 2, n1)

                    state_r(3, n, q)
                    mask_a(3, n)
                    mask_aq(3, n, p)
                    growT(2, n, p)
                    tap(0, 3, n1)
                    keep_m(2, n)
                    tap(1, 1, n1)
                    gated(n, q)

                    mask_a(4, n)
                    mask_aq(4, n, p)
                    growT(3, n, p)
                    tap(1, 2, n1)
                    keep_m(3, n)
                    norm(n, q)
                    tap(1, 3, n1)
                    tap(2, 1, n1)

                    mask_a(5, n)
                    mask_aq(5, n, p)
                    growT(4, n, p)
                    tap(2, 2, n1)
                    keep_m(4, n)
                    tap(2, 3, n1)
                    mul_kq(n1, q)

                    mask_a(6, n)
                    mask_aq(6, n, p)
                    growT(5, n, p)
                    collect(0, n, b)
                    keep_m(5, n)
                    collect(1, n, b)
                    stats(n1, q, b1, h + 1 if b == B - 1 else h)

                    if b1 == B - 1:
                        dve.wait_ge(proj[4], n1 + 1)
                        split_w(h + 1)
                    dve.wait_ge(stat_v, 5 * n + 10)
                    begin(AqT[:, q, :, :], 2, q)
                    dve.wait_ge(y_mm, 7 * n + 7)
                    begin(M[:, :, :], 4, q)
                    growT(6, n, p)
                    begin(MT[:, q, :, :], 4, q)
                    mask_a(0, n1)
                    mask_aq(0, n1, q)
            n = H * B
            for i in range(TB):
                if i:
                    state_r(i, n, 1)
                if i < TB - 1:
                    state_s(i, n, 1)
            gated(n, 1)
            norm(n, 1)
            collect(0, n, 0)
            collect(1, n, 0)
            nout.vector(dve, lambda i: dve.wait_ge(acc_made, 4 * B * H + 8))

        @block.scalar
        def _(act):
            s_ = nc.scalar

            def split_w(h):
                act.wait_ge(w_in, 32 * (h + 1))
                s_.activation(w[:, 0, :, :], w_raw[:, :, :], ACT.Identity, scale=WS).then_inc(w_hi, 1)
                s_.activation(hc[:, 0:3 * TAPS], hc_raw[:, 0:3 * TAPS], ACT.Identity, scale=1.0 / WS).then_inc(w_hi, 1)
                s_.activation(hc[:, 3 * TAPS:], hc_raw[:, 3 * TAPS:], ACT.Identity).then_inc(w_hi, 1)

            def first_tap(s, n):
                act.wait_ge(proj[s], n + 1)
                s_.activation(y[:, s, :], pp[(0, 1, 0)[s]][:, :], ACT.Identity,
                              scale=hc[:, s * TAPS + 3:s * TAPS + 4]).then_inc(tap0[s], 1)

            def silu(s, n, p):
                act.wait_ge(tapped[s], 3 * n + 3)
                dst = (kq[:, p, 1, :], kq[:, p, 0, :], vc[:, :])[s]
                s_.activation(dst, y[:, s, :], ACT.Silu).then_inc(silud[s], 1)

            def begin_kQ(n, p):
                act.wait_ge(silud[1], n + 1)
                s_.activation(kQ[:, p, :], kq[:, p, 0, :], ACT.Identity).then_inc(kQ_begun, 1)

            def squares(n, p):
                s_.activation(sqr[:, 0:2, :], kq[:, p, :, :], ACT.Square).then_inc(squared, 1)

            def tanh_gate(n, p):
                act.wait_ge(proj[4], n + 1)
                s_.activation(sg[:, p, :], pp[1][:, :], ACT.Tanh, scale=0.5 / WS).then_inc(tanhd, 1)

            def gate_input(n):
                act.wait_ge(proj[3], n + 1)
                s_.activation(gx[:, 0, :], pp[1][:, :], ACT.Identity,
                              scale=1.0 / WS, bias=hc[:, 3 * TAPS:3 * TAPS + 1]).then_inc(gate_in, 1)

            def gate_log(k, n):
                if k == 0:
                    act.wait_ge(gate_in, n + 1)
                    s_.activation(gx[:, 1, :], gx[:, 0, :], ACT.Abs).then_inc(gate_ln, 1)
                elif k == 1:
                    act.wait_ge(gate_ln, 3 * n + 1)
                    s_.activation(gx[:, 1, :], gx[:, 1, :], ACT.Exp, scale=-1.0).then_inc(gate_ln, 1)
                else:
                    act.wait_ge(gate_ln, 3 * n + 2)
                    s_.activation(gx[:, 1, :], gx[:, 1, :], ACT.Ln, bias=1.0).then_inc(gate_ln, 1)

            def decays(p, h):
                s_.activation(dec[:, p, 0:L], gx[:, 1, :], ACT.Exp, scale=negA[:, bass.ds(h, 1)]).then_inc(gate_out, 1)

            def roots(n, p):
                act.wait_ge(stat_v, 5 * n + 1)
                s_.activation(rt[:, 0, :], st[:, p, 0, :], ACT.Ln).then_inc(rooted, 1)
                act.wait_ge(rooted, 2 * n + 1)
                s_.activation(rt[:, 1, :], rt[:, 0, :], ACT.Exp, scale=0.5).then_inc(rooted, 1)

            def keep_v(n, p):
                act.wait_ge(rooted, 2 * n + 2)
                act.wait_ge(v_turned, n + 1)
                for i in range(TB):
                    k = s_.activation(Vt[:, p, i, :], pp[0][:, i * P:(i + 1) * P], ACT.Identity,
                                      scale=rt[:, 1, i:i + 1])
                k.then_inc(v_kept, 1)

            def keep_y(j, n):
                act.wait_ge(y_mm, 7 * n + j + 1)
                k = 0 if j < LEVELS - 1 else 64
                s_.activation(left(Yf[k:P, j, :, :], j), dense(pY[k:P, 0:256].rearrange("p (i t) -> p i t", i=TB), j),
                              ACT.Identity).then_inc(y_kept, 1)

            def keep_kq(n):
                act.wait_ge(kq_turned, n + 1)
                s_.activation(kQt[:, :, :], pp[1][:, :].rearrange("p (i t) -> p i t", i=TB),
                              ACT.Identity).then_inc(kq_kept, 1)

            def keep_u(i, n):
                act.wait_ge(u_mm, 4 * n + i + 1)
                s_.activation(U[:, i % 2, :], pU, ACT.Identity).then_inc(u_kept, 1)

            def square_out(n):
                act.wait_ge(og_made, n + 1)
                s_.activation(osq[:, :], pO[:, :], ACT.Square).then_inc(osq_made, 1)

            def norm(n):
                act.wait_ge(ca_v, n + 1)
                s_.activation(ca[:, 1, :], ca[:, 0, :], ACT.Ln).then_inc(ca_s, 1)
                act.wait_ge(ca_s, 2 * n + 1)
                s_.activation(ca[:, 2, :], ca[:, 1, :], ACT.Exp, scale=-0.5).then_inc(ca_s, 1)

            for s, c in CREDIT["ACT"]:
                act.sem_inc(s, c)
            act.wait_ge(zeroed, ZEROED)
            split_w(0)
            act.wait_ge(w_hi, 3)
            s_.preload_act_table_set("natural_log_exp_and_others")
            gate_input(0)
            first_tap(0, 0)
            for k in range(3):
                gate_log(k, 0)
            first_tap(1, 0)
            first_tap(2, 0)
            act.wait_ge(gate_sp, 1)
            decays(0, 0)
            s_.preload_act_table_set("silu_and_others")
            for s in range(3):
                silu(s, 0, 0)
            begin_kQ(0, 0)
            squares(0, 0)
            tanh_gate(0, 0)
            s_.preload_act_table_set("natural_log_exp_and_others")
            roots(0, 0)
            keep_v(0, 0)
            with act.Fori(0, H) as h:
                for b in range(B):
                    n, n1, b1, p, q = h * B + b, h * B + b + 1, (b + 1) % B, b % 2, (b + 1) % 2
                    h1 = h + 1 if b == B - 1 else h
                    keep_y(0, n)
                    keep_u(0, n)
                    if b1 == 0:
                        act.wait_ge(w_hi, 3 * h + 6)
                    gate_input(n1)
                    gate_log(0, n1)
                    keep_u(1, n)
                    gate_log(1, n1)

                    keep_y(1, n)
                    first_tap(0, n1)
                    gate_log(2, n1)
                    keep_u(2, n)

                    keep_y(2, n)
                    act.wait_ge(gate_sp, n1 + 1)
                    keep_u(3, n)
                    decays(q, h1)
                    first_tap(1, n1)

                    keep_y(3, n)
                    square_out(n)
                    first_tap(2, n1)
                    norm(n)

                    s_.preload_act_table_set("silu_and_others")
                    keep_y(4, n)
                    silu(0, n1, q)
                    silu(1, n1, q)
                    begin_kQ(n1, q)
                    squares(n1, q)

                    keep_y(5, n)
                    tanh_gate(n1, q)
                    silu(2, n1, q)
                    if b1 == B - 1:
                        split_w(h + 1)
                    s_.preload_act_table_set("natural_log_exp_and_others")

                    keep_y(6, n)
                    roots(n1, q)
                    keep_v(n1, q)
                    keep_kq(n)
            n = H * B
            for i in range(TB):
                keep_u(i, n)
            square_out(n)
            norm(n)
            nout.scalar(act)

        @block.gpsimd
        def _(pool):
            g = nc.gpsimd

            def products(n, p):
                for j in range(LEVELS):
                    if j:
                        pool.wait_ge(tot, 7 * n + j)
                    src = dec[:, p, tot_at(j):tot_at(j + 1)].rearrange("p (n s) -> p n s", s=2)
                    g.tensor_tensor(dec[:, p, tot_at(j + 1):tot_at(j + 2)], src[:, :, 0], src[:, :, 1],
                                    ALU.mult).then_inc(tot, 1)

            def begin(n, p):
                pool.wait_ge(gate_out, n + 1)
                pool.wait_ge(silud[0], n + 1)
                pool.wait_ge(silud[1], n + 1)
                if not isinstance(n, int):
                    pool.wait_ge(o_mm, 4 * n)
                g.tensor_tensor(kqP[:, p, :, :], kq[:, p, :, :],
                                dec[:, p, 0:L].unsqueeze(1).to_broadcast([P, 2, L]), ALU.mult).then_inc(kqP_begun, 1)

            def scale(j, n, p):
                w_ = 1 << j
                nb = L >> (j + 1)
                pool.wait_ge(pairs, 7 * n + j + 1)
                if j:
                    pool.wait_ge(tot, 7 * n + j)
                    pool.wait_ge(scaled, 14 * n + 2 * j)
                f = dec[:, p, tot_at(j):tot_at(j + 1)].rearrange("p (n s) -> p n s", s=2)
                r = right(kqP[:, p, :, :], j)
                g.tensor_tensor(r, r, f[:, :, 0].unsqueeze(1).unsqueeze(3).to_broadcast([P, 2, nb, w_]),
                                ALU.mult).then_inc(scaled, 1)
                k = left(kQ[:, p, :], j)
                g.tensor_tensor(k, k, f[:, :, 1].unsqueeze(2).to_broadcast([P, nb, w_]),
                                ALU.mult).then_inc(scaled, 1)

            for t in (Vt[:, 1, :, :], MT[:, 1, :, :], AqT[:, 1, :, :], kqP[:, 1, :, :], kQt[:, :, :], sg[:, 1, :],
                      dec[:, 1, :], wo[:, :]):
                g.memset(t, 0.0).then_inc(zeroed, 1)
            g.memset(st[:, 1, :, :], 1.0).then_inc(zeroed, 1)
            pool.wait_ge(consts, 32)
            g.tensor_scalar(onw[:, :], onw[:, :], 0.5, None, ALU.mult).then_inc(onw_half, 1)
            pool.wait_ge(onw_half, 1)
            begin(0, 0)
            products(0, 0)
            scale(0, 0, 0)
            with pool.Fori(0, H) as h:
                for b in range(B):
                    n, n1, p, q = h * B + b, h * B + b + 1, b % 2, (b + 1) % 2
                    for j in range(1, 6):
                        scale(j, n, p)
                    if b == 0:
                        pool.wait_ge(wo_in, 16 * (h + 1))
                        pool.wait_ge(wo_mm, 2 * n + 2)
                        g.tensor_tensor(wo[:, :], wo_raw[:, :], onw[:, 0:1].to_broadcast([P, D]),
                                        ALU.mult).then_inc(wo_scaled, 1)
                    begin(n1, q)
                    scale(6, n, p)
                    products(n1, q)
                    scale(0, n1, q)


def laid_out_delta(g, chunks):
    def again(w):
        return np.concatenate([w, w[:1]])

    def by_head(name):
        return g(name).reshape(KC, P, H, DK).transpose(2, 1, 0, 3)

    s = np.arange(P)[:, None, None]
    j = np.arange(LEVELS)[None, :, None]
    t = np.arange(P // 2)[None, None, :]
    w = 1 << j
    pair_mask = ((s // (2 * w) == t // w) & (s % (2 * w) < w)).astype(np.float32)
    conv = [g(f"L1_attn_conv_{n}_w").reshape(H, DK, TAPS) for n in "qkv"]
    return {
        "da_wfga": np.stack([chunks(g("L1_attn_Wfa")), chunks(g("L1_attn_Wga"))], axis=2),
        "da_wb": chunks(again(g("L1_attn_Wb").T).T),
        "da_alog": again(g("L1_attn_A_log").reshape(H)),
        "da_w": again(np.concatenate(
            [by_head(f"L1_attn_W{n}")[:, :, kc] for kc in range(KC) for n in "qkv"]
            + [g(f"L1_attn_W{n}").reshape(P, H, DK).transpose(1, 0, 2) for n in ("fb", "gb")], axis=2
        ).reshape(H, P, 3 * KC + 2, DK)),
        "da_hc": again(np.concatenate(conv + [g("L1_attn_dt_bias").reshape(H, DK, 1)], axis=2)),
        "da_wo": again(g("L1_attn_Wo").reshape(H, DK, D)),
        "da_onw": g("L1_attn_o_norm_w").reshape(DK, 1),
        "da_mask": pair_mask,
    }


HF = 1024
HC = HF // P


def stage_hadamard_ffn(nc, x, ident, bk, a):
    ctx = ExitStack()
    with ctx:
        m = Pools(nc, ctx)
        xT = m.sb("ff_xT", [P, KC, T])
        xh = m.sb("ff_xh", [P, NT, D])
        w13_raw = m.sb("ff_w13_raw", [P, KC, 2, HF])
        w13 = m.sb("ff_w13", [P, 2, KC, 2, HF], F16)
        xs = m.sb("ff_xs", [P, 2, KC, T], F16)
        w2 = m.sb("ff_w2", [P, 2, HC, D])
        sign = m.sb("ff_sign", [P, P])
        sl = m.sb("ff_sl", [P, 2, L])
        hid = m.sb("ff_hid", [P, 2, HC, L])
        nin = NormIn(nc, m, "ff_in", x, ident, xT, xh, bk[0:4])
        nout = NormOut(nc, m, "ff_out", x, xh)
        w2_in = m.sem("ff_w2_in")
        w13_hi = m.sem("ff_w13_hi")
        w13_split = m.sem("ff_w13_split")
        x_hi = m.sem("ff_x_hi")
        x_split = m.sem("ff_x_split")
        w13_in = m.sem("ff_w13_in")
        sign_mm = m.sem("ff_sign_mm")
        sign_kept = m.sem("ff_sign_kept")
        turned = m.sem("ff_turned")
        mm_g = m.sem("ff_mm_g")
        mm_u = m.sem("ff_mm_u")
        acted = m.sem("ff_acted")
        gated = m.sem("ff_gated")
        out_mm = m.sem("ff_out_mm")
        out_kept = m.sem("ff_out_kept")
        block = ctx.enter_context(nc.Block())

        @block.sync
        def _(sp):
            sp.dma_start(sign[:, :], a["ff_sign"]).then_inc(w2_in, 16)
            sp.dma_start(w2[:, 0, :, :], a["ff_w2"]).then_inc(w2_in, 16)
            sp.dma_start(w13_raw[:, :, :, :], a["ff_w13"]).then_inc(w13_in, 16)

        @block.tensor
        def _(pe):
            mmul = nc.tensor.matmul
            pe.wait_ge(w2_in, 32)
            for c in range(HC // 2):
                for s in range(2):
                    mm = mmul(bk[4 + c][:, s * D:(s + 1) * D], sign[:, :], w2[:, 0, 2 * c + s, :], start=True, stop=True)
                mm.then_inc(sign_mm, 1)
            nin.tensor(pe)
            pe.wait_ge(sign_kept, HC // 2)

            def piece(n):
                g, c, q = n // HC, n % HC, n % 2
                if n == 0:
                    nin.done(pe)
                if c == 0:
                    pe.wait_ge(x_split, g + 1)
                if g == 0:
                    pe.wait_ge(w13_split, c // 2 + 1)
                for s, done in ((0, mm_g), (1, mm_u)):
                    if n >= 2:
                        pe.wait_ge(gated, n - 1)
                    for kc in range(KC):
                        for i, (pw, px) in enumerate(PARTS):
                            mm = mmul(bk[2 * q + s][:, :], w13[:, pw, kc, s, c * P:(c + 1) * P],
                                      xs[:, px, kc, g * L:(g + 1) * L],
                                      start=kc == 0 and i == 0, stop=kc == KC - 1 and i == 2)
                    mm.then_inc(done, 1)

            def outputs(g):
                pe.wait_ge(gated, HC * (g + 1))
                if g == 0:
                    pe.wait_ge(turned, 6)
                for j in range(L // P):
                    i = g * (L // P) + j
                    if i >= 2:
                        pe.wait_ge(out_kept, i - 1)
                    for c in range(HC):
                        mm = mmul(bk[4 + i % 2][:, 0:D], hid[:, g % 2, c, j * P:(j + 1) * P], w2[:, 1, c, :],
                                  start=c == 0, stop=c == HC - 1)
                    mm.then_inc(out_mm, 1)

            for g in range(B):
                for c in range(HC):
                    piece(g * HC + c)
                    if c == 1 and g >= 1:
                        outputs(g - 1)
            outputs(B - 1)

        @block.scalar
        def _(act):
            s_ = nc.scalar
            for c in range(HC // 2):
                act.wait_ge(sign_mm, c + 1)
                s_.activation(w2[:, 0, 2 * c:2 * c + 2, :], bk[4 + c][:, :].rearrange("p (s d) -> p s d", s=2),
                              ACT.Identity, scale=1.0 / 32.0 / WS).then_inc(sign_kept, 1)
            nin.scalar(act)
            act.wait_ge(w13_in, 16)
            for g in range(B):
                t = slice(2 * g * P, (2 * g + 2) * P)
                s_.activation(w13[:, 0, :, :, t], w13_raw[:, :, :, t], ACT.Identity, scale=WS).then_inc(w13_hi, 1)
                nin.done(act, g + 1)
                s_.activation(xs[:, 0, :, g * L:(g + 1) * L], xT[:, :, g * L:(g + 1) * L],
                              ACT.Identity).then_inc(x_hi, 1)

            def keep(i):
                act.wait_ge(out_mm, i + 1)
                s_.activation(xh[:, i, :], bk[4 + i % 2][:, 0:D], ACT.Identity).then_inc(out_kept, 1)

            for n in range(B * HC):
                act.wait_ge(mm_g, n + 1)
                if n >= 2:
                    act.wait_ge(gated, n - 1)
                s_.activation(sl[:, n % 2, :], bk[2 * (n % 2)][:, :], ACT.Silu, scale=1.0 / WS).then_inc(acted, 1)
                if n % HC == 1 and n > HC:
                    for j in range(4):
                        keep(4 * (n // HC - 1) + j)
            for j in range(4):
                keep(4 * (B - 1) + j)
            nout.scalar(act)

        @block.vector
        def _(dve):
            v = nc.vector
            nin.vector(dve)
            for g in range(B):
                t = slice(2 * g * P, (2 * g + 2) * P)
                dve.wait_ge(w13_hi, g + 1)
                v.scalar_tensor_tensor(out=w13[:, 1, :, :, t], in0=w13_raw[:, :, :, t], scalar=WS,
                                       in1=w13[:, 0, :, :, t], op0=ALU.mult, op1=ALU.subtract).then_inc(w13_split, 1)

            def transform():
                dve.wait_ge(sign_kept, HC // 2)
                for r in range(3):
                    src = w2[:, r % 2, :, :].rearrange("p (n s w) d -> p n s (w d)", s=2, w=1 << r)
                    dst = w2[:, (r + 1) % 2, :, :].rearrange("p (n s w) d -> p n s (w d)", s=2, w=1 << r)
                    if r:
                        dve.wait_ge(turned, 2 * r)
                    v.tensor_tensor(dst[:, :, 0], src[:, :, 0], src[:, :, 1], ALU.add).then_inc(turned, 1)
                    v.tensor_tensor(dst[:, :, 1], src[:, :, 0], src[:, :, 1], ALU.subtract).then_inc(turned, 1)

            for n in range(B * HC):
                g, c, q = n // HC, n % HC, n % 2
                dve.wait_ge(acted, n + 1)
                dve.wait_ge(mm_u, n + 1)
                if c == 0 and g >= 2:
                    dve.wait_ge(out_mm, 4 * (g - 1))
                if n == 2:
                    transform()
                v.tensor_tensor(hid[:, g % 2, c, :], sl[:, q, :], bk[2 * q + 1][:, :], ALU.mult).then_inc(gated, 1)
            nout.vector(dve, lambda i: dve.wait_ge(out_kept, i + 1))

        @block.gpsimd
        def _(pool):
            for g in range(B):
                t = slice(g * L, (g + 1) * L)
                pool.wait_ge(x_hi, g + 1)
                nin.done(pool, g + 1)
                nc.gpsimd.tensor_tensor(xs[:, 1, :, t], xT[:, :, t], xs[:, 0, :, t], ALU.subtract).then_inc(x_split, 1)


def laid_out_ffn(g, chunks):
    s = np.ones((1, 1), np.float32)
    while s.shape[0] < P:
        s = np.block([[s, s], [s, -s]])
    return {
        "ff_w13": np.stack([chunks(g("L1_ffn_W1").T), chunks(g("L1_ffn_W3").T)], axis=2),
        "ff_w2": chunks(g("L1_ffn_W2").T),
        "ff_sign": s.astype(np.float32),
    }


def program(nc, a, out, stages=4):
    ctx = ExitStack()
    with ctx:
        m = Pools(nc, ctx)
        x = m.sb("x", [P, NT, D])
        ident = m.sb("ident", [P, P])
        banks = [m.ps(f"bank{i}") for i in range(8)]
        x_in, x_out = m.sem("x_in"), m.sem("x_out")
        with nc.Block() as block:
            @block.sync
            def _(sp):
                sp.dma_start(x[:, :, :], a["x"].rearrange("(i p) d -> p i d", p=P)).then_inc(x_in, 16)
                sp.dma_start(ident[:, :], a["ident"]).then_inc(x_in, 16)
                sp.wait_ge(x_in, 32)
        if stages >= 1:
            stage_recurrence(nc, x, ident, banks, a["ra_w_in"], a["ra_w_out"], a["ra_vecs"], a["ra_out_b"])
        if stages >= 2:
            stage_experts(nc, x, ident, banks, a)
        if stages >= 3:
            stage_delta(nc, x, ident, banks, a)
        if stages >= 4:
            stage_hadamard_ffn(nc, x, ident, banks, a)
        with nc.Block() as block:
            @block.sync
            def _(sp):
                sp.dma_start(out.rearrange("(i p) d -> p i d", p=P), x[:, :, :]).then_inc(x_out, 16)
                sp.wait_ge(x_out, 16)


def laid_out(i):
    def chunks(w):
        return w.reshape(-1, P, w.shape[-1]).transpose(1, 0, 2)

    g = lambda n: np.asarray(i[n])
    w_in = np.stack([chunks(g(f"L0_attn_{n}_w").T) for n in ("A", "D", "B", "Ca", "Cb")], axis=2)
    r = {
        "x": g("L0_attn_x").reshape(T, D),
        "ident": np.eye(P, dtype=np.float32),
        "ra_w_in": w_in,
        "ra_w_out": chunks(g("L0_attn_out_w").T),
        "ra_vecs": np.stack([g("L0_attn_rms_w").reshape(KC, P).T, g("L0_attn_A_b").reshape(KC, P).T], axis=1),
        "ra_out_b": g("L0_attn_out_b"),
    }
    for more in (laid_out_experts, laid_out_delta, laid_out_ffn):
        r.update(more(g, chunks))
    return {k: np.ascontiguousarray(v) for k, v in r.items()}


STAGES = 4


def kernel(**inputs):
    import concourse.bacc as bacc
    from concourse.bass_utils import run_bass_kernel_spmd

    nc = bacc.Bacc("TRN2", target_bir_lowering=False, num_devices=1)
    arrays = laid_out(inputs)
    args = {k: nc.dram_tensor(f"in_{k}", v.shape, mybir.dt.from_np(v.dtype), kind="ExternalInput").ap()
            for k, v in arrays.items()}
    out = nc.dram_tensor("out_x", (T, D), F32, kind="ExternalOutput").ap()
    program(nc, args, out, STAGES)
    r = run_bass_kernel_spmd(nc, [{f"in_{k}": v for k, v in arrays.items()}], core_ids=[0])
    return r.results[0]["out_x"].reshape(B, L, D)
```
